# Optimizing a Trainium2 kernel written in Bass

```python
import numpy as np
import jax
import jax.numpy as jnp

def _softmax(x, axis=-1):
    return jax.nn.softmax(x, axis=axis)

def _gelu(x):
    return jax.nn.gelu(x, approximate=True)

def _silu(x):
    return jax.nn.silu(x)

def _sigmoid(x):
    return jax.nn.sigmoid(x)

def _layernorm(x, axis=-1, eps=1e-05):
    m = jnp.mean(x, axis=axis, keepdims=True)
    v = jnp.var(x, axis=axis, keepdims=True)
    return (x - m) / jnp.sqrt(v + eps)

def _scatter_add(tgt, idx, src, axis=0):
    return tgt.at[idx].add(src)

def _segment_sum(src, seg, n):
    return jax.ops.segment_sum(src, seg, n)
kernel_name = 'mk_lm_tower_d1_tok_ids256_r4_70e40f'

def setup_inputs(seed: int=0):
    np.random.seed(seed)
    _w = jnp.asarray

    def _rec_inputs():
        import jax
        import jax.numpy as jnp
        _rk = jax.random.key(seed)
        x = jax.random.randint(jax.random.fold_in(_rk, 1), (128, 128), 0, 250, jnp.int32)
        return x
    x = _rec_inputs()

    def _L0_tok_setup():
        import jax, jax.numpy as jnp
        import numpy as np
        B, T, H, VOCAB = (128, 128, 64, 250)
        EPS = 1e-12

        def _pos_graph(seq_inputs):
            si = seq_inputs[:, :, None]
            mask = si != 0
            equal = si == si.transpose(0, 2, 1)
            tril = jnp.tril(jnp.ones((si.shape[1], si.shape[1]), dtype=jnp.float32))
            rel = equal.astype(jnp.float32) * tril
            rel = rel * mask.astype(jnp.float32) * mask.transpose(0, 2, 1).astype(jnp.float32)
            norm = rel.sum(-2, keepdims=True)
            norm = jnp.where(norm == 0, 1.0, norm)
            return rel / norm

        def _get_pos_emb(seq_inputs, emb_table):
            seq_mask = seq_inputs != 0
            length = seq_mask.sum(1, keepdims=True)
            coo = jnp.arange(seq_inputs.shape[1])[None, :] * seq_mask
            pos_index = (length - coo) * seq_mask
            return emb_table[pos_index]
        key = jax.random.key(seed)
        k1, k2, k3, k4 = jax.random.split(key, 4)
        stdv = 1.0 / np.sqrt(H)
        seq_inputs = jax.random.randint(k1, (B, T), 0, VOCAB, dtype=jnp.int64 if jax.config.jax_enable_x64 else jnp.int32)
        emb_table = jax.random.normal(k2, (T + 1, H), dtype=jnp.float32)
        W_in = jax.random.uniform(k3, (H, H), minval=-stdv, maxval=stdv, dtype=jnp.float32)
        b_oah = jax.random.uniform(k4, (H,), minval=-stdv, maxval=stdv, dtype=jnp.float32)
        return {'seq_inputs': seq_inputs, 'emb_table': emb_table, 'W_in': W_in, 'b_oah': b_oah}
    _L0_tok_all = _L0_tok_setup()
    _L0_tok_in = {k: v for k, v in _L0_tok_all.items() if k in ('emb_table', 'W_in', 'b_oah')}
    del _L0_tok_all

    def _L0_attn_setup():
        import jax, jax.numpy as jnp
        import numpy as np
        B, L, D = (4, 1024, 64)
        key = jax.random.key(seed)
        kx, kq, kk, kv, ko = jax.random.split(key, 5)
        std = 0.02
        return {'x': jax.random.normal(kx, (B, L, D), dtype=jnp.float32), 'Wq': std * jax.random.normal(kq, (D, D), dtype=jnp.float32), 'Wk': std * jax.random.normal(kk, (D, D), dtype=jnp.float32), 'Wv': std * jax.random.normal(kv, (D, D), dtype=jnp.float32), 'Wo': std * jax.random.normal(ko, (D, D), dtype=jnp.float32)}
    _L0_attn_all = _L0_attn_setup()
    _L0_attn_in = {k: v for k, v in _L0_attn_all.items() if k in ('Wq', 'Wk', 'Wv', 'Wo')}
    del _L0_attn_all

    def _L0_ffn_setup():
        import jax, jax.numpy as jnp
        import numpy as np
        B, S, H, NH, NE = (4, 256, 64, 4, 4)
        D = H // NH
        EPS = 1e-08

        def layernorm(x, g, b):
            m = jnp.mean(x, axis=-1, keepdims=True)
            v = jnp.mean((x - m) ** 2, axis=-1, keepdims=True)
            return (x - m) / jnp.sqrt(v + EPS) * g + b
        key = jax.random.key(seed)
        ks = jax.random.split(key, 18)
        sc = 0.05
        return {'x': jax.random.normal(ks[0], (B, S, H), jnp.float32), 'hl_w': jax.random.normal(ks[1], (NH, D, H), jnp.float32) * sc, 'hl_b': jax.random.normal(ks[2], (NH, D), jnp.float32) * sc, 'wq': jax.random.normal(ks[3], (NH, NE, D, D), jnp.float32) * sc, 'wk': jax.random.normal(ks[4], (NH, D, D), jnp.float32) * sc, 'wv': jax.random.normal(ks[5], (NH, D, D), jnp.float32) * sc, 'gate_w': jax.random.normal(ks[6], (NH, NE, NE * D), jnp.float32) * sc, 'gate_b': jax.random.normal(ks[7], (NH, NE), jnp.float32) * sc, 'ln_g': jnp.ones((D,), jnp.float32), 'ln_b': jnp.zeros((D,), jnp.float32), 'fc1_w': jax.random.normal(ks[8], (D, D), jnp.float32) * sc, 'fc1_b': jax.random.normal(ks[9], (D,), jnp.float32) * sc, 'fc2_w': jax.random.normal(ks[10], (D, D), jnp.float32) * sc, 'fc2_b': jax.random.normal(ks[11], (D,), jnp.float32) * sc, 'fnorm_g': jnp.ones((D,), jnp.float32), 'fnorm_b': jnp.zeros((D,), jnp.float32), 'fgate_w': jax.random.normal(ks[12], (NH, H), jnp.float32) * sc}
    _L0_ffn_all = _L0_ffn_setup()
    _L0_ffn_in = {k: v for k, v in _L0_ffn_all.items() if k in ('hl_w', 'hl_b', 'wq', 'wk', 'wv', 'gate_w', 'gate_b', 'ln_g', 'ln_b', 'fc1_w', 'fc1_b', 'fc2_w', 'fc2_b', 'fnorm_g', 'fnorm_b', 'fgate_w')}
    del _L0_ffn_all
    return {'x': x, 'L0_tok_emb_table': _L0_tok_in['emb_table'], 'L0_tok_W_in': _L0_tok_in['W_in'], 'L0_tok_b_oah': _L0_tok_in['b_oah'], 'L0_attn_Wq': _L0_attn_in['Wq'], 'L0_attn_Wk': _L0_attn_in['Wk'], 'L0_attn_Wv': _L0_attn_in['Wv'], 'L0_attn_Wo': _L0_attn_in['Wo'], 'L0_ffn_hl_w': _L0_ffn_in['hl_w'], 'L0_ffn_hl_b': _L0_ffn_in['hl_b'], 'L0_ffn_wq': _L0_ffn_in['wq'], 'L0_ffn_wk': _L0_ffn_in['wk'], 'L0_ffn_wv': _L0_ffn_in['wv'], 'L0_ffn_gate_w': _L0_ffn_in['gate_w'], 'L0_ffn_gate_b': _L0_ffn_in['gate_b'], 'L0_ffn_ln_g': _L0_ffn_in['ln_g'], 'L0_ffn_ln_b': _L0_ffn_in['ln_b'], 'L0_ffn_fc1_w': _L0_ffn_in['fc1_w'], 'L0_ffn_fc1_b': _L0_ffn_in['fc1_b'], 'L0_ffn_fc2_w': _L0_ffn_in['fc2_w'], 'L0_ffn_fc2_b': _L0_ffn_in['fc2_b'], 'L0_ffn_fnorm_g': _L0_ffn_in['fnorm_g'], 'L0_ffn_fnorm_b': _L0_ffn_in['fnorm_b'], 'L0_ffn_fgate_w': _L0_ffn_in['fgate_w']}

def reference(x, L0_tok_emb_table, L0_tok_W_in, L0_tok_b_oah, L0_attn_Wq, L0_attn_Wk, L0_attn_Wv, L0_attn_Wo, L0_ffn_hl_w, L0_ffn_hl_b, L0_ffn_wq, L0_ffn_wk, L0_ffn_wv, L0_ffn_gate_w, L0_ffn_gate_b, L0_ffn_ln_g, L0_ffn_ln_b, L0_ffn_fc1_w, L0_ffn_fc1_b, L0_ffn_fc2_w, L0_ffn_fc2_b, L0_ffn_fnorm_g, L0_ffn_fnorm_b, L0_ffn_fgate_w):
    import jax
    import jax.numpy as jnp

    def _L0_tok_ref(seq_inputs, emb_table, W_in, b_oah):
        import jax, jax.numpy as jnp
        import numpy as np
        B, T, H, VOCAB = (128, 128, 64, 250)
        EPS = 1e-12

        def _pos_graph(seq_inputs):
            si = seq_inputs[:, :, None]
            mask = si != 0
            equal = si == si.transpose(0, 2, 1)
            tril = jnp.tril(jnp.ones((si.shape[1], si.shape[1]), dtype=jnp.float32))
            rel = equal.astype(jnp.float32) * tril
            rel = rel * mask.astype(jnp.float32) * mask.transpose(0, 2, 1).astype(jnp.float32)
            norm = rel.sum(-2, keepdims=True)
            norm = jnp.where(norm == 0, 1.0, norm)
            return rel / norm

        def _get_pos_emb(seq_inputs, emb_table):
            seq_mask = seq_inputs != 0
            length = seq_mask.sum(1, keepdims=True)
            coo = jnp.arange(seq_inputs.shape[1])[None, :] * seq_mask
            pos_index = (length - coo) * seq_mask
            return emb_table[pos_index]
        step = 1
        A_in = _pos_graph(seq_inputs)
        pe = _get_pos_emb(seq_inputs, emb_table)
        nrm = jnp.sqrt(jnp.sum(pe * pe, axis=1, keepdims=True))
        pe = pe / jnp.maximum(nrm, EPS)
        for _ in range(step):
            h_n = jnp.einsum('bth,oh->bto', pe, W_in)
            pe = jnp.einsum('bji,bjh->bih', A_in, h_n) + b_oah
        return pe

    def _L0_attn_ref(x, Wq, Wk, Wv, Wo):
        import jax, jax.numpy as jnp
        import numpy as np
        B, L, D = (4, 1024, 64)
        q = x @ Wq.T
        k = x @ Wk.T
        v = x @ Wv.T
        logits = jnp.einsum('bld,bmd->blm', q, k)
        Lq = x.shape[1]
        causal_mask = jnp.triu(jnp.ones((Lq, Lq), dtype=bool), k=1)
        logits = jnp.where(causal_mask[None], jnp.asarray(0.0, logits.dtype), logits)
        attn = jax.nn.relu(logits)
        row_counts = jnp.maximum(jnp.arange(Lq, dtype=attn.dtype), 1.0)
        attn = attn / row_counts[None, :, None]
        ctx = jnp.einsum('blm,bmd->bld', attn, v)
        return ctx @ Wo.T

    def _L0_ffn_ref(x, hl_w, hl_b, wq, wk, wv, gate_w, gate_b, ln_g, ln_b, fc1_w, fc1_b, fc2_w, fc2_b, fnorm_g, fnorm_b, fgate_w):
        import jax, jax.numpy as jnp
        import numpy as np
        B, S, H, NH, NE = (4, 256, 64, 4, 4)
        D = H // NH
        EPS = 1e-08

        def layernorm(x, g, b):
            m = jnp.mean(x, axis=-1, keepdims=True)
            v = jnp.mean((x - m) ** 2, axis=-1, keepdims=True)
            return (x - m) / jnp.sqrt(v + EPS) * g + b
        b, s, h = x.shape
        nh, d, _ = wk.shape
        ne = wq.shape[1]
        sx = jnp.einsum('bsh,ndh->bnsd', x, hl_w) + hl_b[None, :, None, :]
        pad = sx == 0
        q = jnp.einsum('bnsd,neod->bneso', sx, wq)
        k = jnp.einsum('bnsd,nod->bnso', sx, wk)
        v = jnp.einsum('bnsd,nod->bnso', sx, wv)
        causal = jnp.where(jnp.tril(jnp.ones((s, s), bool)), 0.0, -jnp.inf).astype(x.dtype)
        scores = jnp.einsum('bnesd,bntd->bnest', q, k) * d ** 0.5 + causal
        att = jax.nn.softmax(scores, axis=-1)
        qkv = jnp.einsum('bnest,bntd->bnesd', att, v)
        qkv = jnp.where(pad[:, :, None], 0.0, qkv)
        out = jnp.transpose(qkv, (0, 1, 3, 2, 4)).reshape(b, nh, s, ne * d)
        gs = jax.nn.softmax(jnp.einsum('bnsf,nef->bnse', out, gate_w) + gate_b[None, :, None, :], axis=-1)
        mixed = jnp.einsum('bnsed,bnse->bnsd', out.reshape(b, nh, s, ne, d), gs)
        resid = sx[jnp.arange(nh), jnp.arange(nh)]
        hn = layernorm(mixed + resid, ln_g, ln_b)
        f_n = jnp.transpose(hn, (0, 2, 1, 3)).reshape(b, s, h)
        fx = f_n.reshape(b, s, nh, d)
        pm = fx == 0
        hx = jnp.where(pm, 0.0, fx @ fc1_w.T + fc1_b)
        hx = jax.nn.relu(hx)
        hx = jnp.where(pm, 0.0, hx @ fc2_w.T + fc2_b)
        hx = layernorm(hx + fx, fnorm_g, fnorm_b)
        fout = hx.reshape(b, s, h)
        fg = jax.nn.softmax(fout @ fgate_w.T, axis=-1)
        return (fout.reshape(b, s, nh, d) * fg[..., None]).reshape(b, s, h)
    h = _L0_tok_ref(x, L0_tok_emb_table, L0_tok_W_in, L0_tok_b_oah)
    h = h + _L0_attn_ref(_layernorm(h, axis=-1), L0_attn_Wq, L0_attn_Wk, L0_attn_Wv, L0_attn_Wo)
    h = h + _L0_ffn_ref(_layernorm(h, axis=-1), L0_ffn_hl_w, L0_ffn_hl_b, L0_ffn_wq, L0_ffn_wk, L0_ffn_wv, L0_ffn_gate_w, L0_ffn_gate_b, L0_ffn_ln_g, L0_ffn_ln_b, L0_ffn_fc1_w, L0_ffn_fc1_b, L0_ffn_fc2_w, L0_ffn_fc2_b, L0_ffn_fnorm_g, L0_ffn_fnorm_b, L0_ffn_fgate_w)
    return h

_drawn_inputs = setup_inputs


def setup_inputs(seed=0):
    import zlib

    import numpy as np

    out = dict(_drawn_inputs(seed))
    spreads = {'L0_ffn_ln_g': (1.0, 0.2),
     'L0_ffn_ln_b': (0.0, 0.1),
     'L0_ffn_fnorm_g': (1.0, 0.2),
     'L0_ffn_fnorm_b': (0.0, 0.1)}
    factors = {'L0_ffn_wq': 8.0,
     'L0_ffn_wk': 8.0,
     'L0_ffn_gate_w': 147.493,
     'L0_ffn_gate_b': 41.453,
     'L0_ffn_fc1_b': 8.0}
    for name, (base, spread) in spreads.items():
        noise = np.random.default_rng([zlib.crc32(name.encode()), seed]).standard_normal(out[name].shape)
        drawn = base * np.exp(spread * noise) if base else spread * noise
        out[name] = jnp.asarray(drawn.astype(out[name].dtype))
    for name, factor in factors.items():
        out[name] = (out[name] * factor).astype(out[name].dtype)
    return out
```

```python
import numpy as np
import concourse.bass as bass
from concourse import mybir
from contextlib import ExitStack

F32 = mybir.dt.float32
F32R = mybir.dt.float32r
BF16 = mybir.dt.bfloat16
I32 = mybir.dt.int32
ALU = mybir.AluOpType
ACT = mybir.ActivationFunctionType
X = mybir.AxisListType.X

B, T, H = 128, 128, 64
NH, NE, D = 4, 4, 16
GB = 4
NG = B // GB
BLK = 32
NBLK = T // BLK

C_ID, C_KEEP_JI, C_KEEP_ML, C_ONE, C_RC = 0, 128, 256, 384, 385
C_NHALF = 386
C_ONEHOT, C_TRI, C_SEL, C_OWN = 388, 516, 644, 1156
N_CONST = 1156 + 512
NEVER = -1.0e30
Q_ROWS = 96
C_ROWS = 100


def shape_constants():
    c = np.zeros((128, N_CONST), np.float32)
    r = np.arange(128)
    c[:, C_ID:C_ID + 128] = np.eye(128)
    c[:, C_KEEP_JI:C_KEEP_JI + 128] = r[:, None] >= r[None, :]
    c[:, C_KEEP_ML:C_KEEP_ML + 128] = r[:, None] <= r[None, :]
    c[:, C_ONE] = 1.0
    c[:, C_RC] = 1.0 / np.maximum(r, 1)
    c[:, C_NHALF] = -0.5
    for e in range(NE):
        c[0:BLK, C_ONEHOT + e * BLK:C_ONEHOT + (e + 1) * BLK] = np.eye(BLK)
    for n in range(NH):
        c[0:BLK, C_TRI + n * BLK:C_TRI + (n + 1) * BLK] = np.where(r[None, :BLK] > r[:BLK, None], NEVER, 0)
    sel = c[:, C_SEL:C_SEL + 512].reshape(128, NE, 128)
    for n in range(NH):
        for d in range(D):
            sel[32 * n + d, :, 16 * n + d] = 1
        sel[32 * n + D, :, 64 + n] = 1
    own = c[:, C_OWN:C_OWN + 512].reshape(128, NH, 128)
    for n in range(NH):
        own[96 + 2 * (n % 2):98 + 2 * (n % 2), n, :] = 1
    return c


def at_least(eng, semaphore, value):
    if isinstance(value, int) and value <= 0:
        return
    eng.wait_ge(semaphore, value)


def pipeline(eng, step):
    step(0, 0, 2)
    step(1, 1, 2)
    with eng.Fori(1, NG // 2 - 1) as it:
        step(2 * it, 0, 2)
        step(2 * it + 1, 1, 2)
    step(NG - 2, 0, 1)
    step(NG - 1, 1, 0)


def signals(nc, ctx, prefix, names):
    return {n: ctx.enter_context(nc.semaphore(f"{prefix}_{n}")) for n in names.split()}


def load_inputs(nc, ctx, ins, S):
    pass


def token_graph(nc, ins, M, ps):
    H_all = M["H"]
    cst = M["cst"]
    ctx = ExitStack()
    with ctx:
        def sb(name, shape, dt=F32):
            return ctx.enter_context(nc.sbuf_tensor(name, shape, dt))
        ids = sb("a_ids", [B, T], I32)
        idf = sb("a_idf", [B, T])
        seen = sb("a_seen", [B, T])
        cnt = sb("a_cnt", [B, 4])
        row = sb("a_row", [1, B])
        row_i = sb("a_row_i", [1, B], I32)
        id_t = sb("a_id_t", [T, B])
        off_t = sb("a_off_t", [T, B])
        key_t = sb("a_key_t", [T, B])
        seen_t = sb("a_seen_t", [T, B])
        emb0 = sb("a_emb0", [1, H])
        sq0 = sb("a_sq0", [1, 2 * H])
        base = sb("a_base", [128, B // 2])
        w_in = sb("a_w_in", [128, 128])
        b_oah = sb("a_b_oah", [128, H])
        pe_rows = sb("a_pe_rows", [T, 2, GB, H + 1])
        id_rows = sb("a_id_rows", [128, 2, GB, T], I32)
        rel = sb("a_rel", [T, 2, GB, T])
        sq = sb("a_sq", [T, 2, GB, H])
        rn = sb("a_rn", [T, 2, GB, 2])
        agg = sb("a_agg", [T, 2, GB, H])
        inv = sb("a_inv", [128, 2, 4])
        xt = sb("a_xt", [128, 2, 2, T])
        S = signals(nc, ctx, "a", "ids consts weights zeroed ones idf seen count row row_i id_t off_t key_t seen_t "
                    "sq0 base ps_count ps_id ps_base pe_in0 pe_in1 row_in0 row_in1 rel sq ps_agg ps_nrm rn rn1 agg inv0 inv1 inv "
                    "ps_xt xt ps_h h")
        table = ins["table"]

        with nc.Block() as block:
            @block.sync
            def _(sp):
                sp.dma_start(ids[:], ins["x"]).then_inc(S["ids"], 16)
                sp.dma_start(cst[:], ins["consts"]).then_inc(S["consts"], 16)
                sp.dma_start(emb0[:], ins["table"][128:129, :]).then_inc(S["weights"], 16)
                sp.dma_start(b_oah[:], ins["b_oah"].to_broadcast([128, H])).then_inc(S["weights"], 16)
                sp.wait_ge(S["zeroed"], 1)
                sp.dma_start(w_in[0:H, 0:H], ins["W_in_t"]).then_inc(S["weights"], 16)
                sp.dma_start(w_in[H:128, H:128], ins["W_in_t"]).then_inc(S["weights"], 16)
                sp.wait_ge(S["row_i"], 1)
                sp.wait_ge(S["ones"], 2)

                def fetch(it):
                    for u in range(2):
                        g = 2 * it + u
                        at_least(sp, S["ps_agg"], g - 1)
                        at_least(sp, S["sq"], g - 1)
                        sp.dma_start(id_rows[:, u, :, :], ins["x"][bass.ds(g * GB, GB), :].rearrange("(o b) t -> o b t", o=1)
                                     .to_broadcast([128, GB, T])).then_inc(S[f"row_in{u}"], 16)
                        for q in range(GB):
                            first = sp.value_load(row_i[0:1, bass.ds(g * GB + q, 1)], min_val=0, max_val=T)
                            sp.dma_start(pe_rows[:, u, q, 0:H], table[bass.ds(first, T), :]).then_inc(S[f"pe_in{u}"], 16)

                fetch(0)
                with sp.Fori(1, NG // 2) as it:
                    fetch(it)

            @block.gpsimd
            def _(pool):
                pool.memset(w_in[:], 0.0).then_inc(S["zeroed"], 1)
                pool.wait_ge(S["consts"], 16)
                for u in range(2):
                    pool.memset(pe_rows[:, u, :, H:H + 1], 1.0).then_inc(S["ones"], 1)

                def step(it):
                    for u in range(2):
                        g = 2 * it + u
                        pool.wait_ge(S["inv0"], g + 1)
                        pool.tensor_tensor(inv[:, u, 2:4], inv[:, u, 0:2], cst[:, C_NHALF:C_NHALF + 1].to_broadcast([128, 2]), ALU.pow).then_inc(S["inv"], 1)
                step(0)
                with pool.Fori(1, NG // 2) as it:
                    step(it)

            @block.vector
            def _(dve):
                dve.wait_ge(S["ids"], 16)
                dve.tensor_copy(idf[:], ids[:]).then_inc(S["idf"], 1)
                dve.wait_ge(S["idf"], 1)
                dve.tensor_scalar(seen[:], idf[:], 0.0, None, ALU.not_equal).then_inc(S["seen"], 1)
                dve.wait_ge(S["seen"], 1)
                dve.tensor_reduce(cnt[:, 0:1], seen[:], X, ALU.add).then_inc(S["count"], 1)
                dve.wait_ge(S["count"], 1)
                dve.tensor_scalar(cnt[:, 1:2], cnt[:, 0:1], -1.0, float(T), ALU.mult, ALU.add).then_inc(S["count"], 1)
                dve.wait_ge(S["ps_count"], 1)
                dve.tensor_copy(row[:], ps[0][0:1, 0:B]).then_inc(S["row"], 1)
                dve.tensor_copy(row_i[:], ps[0][0:1, 0:B]).then_inc(S["row_i"], 1)
                dve.wait_ge(S["ps_id"], 1)
                dve.tensor_copy(id_t[:], ps[1][:, 0:B]).then_inc(S["id_t"], 1)
                dve.wait_ge(S["id_t"], 1)
                dve.tensor_scalar(off_t[:], id_t[:], 0.0, -0.5, ALU.is_equal, ALU.mult).then_inc(S["off_t"], 1)
                dve.tensor_scalar(seen_t[:], id_t[:], 0.0, None, ALU.not_equal).then_inc(S["seen_t"], 1)
                dve.wait_ge(S["off_t"], 1)
                dve.tensor_tensor(key_t[:], id_t[:], off_t[:], ALU.add).then_inc(S["key_t"], 1)
                dve.wait_ge(S["weights"], 64)
                for k in range(2):
                    dve.tensor_tensor(sq0[0:1, k * H:(k + 1) * H], emb0[:], emb0[:], ALU.mult).then_inc(S["sq0"], 1)
                dve.wait_ge(S["ps_base"], 1)
                dve.tensor_copy(base[:], ps[2][:, 0:B // 2]).then_inc(S["base"], 1)
                dve.wait_ge(S["base"], 1)
                dve.wait_ge(S["key_t"], 1)
                dve.wait_ge(S["seen_t"], 1)
                dve.wait_ge(S["consts"], 16)

                def graph(it, g, u):
                    dve.wait_ge(S[f"row_in{u}"], 16 * (it + 1))
                    at_least(dve, S["ps_agg"], g - 1)
                    for q in range(GB):
                        ins_ = dve.scalar_tensor_tensor(
                            rel[:, u, q, :], id_rows[:, u, q, :], key_t[:, bass.ds(g * GB + q, 1)],
                            cst[:, C_KEEP_JI:C_KEEP_JI + T], ALU.is_equal, ALU.mult)
                    ins_.then_inc(S["rel"], 1)
                    dve.wait_ge(S[f"pe_in{u}"], 16 * GB * (it + 1))
                    at_least(dve, S["ps_nrm"], g - 1)
                    for q in range(GB):
                        ins_ = dve.scalar_tensor_tensor(
                            sq[:, u, q, :], pe_rows[:, u, q, 0:H], seen_t[:, bass.ds(g * GB + q, 1)],
                            pe_rows[:, u, q, 0:H], ALU.mult, ALU.mult)
                    ins_.then_inc(S["sq"], 1)

                def mean(it, g, u):
                    a = ps[u][:, 0:GB * 66].rearrange("p (b c) -> p b c", b=GB)
                    dve.wait_ge(S["ps_agg"], g + 1)
                    dve.tensor_scalar(rn[:, u, :, 0:1], a[:, :, H:H + 1], 1.0, None, ALU.max).then_inc(S["rn"], 1)
                    dve.wait_ge(S["rn"], g + 1)
                    dve.reciprocal(rn[:, u, :, 1:2], rn[:, u, :, 0:1]).then_inc(S["rn1"], 1)
                    dve.wait_ge(S["rn1"], g + 1)
                    at_least(dve, S["ps_xt"], g - 1)
                    dve.tensor_tensor(agg[:, u, :, :], a[:, :, 0:H],
                                      rn[:, u, :, 1:2].to_broadcast([T, GB, H]), ALU.mult).then_inc(S["agg"], 1)
                    dve.wait_ge(S["ps_nrm"], g + 1)
                    at_least(dve, S["xt"], g - 1)
                    for p in range(2):
                        ins_ = dve.tensor_scalar(inv[:, u, p:p + 1], ps[2 + u][:, p:p + 1], base[:, bass.ds(2 * g + p, 1)], 1e-24,
                                                 ALU.add, ALU.max)
                    ins_.then_inc(S["inv0"], 1)

                def store(it, g, u):
                    dve.wait_ge(S["ps_h"], g + 1)
                    dve.tensor_tensor(H_all[:, bass.ds(g * GB, GB), :],
                                      ps[6 + u][:, 0:GB * H].rearrange("p (b c) -> p b c", b=GB),
                                      b_oah[:].rearrange("p (o c) -> p o c", o=1).to_broadcast([128, GB, H]), ALU.add).then_inc(S["h"], 1)

                def step(it):
                    for f in (graph, mean, store):
                        for u in range(2):
                            f(it, 2 * it + u, u)
                step(0)
                with dve.Fori(1, NG // 2) as it:
                    step(it)

            @block.scalar
            def _(act):
                def step(it):
                    for u in range(2):
                        g = 2 * it + u
                        act.wait_ge(S["ps_xt"], g + 1)
                        act.wait_ge(S["inv"], g + 1)
                        at_least(act, S["ps_h"], g - 1)
                        for p in range(2):
                            ins_ = act.activation(xt[:, u, p, :], ps[4 + u][:, p * T:(p + 1) * T], ACT.Copy,
                                                  scale=inv[:, u, 2 + p:3 + p])
                        ins_.then_inc(S["xt"], 1)
                step(0)
                with act.Fori(1, NG // 2) as it:
                    step(it)

            @block.tensor
            def _(pe):
                ident = cst[:, C_ID:C_ID + 128]
                pe.wait_ge(S["consts"], 16)
                pe.wait_ge(S["count"], 2)
                pe.transpose(ps[0][0:1, 0:B], cnt[:, 1:2], ident).then_inc(S["ps_count"], 1)
                pe.wait_ge(S["idf"], 1)
                pe.transpose(ps[1][:, 0:B], idf[:], ident).then_inc(S["ps_id"], 1)
                pe.wait_ge(S["sq0"], 2)
                pe.wait_ge(S["row"], 1)
                pairs = row[0:1, :].rearrange("o (p k) -> o k p", k=2)
                for k in range(2):
                    m = pe.matmul(ps[2][k * H:(k + 1) * H, 0:B // 2], sq0[0:1, k * H:(k + 1) * H], pairs[:, k, :],
                                  start=True, stop=True)
                m.then_inc(S["ps_base"], 1)
                pe.wait_ge(S["weights"], 64)
                pe.wait_ge(S["base"], 1)
                pe.wait_ge(S["id_t"], 1)
                pe.wait_ge(S["row_i"], 1)

                def gather(it, g, u):
                    pe.wait_ge(S["rel"], g + 1)
                    pe.wait_ge(S[f"pe_in{u}"], 16 * GB * (it + 1))
                    at_least(pe, S["agg"], g - 1)
                    for q in range(GB):
                        m = pe.matmul(ps[u][:, q * 66:q * 66 + H + 1], rel[:, u, q, :], pe_rows[:, u, q, :],
                                      start=True, stop=True)
                    m.then_inc(S["ps_agg"], 1)
                    pe.wait_ge(S["sq"], g + 1)
                    at_least(pe, S["inv0"], g - 1)
                    for p in range(2):
                        m = pe.matmul(ps[2 + u][:, p:p + 1], sq[:, u, 2 * p:2 * p + 2, :].rearrange("p b c -> p (b c)"),
                                      cst[:, C_ONE:C_ONE + 1], start=True, stop=True)
                    m.then_inc(S["ps_nrm"], 1)

                def turn(it, g, u):
                    pe.wait_ge(S["agg"], g + 1)
                    at_least(pe, S["xt"], g - 1)
                    for p in range(2):
                        m = pe.transpose(ps[4 + u][:, p * T:(p + 1) * T],
                                         agg[:, u, 2 * p:2 * p + 2, :].rearrange("p b c -> p (b c)"), ident)
                    m.then_inc(S["ps_xt"], 1)

                def project(it, g, u):
                    pe.wait_ge(S["xt"], g + 1)
                    at_least(pe, S["h"], g - 1)
                    for p in range(2):
                        m = pe.matmul(ps[6 + u][:, p * 128:(p + 1) * 128], xt[:, u, p, :], w_in[:], start=True, stop=True)
                    m.then_inc(S["ps_h"], 1)

                def step(it):
                    for f in (gather, turn, project):
                        for u in range(2):
                            f(it, 2 * it + u, u)
                step(0)
                with pe.Fori(1, NG // 2) as it:
                    step(it)


def norm_stats(dve, x, stats, tmp, mean, var, xc, S, g):
    for q in range(GB):
        i = dve.bn_stats(stats[:, q, :], x[:, q, :])
    i.then_inc(S["stats"], 1)
    dve.wait_ge(S["stats"], g + 1)
    dve.tensor_tensor(tmp[:, 0], stats[:, :, 1:2], stats[:, :, 4:5], ALU.add)
    dve.tensor_tensor(tmp[:, 1], stats[:, :, 1:2], stats[:, :, 4:5], ALU.subtract)
    dve.tensor_tensor(tmp[:, 2], stats[:, :, 2:3], stats[:, :, 5:6], ALU.add).then_inc(S["sums"], 1)
    dve.wait_ge(S["sums"], g + 1)
    dve.tensor_tensor(tmp[:, 3], tmp[:, 1], tmp[:, 1], ALU.mult)
    dve.tensor_scalar(mean[:], tmp[:, 0], 0.5, None, ALU.mult).then_inc(S["mean"], 1)
    dve.wait_ge(S["mean"], g + 1)
    dve.scalar_tensor_tensor(tmp[:, 4], tmp[:, 3], float(H // 4), tmp[:, 2], ALU.mult, ALU.add)
    dve.tensor_tensor(xc, x, mean[:].to_broadcast([T, GB, H]), ALU.subtract).then_inc(S["xc"], 1)
    dve.wait_ge(S["xc"], g + 1)
    dve.tensor_scalar(var, tmp[:, 4], 1.0 / H, 1e-5, ALU.mult, ALU.add).then_inc(S["var"], 1)


def relu_attention(nc, ins, M, ps):
    H_all, cst = M["H"], M["cst"]
    ctx = ExitStack()
    with ctx:
        def sb(name, shape, dt=F32):
            return ctx.enter_context(nc.sbuf_tensor(name, shape, dt))
        w4 = sb("b_w4", [H, 4, H])
        w_qk = sb("b_w_qk", [128, 128])
        w_vo = sb("b_w_vo", [128, 128])
        stats = sb("b_stats", [T, 2, GB, 6])
        tmp = sb("b_tmp", [T, 2, 5, GB, 1])
        mean = sb("b_mean", [T, 2, GB, 1])
        xc = sb("b_xc", [T, 2, GB, H])
        var = sb("b_var", [T, 2, GB, 1])
        rstd = sb("b_rstd", [T, 2, GB, 1])
        xn = sb("b_xn", [T, 2, GB, H])
        xt = sb("b_xt", [128, 2, 2, T])
        ubd = sb("b_ubd", [128, 2, 2, 2 * T])
        val = sb("b_val", [T, 2, 2, 2 * H])
        att = sb("b_att", [T, 2, GB, T])
        S = signals(nc, ctx, "b", "w4 zeroed ps_w w stats sums mean xc var rstd xn ps_xt xt u ps_v v ps_l att ps_c h")
        ident = cst[:, C_ID:C_ID + 128]
        with nc.Block() as block:
            @block.sync
            def _(sp):
                for k, n in enumerate(("Wq", "Wk", "Wv", "Wo_t")):
                    sp.dma_start(w4[:, k, :], ins[n]).then_inc(S["w4"], 16)

            @block.gpsimd
            def _(pool):
                for t in (w_qk, w_vo, ubd):
                    i = pool.memset(t[:], 0.0).then_inc(S["zeroed"], 1)

                def step(it):
                    for u in range(2):
                        g = 2 * it + u
                        pool.wait_ge(S["var"], g + 1)
                        pool.tensor_tensor(rstd[:, u, :, :], var[:, u, :, :], cst[:, C_NHALF:C_NHALF + 1].rearrange("p (o c) -> p o c", o=1).to_broadcast([T, GB, 1]),
                                           ALU.pow).then_inc(S["rstd"], 1)
                        pool.wait_ge(S["rstd"], g + 1)
                        at_least(pool, S["ps_xt"], g - 1)
                        pool.tensor_tensor(xn[:, u], xc[:, u], rstd[:, u].to_broadcast([T, GB, H]), ALU.mult).then_inc(S["xn"], 1)
                step(0)
                with pool.Fori(1, NG // 2) as it:
                    step(it)

            @block.vector
            def _(dve):
                dve.wait_ge(S["ps_w"], 1)
                dve.wait_ge(S["zeroed"], 3)
                for k in range(2):
                    r = slice(k * H, (k + 1) * H)
                    dve.tensor_copy(w_qk[r, r], ps[0][r, 0:H]).then_inc(S["w"], 1)
                    dve.tensor_copy(w_vo[r, r], ps[0][r, H:2 * H]).then_inc(S["w"], 1)

                def norm(it, g, u):
                    at_least(dve, S["xn"], g - 1)
                    norm_stats(dve, H_all[:, bass.ds(g * GB, GB), :], stats[:, u], tmp[:, u], mean[:, u], var[:, u], xc[:, u], S, g)

                def attend(it, g, u):
                    dve.wait_ge(S["ps_l"], g + 1)
                    at_least(dve, S["ps_c"], g - 1)
                    dve.scalar_tensor_tensor(att[:, u, :, :], ps[4 + u][:, :].rearrange("p (b l) -> p b l", b=GB), 0.0,
                                             cst[:, C_KEEP_ML:C_KEEP_ML + T].rearrange("p (o l) -> p o l", o=1)
                                             .to_broadcast([T, GB, T]), ALU.max, ALU.mult).then_inc(S["att"], 1)

                def store(it, g, u):
                    dve.wait_ge(S["ps_c"], g + 1)
                    c = ps[6 + u][:, :].rearrange("p (b c) -> p b c", b=GB)
                    for q in range(GB):
                        o = (q % 2) * H
                        i = dve.scalar_tensor_tensor(H_all[:, bass.ds(g * GB + q, 1), :], c[:, q:q + 1, o:o + H],
                                                     cst[:, C_RC:C_RC + 1], H_all[:, bass.ds(g * GB + q, 1), :],
                                                     ALU.mult, ALU.add)
                    i.then_inc(S["h"], 1)

                def step(it):
                    for f in (norm, attend, store):
                        for u in range(2):
                            f(it, 2 * it + u, u)
                step(0)
                with dve.Fori(1, NG // 2) as it:
                    step(it)

            @block.scalar
            def _(act):
                act.wait_ge(S["zeroed"], 3)

                def turned(it, g, u):
                    act.wait_ge(S["ps_xt"], g + 1)
                    at_least(act, S["ps_l"], g - 1)
                    act.activation(xt[:, u, :, :].rearrange("p a b -> p (a b)"), ps[u][:, 0:2 * T], ACT.Copy).then_inc(S["xt"], 1)

                def queries(it, g, u):
                    act.wait_ge(S["ps_v"], g + 1)
                    at_least(act, S["ps_l"], g - 1)
                    for k in range(2):
                        r = slice(k * H, (k + 1) * H)
                        i = act.activation(ubd[r, u, :, k * T:(k + 1) * T],
                                           ps[2 + u][r, 0:2 * T].rearrange("p (a b) -> p a b", a=2), ACT.Copy)
                    i.then_inc(S["u"], 1)

                def values(it, g, u):
                    act.wait_ge(S["ps_v"], g + 1)
                    at_least(act, S["ps_c"], g - 1)
                    act.activation(val[:, u, :, :].rearrange("p a b -> p (a b)"), ps[2 + u][:, 256:512], ACT.Copy).then_inc(S["v"], 1)

                def step(it):
                    for f in (turned, queries, values):
                        for u in range(2):
                            f(it, 2 * it + u, u)
                step(0)
                with act.Fori(1, NG // 2) as it:
                    step(it)

            @block.tensor
            def _(pe):
                pe.wait_ge(S["w4"], 64)
                for k in range(2):
                    r = slice(k * H, (k + 1) * H)
                    pe.matmul(ps[0][r, 0:H], w4[:, 0, :], w4[:, 1, :], start=True, stop=True)
                    m = pe.matmul(ps[0][r, H:2 * H], w4[:, 2, :], w4[:, 3, :], start=True, stop=True)
                m.then_inc(S["ps_w"], 1)
                pe.wait_ge(S["w"], 4)

                def turn(it, g, u):
                    pe.wait_ge(S["xn"], g + 1)
                    at_least(pe, S["xt"], g - 1)
                    for p in range(2):
                        m = pe.transpose(ps[u][:, p * T:(p + 1) * T], xn[:, u, 2 * p:2 * p + 2, :].rearrange("p b c -> p (b c)"), ident)
                    m.then_inc(S["ps_xt"], 1)

                def project(it, g, u):
                    pe.wait_ge(S["xt"], g + 1)
                    at_least(pe, S["v"], g - 1)
                    pe.matmul(ps[2 + u][:, 0:2 * T], w_qk[:], xt[:, u, :, :].rearrange("p a b -> p (a b)"), start=True, stop=True)
                    for p in range(2):
                        m = pe.matmul(ps[2 + u][:, 256 + p * 128:256 + (p + 1) * 128], xt[:, u, p, :], w_vo[:], start=True, stop=True)
                    m.then_inc(S["ps_v"], 1)

                def logits(it, g, u):
                    pe.wait_ge(S["u"], g + 1)
                    at_least(pe, S["att"], g - 1)
                    for p in range(2):
                        m = pe.matmul(ps[4 + u][:, p * 2 * T:(p + 1) * 2 * T], xt[:, u, p, :], ubd[:, u, p, :], start=True, stop=True)
                    m.then_inc(S["ps_l"], 1)

                def context(it, g, u):
                    pe.wait_ge(S["att"], g + 1)
                    pe.wait_ge(S["v"], g + 1)
                    at_least(pe, S["h"], g - 1)
                    for q in range(GB):
                        m = pe.matmul(ps[6 + u][:, q * 128:(q + 1) * 128], att[:, u, q, :], val[:, u, q // 2, :], start=True, stop=True)
                    m.then_inc(S["ps_c"], 1)

                def step(it):
                    for f in (turn, project, logits, context):
                        for u in range(2):
                            f(it, 2 * it + u, u)
                step(0)
                with pe.Fori(1, NG // 2) as it:
                    step(it)


def head_attention(nc, ins, M, ps):
    H_all, cst, mix, res = M["H"], M["cst"], M["mix"], M["res"]
    ctx = ExitStack()
    with ctx:
        def sb(name, shape, dt=F32):
            return ctx.enter_context(nc.sbuf_tensor(name, shape, dt))
        hl_d = sb("c_hl_d", [D, NH, H + 1])
        hl_t = sb("c_hl_t", [H + 1, H])
        wq_o = sb("c_wq_o", [D, NH * NE, D])
        wk_o = sb("c_wk_o", [D, NH, D])
        wv_d = sb("c_wv_d", [D, NH, D])
        qk_d = sb("c_qk_d", [D, NH, NE * D])
        w_q = sb("c_w_q", [H + 1, 2, NE, 3, 2, D])
        w_k = sb("c_w_k", [H + 1, NH, 3, 2, D])
        w_np = sb("c_w_np", [H + 1, NH, 32])
        w_v = sb("c_w_v", [H + 1, 128])
        gate_b = sb("c_gate_b", [128, NH * NE])
        onehot = sb("c_onehot", [128, 128], BF16)
        tri = sb("c_tri", [128, NH, BLK], BF16)
        sel = cst[:, C_SEL:C_SEL + 512].rearrange("p (e c) -> p e c", e=NE)

        stats = sb("c_stats", [T, 2, GB, 6])
        tmp = sb("c_tmp", [T, 2, 5, GB, 1])
        mean = sb("c_mean", [T, 2, GB, 1])
        xc = sb("c_xc", [T, 2, GB, H])
        var = sb("c_var", [T, 2, GB, 1])
        rstd = sb("c_rstd", [T, 2, GB, 1])
        xn = sb("c_xn", [T, 2, GB, H + 1])
        xt = sb("c_xt", [H + 1, 2, GB * T])
        Q = sb("c_q", [C_ROWS, 2, GB, 2, NE * T], F32R)
        K = sb("c_k", [C_ROWS, 2, NH, GB, T], F32R)
        V = sb("c_v", [T, 2, GB, NH, 32])
        live = sb("c_live", [128, 2, GB, T])
        nmax = sb("c_nmax", [128, 2, GB, 16])
        nmax2 = sb("c_nmax2", [128, 2, GB, 2, 2, 8], F32R)
        nmax_t = sb("c_nmax_t", [128, 2, 128])
        P = sb("c_p", [T, 2, NH, NE * T])
        om = sb("c_om", [128, 2, NE, T])
        rs = sb("c_rs", [T, 2, GB, NE, NH])
        oz = sb("c_oz", [T, 2, GB, NE, NH, D])
        ty = sb("c_ty", [T, 2, GB, NE, NH * NE])
        lg = sb("c_lg", [T, 2, GB, NH * NE])
        lm = sb("c_lm", [T, 2, GB, NH])
        ls = sb("c_ls", [T, 2, GB, NH])
        li = sb("c_li", [T, 2, GB, NH])
        eg = sb("c_eg", [T, 2, GB, NH * NE])
        gs = sb("c_gs", [T, 2, GB, NH * NE])

        S = signals(nc, ctx, "c", "w zeroed ps_w1 ps_w2 qk_d built stats sums mean xc var rstd xn ps_xt xt ps_k kr kl ps_np live ps_v v "
                    "ps_q qr ql ps_mx mx nmax2r nmax2 ps_ct ct cmax0 cmax1 ps_s ex sel ps_o om ps_z rs oz "
                    "lg0 lg1 lm lg2 eg ls li gs prod mix res")
        ident = cst[:, C_ID:C_ID + 128]
        PJ, MXB, SB_, OB, ZB = ps[0:2], ps[2:4], ps[4:6], ps[6], ps[7]

        TASKS = ["xt"] + ["k"] * 4 + ["np", "v"] + ["q"] * 8 + ["ct"]

        def release(pe, t, g):
            t -= 2
            if t < 0:
                t, g = t + len(TASKS), g - 1
            kind, k = TASKS[t], TASKS[:t].count(TASKS[t])
            of = {"xt": ("xt", 1), "k": ("kl", 4), "np": ("live", 1), "v": ("v", 1), "q": ("ql", 8), "ct": ("ct", 1)}[kind]
            at_least(pe, S[of[0]], g * of[1] + k + 1)

        with nc.Block() as block:
            @block.sync
            def _(sp):
                sp.dma_start(hl_d[:], ins["hl_d"]).then_inc(S["w"], 16)
                sp.dma_start(hl_t[:], ins["hl_t"]).then_inc(S["w"], 16)
                sp.dma_start(wq_o[:], ins["wq_o"]).then_inc(S["w"], 16)
                sp.dma_start(wk_o[:], ins["wk_o"]).then_inc(S["w"], 16)
                sp.dma_start(wv_d[:], ins["wv_d"]).then_inc(S["w"], 16)
                sp.dma_start(gate_b[:], ins["gate_b"].to_broadcast([128, NH * NE])).then_inc(S["w"], 16)
                for n in range(NH):
                    sp.dma_start(sel[32 * n:32 * n + D, :, 80 + 4 * n:84 + 4 * n], ins["gate_w"][n]).then_inc(S["w"], 16)

                def maxima(g, u):
                    sp.wait_ge(S["ct"], g + 1)
                    for b in range(GB):
                        sp.dma_start(Q[Q_ROWS:C_ROWS, u, b, :, :].bitcast(F32), nmax_t[32 * b:32 * b + 32, u, :]).then_inc(S[f"cmax{u}"], 16)
                maxima(0, 0)
                maxima(1, 1)
                with sp.Fori(1, NG // 2) as it:
                    maxima(2 * it, 0)
                    maxima(2 * it + 1, 1)

            @block.gpsimd
            def _(pool):
                for t in (w_q, w_k, w_np, V):
                    i = pool.memset(t[:], 0.0).then_inc(S["zeroed"], 1)
                pool.wait_ge(S["zeroed"], 4)
                pool.memset(w_np[H:H + 1, :, D:32], 1.0).then_inc(S["zeroed"], 1)
                pool.wait_ge(S["zeroed"], 5)
                pool.memset(V[:, :, :, :, D:D + 1].rearrange("p u b n o -> p (u b n) o"), 1.0).then_inc(S["zeroed"], 1)
                pool.memset(xn[:, :, :, H:H + 1].rearrange("p u b o -> p (u b) o"), 1.0).then_inc(S["zeroed"], 1)

                def norm(g, u):
                    pool.wait_ge(S["var"], g + 1)
                    pool.tensor_tensor(rstd[:, u, :, :], var[:, u, :, :],
                                       cst[:, C_NHALF:C_NHALF + 1].rearrange("p (o c) -> p o c", o=1).to_broadcast([T, GB, 1]),
                                       ALU.pow).then_inc(S["rstd"], 1)
                    pool.wait_ge(S["rstd"], g + 1)
                    at_least(pool, S["ps_xt"], g - 1)
                    pool.tensor_tensor(xn[:, u, :, 0:H], xc[:, u], rstd[:, u].to_broadcast([T, GB, H]), ALU.mult).then_inc(S["xn"], 1)

                def select(g, b):
                    for m in range(2):
                        pool.wait_ge(S["ex"], 4 * (GB * g + b) + 2 * m + 2)
                        for h in range(2):
                            v = P[:, b % 2, 2 * m + h, :].rearrange("p (a e s) -> p a e s", a=NBLK, e=NE)
                            if h == 0:
                                pool.tensor_tensor(v[:, 0], v[:, 0], cst[:, C_KEEP_ML:C_KEEP_ML + BLK].rearrange("p (o s) -> p o s", o=1)
                                                   .to_broadcast([T, NE, BLK]), ALU.mult)
                            a = 1 - h
                            i = pool.affine_select(out=v[:, a:], in_=v[:, a:], compare_op=ALU.is_ge, fill=0.0, base=a * BLK,
                                                   pattern=[[BLK, NBLK - a], [0, NE], [1, BLK]], channel_multiplier=-1)
                        i.then_inc(S["sel"], 1)

                def mixing(g, u):
                    pool.wait_ge(S["gs"], g + 1)
                    for b in range(GB):
                        w = gs[:, u, b, :].rearrange("p (n e o) -> p e n o", n=NH, o=1)
                        i = pool.tensor_tensor(oz[:, u, b], oz[:, u, b], w.to_broadcast([T, NE, NH, D]), ALU.mult)
                    i.then_inc(S["prod"], 1)

                def step(g, u, front):
                    for b in range(GB):
                        select(g, b)
                        if b == 1 and not (isinstance(g, int) and g == 0):
                            mixing(g - 1, 1 - u)
                    if front == 2:
                        norm(g + 2, u)
                norm(0, 0)
                norm(1, 1)
                pipeline(pool, step)
                mixing(NG - 1, 1)

            @block.vector
            def _(dve):
                dve.tensor_copy(onehot[:], cst[:, C_ONEHOT:C_ONEHOT + 128]).then_inc(S["built"], 1)
                dve.tensor_copy(tri[:].rearrange("p n s -> p (n s)"), cst[:, C_TRI:C_TRI + 128]).then_inc(S["built"], 1)
                for u in range(2):
                    for b in range(GB):
                        dve.tensor_copy(K[Q_ROWS:C_ROWS, u, :, b, :],
                                        cst[Q_ROWS:C_ROWS, C_OWN:C_OWN + 512].rearrange("p (n t) -> p n t", n=NH)).then_inc(S["built"], 1)
                dve.wait_ge(S["w"], 160)
                dve.wait_ge(S["zeroed"], 7)
                dve.tensor_copy(w_np[:, :, 0:D], hl_t[:].rearrange("h (n d) -> h n d", n=NH)).then_inc(S["built"], 1)
                dve.tensor_copy(w_v[:, H:2 * H], hl_t[:]).then_inc(S["built"], 1)
                for n in range(NH):
                    for r in range(3):
                        dve.tensor_copy(w_k[:, n, r, n % 2, :], hl_t[:, n * D:(n + 1) * D]).then_inc(S["built"], 1)
                dve.wait_ge(S["ps_w1"], 1)
                dve.tensor_scalar(qk_d[:].rearrange("d n c -> d (n c)"), ps[0][0:D, 0:NH * NE * D], float(D) ** 0.5, None,
                                  ALU.mult).then_inc(S["qk_d"], 1)
                dve.wait_ge(S["ps_w2"], 1)
                dve.tensor_copy(w_v[:, 0:H], ps[2][0:H + 1, 0:H]).then_inc(S["built"], 1)
                for n in range(NH):
                    for r in range(3):
                        dve.tensor_copy(w_q[:, n // 2, :, r, n % 2, :],
                                        ps[1][0:H + 1, n * 64:(n + 1) * 64].rearrange("h (e d) -> h e d", e=NE)).then_inc(S["built"], 1)

                def stat(g, u):
                    at_least(dve, S["xn"], g - 1)
                    norm_stats(dve, H_all[:, bass.ds(g * GB, GB), :], stats[:, u], tmp[:, u], mean[:, u], var[:, u], xc[:, u], S, g)

                def k_rest(g, u):
                    for n in range(NH):
                        dve.wait_ge(S["kr"], NH * g + n + 1)
                        k = K[64:96, u, n, :, :].rearrange("p b t -> p (b t)")
                        dve.tensor_tensor(k, PJ[(1 + n) % 2][64:96, :], k.bitcast(F32), ALU.subtract).then_inc(S["kl"], 1)

                def alive(g, u):
                    dve.wait_ge(S["ps_np"], g + 1)
                    at_least(dve, S["om"], GB * (g - 1))
                    dve.tensor_scalar(live[:, u, :, :].rearrange("p b s -> p (b s)"), PJ[5 % 2][:, :], 0.0, None,
                                      ALU.not_equal).then_inc(S["live"], 1)

                def q_rest(g, u, k0):
                    for k in range(k0, k0 + 4):
                        dve.wait_ge(S["qr"], 8 * g + k + 1)
                        m, e = k // NE, k % NE
                        q = Q[32:64, u, :, m, :].rearrange("p b (a e s) -> p b a e s", a=NBLK, e=NE)[:, :, :, e, :]
                        dve.tensor_tensor(q, PJ[(7 + k) % 2][32:64, :].rearrange("p (b a s) -> p b a s", b=GB, s=BLK), q.bitcast(F32),
                                          ALU.subtract).then_inc(S["ql"], 1)

                def maxima(g, u, b):
                    out = nmax[:, u, b, :].rearrange("p (k m a) -> p m k a", k=2, m=2)
                    for j, blocks in enumerate(((3,), (2, 0), (1,))):
                        at = 0
                        dve.wait_ge(S["ps_mx"], 3 * (GB * g + b) + j + 1)
                        if b == 0 and j == 0:
                            at_least(dve, S["nmax2"], g - 1)
                        for a in blocks:
                            w = BLK * (a + 1)
                            i = dve.tensor_reduce(out[:, :, :, a], MXB[(3 * b + j) % 2][:, at:at + NH * w]
                                                  .rearrange("p (m k w) -> p m k w", m=2, k=2), X, ALU.max, negate=True)
                            at += NH * w
                        i.then_inc(S["mx"], 1)

                def split_max(g, u):
                    dve.wait_ge(S["mx"], 3 * GB * (g + 1))
                    at_least(dve, S["ps_ct"], g - 1)
                    v = nmax[:, u, :, :].rearrange("p b (k c) -> p b k c", k=2)
                    dve.tensor_copy(nmax2[:, u, :, :, 0, :], v).then_inc(S["nmax2r"], 1)
                    dve.wait_ge(S["nmax2r"], g + 1)
                    dve.tensor_tensor(nmax2[:, u, :, :, 1, :], v, nmax2[:, u, :, :, 0, :].bitcast(F32), ALU.subtract).then_inc(S["nmax2"], 1)

                def outputs(g, u, b):
                    dve.wait_ge(S["ps_o"], GB * g + b + 1)
                    at_least(dve, S["ps_z"], GB * g + b - 1)
                    dve.tensor_tensor(om[:, b % 2].rearrange("p e (a s) -> p e a s", a=NBLK),
                                      OB[:, :].rearrange("p (a e s) -> p e a s", a=NBLK, e=NE),
                                      live[:, u, b, :].rearrange("p (o a s) -> p o a s", o=1, a=NBLK).to_broadcast([128, NE, NBLK, BLK]),
                                      ALU.mult).then_inc(S["om"], 1)

                def scale(g, u, b):
                    z = ZB[:, :].rearrange("p (e c) -> p e c", e=NE)
                    dve.wait_ge(S["ps_z"], GB * g + b + 1)
                    if b == 0:
                        at_least(dve, S["mix"], g - 1)
                    dve.reciprocal(rs[:, u, b], z[:, :, 64:68]).then_inc(S["rs"], 1)
                    dve.wait_ge(S["rs"], GB * g + b + 1)
                    r = rs[:, u, b].rearrange("p e (n o) -> p e n o", o=1)
                    dve.tensor_tensor(oz[:, u, b], z[:, :, 0:64].rearrange("p e (n d) -> p e n d", n=NH),
                                      r.to_broadcast([T, NE, NH, D]), ALU.mult)
                    dve.tensor_tensor(ty[:, u, b].rearrange("p e (n k) -> p e n k", n=NH),
                                      z[:, :, 80:96].rearrange("p e (n k) -> p e n k", n=NH),
                                      r.to_broadcast([T, NE, NH, NE]), ALU.mult).then_inc(S["oz"], 1)

                def gate_logits(g, u):
                    dve.wait_ge(S["oz"], GB * (g + 1))
                    dve.tensor_reduce(lg[:, u], ty[:, u].rearrange("p b e c -> p b c e"), X, ALU.add).then_inc(S["lg0"], 1)
                    dve.wait_ge(S["lg0"], g + 1)
                    dve.tensor_tensor(lg[:, u], lg[:, u], gate_b[:].rearrange("p (o c) -> p o c", o=1).to_broadcast([T, GB, NH * NE]),
                                      ALU.add).then_inc(S["lg1"], 1)
                    dve.wait_ge(S["lg1"], g + 1)
                    v = lg[:, u].rearrange("p b (n e) -> p (b n) e", n=NH)
                    m = lm[:, u].rearrange("p b (n o) -> p (b n) o", o=1)
                    dve.tensor_reduce(lm[:, u].rearrange("p b n -> p (b n)"), v, X, ALU.max).then_inc(S["lm"], 1)
                    dve.wait_ge(S["lm"], g + 1)
                    dve.tensor_tensor(v, v, m.to_broadcast([T, GB * NH, NE]), ALU.subtract).then_inc(S["lg2"], 1)

                def gate_weights(g, u):
                    dve.wait_ge(S["eg"], g + 1)
                    v = eg[:, u].rearrange("p b (n e) -> p (b n) e", n=NH)
                    dve.tensor_reduce(ls[:, u].rearrange("p b n -> p (b n)"), v, X, ALU.add).then_inc(S["ls"], 1)
                    dve.wait_ge(S["ls"], g + 1)
                    dve.reciprocal(li[:, u], ls[:, u]).then_inc(S["li"], 1)
                    dve.wait_ge(S["li"], g + 1)
                    dve.tensor_tensor(gs[:, u].rearrange("p b (n e) -> p (b n) e", n=NH), v,
                                      li[:, u].rearrange("p b (n o) -> p (b n) o", o=1).to_broadcast([T, GB * NH, NE]),
                                      ALU.mult).then_inc(S["gs"], 1)

                def mixed(g, u):
                    dve.wait_ge(S["prod"], g + 1)
                    dve.tensor_reduce(mix[:, bass.ds(GB * g, GB), :], oz[:, u].rearrange("p b e n d -> p b (n d) e"),
                                      X, ALU.add).then_inc(S["mix"], 1)

                def step(g, u, front):
                    f, v = g + 1, 1 - u
                    first = isinstance(g, int) and g == 0
                    if front:
                        k_rest(f, v)
                        alive(f, v)
                    if not first:
                        gate_weights(g - 1, v)
                    outputs(g, u, 0)
                    if front:
                        q_rest(f, v, 0)
                    outputs(g, u, 1)
                    scale(g, u, 0)
                    if front:
                        q_rest(f, v, 4)
                    outputs(g, u, 2)
                    scale(g, u, 1)
                    if front:
                        maxima(f, v, 0)
                    outputs(g, u, 3)
                    if front:
                        maxima(f, v, 1)
                    scale(g, u, 2)
                    if not first:
                        mixed(g - 1, v)
                    if front:
                        maxima(f, v, 2)
                    scale(g, u, 3)
                    if front:
                        maxima(f, v, 3)
                        split_max(f, v)
                    if front == 2:
                        stat(g + 2, u)
                    gate_logits(g, u)

                stat(0, 0)
                stat(1, 1)
                k_rest(0, 0)
                alive(0, 0)
                q_rest(0, 0, 0)
                q_rest(0, 0, 4)
                for b in range(GB):
                    maxima(0, 0, b)
                split_max(0, 0)
                pipeline(dve, step)
                gate_weights(NG - 1, 1)
                mixed(NG - 1, 1)

            @block.scalar
            def _(act):
                def turned(g, u):
                    act.wait_ge(S["ps_xt"], g + 1)
                    at_least(act, S["ps_q"], 8 * (g - 1))
                    act.activation(xt[:, u, :], PJ[0][0:H + 1, :], ACT.Copy).then_inc(S["xt"], 1)

                def keys(g, u):
                    for n in range(NH):
                        act.wait_ge(S["ps_k"], NH * g + n + 1)
                        at_least(act, S["ps_s"], NH * GB * (g - 1))
                        act.activation(K[0:Q_ROWS, u, n, :, :].rearrange("p b t -> p (b t)"), PJ[(1 + n) % 2][0:Q_ROWS, :],
                                       ACT.Copy).then_inc(S["kr"], 1)

                def values(g, u):
                    act.wait_ge(S["ps_v"], g + 1)
                    at_least(act, S["ps_o"], GB * (g - 1))
                    v = PJ[6 % 2][:, :].rearrange("p (b c) -> p b c", b=GB)
                    i = act.activation(V[:, u, :, :, 0:D], v[:, :, 0:H].rearrange("p b (n d) -> p b n d", n=NH), ACT.Copy)
                    if isinstance(g, int) and g == 0:
                        for n in range(NH):
                            i = act.activation(res[:, n * D:(n + 1) * D], v[:, n, H + n * D:H + (n + 1) * D], ACT.Copy)
                    i.then_inc(S["v"], 1)

                def queries(g, u, k0):
                    for k in range(k0, k0 + 4):
                        act.wait_ge(S["ps_q"], 8 * g + k + 1)
                        m, e = k // NE, k % NE
                        act.activation(Q[0:Q_ROWS, u, :, m, :].rearrange("p b (a e s) -> p b a e s", a=NBLK, e=NE)[:, :, :, e, :],
                                       PJ[(7 + k) % 2][0:Q_ROWS, :].rearrange("p (b a s) -> p b a s", b=GB, s=BLK), ACT.Copy).then_inc(S["qr"], 1)

                def maxima_out(g, u):
                    act.wait_ge(S["ps_ct"], g + 1)
                    if isinstance(g, int):
                        if g >= 2:
                            act.wait_ge(S[f"cmax{u}"], 64 * (g // 2))
                    else:
                        act.wait_ge(S[f"cmax{u}"], 64 * ((g - u) // 2))
                    act.activation(nmax_t[:, u, :], PJ[15 % 2][:, 0:128], ACT.Copy).then_inc(S["ct"], 1)

                def weights(g, b):
                    for n in range(NH):
                        act.wait_ge(S["ps_s"], NH * (GB * g + b) + n + 1)
                        at_least(act, S["ps_o"], GB * g + b - 1)
                        act.activation(P[:, b % 2, n, :], SB_[n % 2][:, :], ACT.Exp).then_inc(S["ex"], 1)

                def gates(g, u):
                    act.wait_ge(S["lg2"], g + 1)
                    act.activation(eg[:, u], lg[:, u], ACT.Exp).then_inc(S["eg"], 1)

                def step(g, u, front):
                    f, v = g + 1, 1 - u
                    if front:
                        turned(f, v)
                    if not (isinstance(g, int) and g == 0):
                        gates(g - 1, v)
                    weights(g, 0)
                    if front:
                        keys(f, v)
                        values(f, v)
                    weights(g, 1)
                    if front:
                        queries(f, v, 0)
                    weights(g, 2)
                    if front:
                        queries(f, v, 4)
                    weights(g, 3)
                    if front:
                        maxima_out(f, v)
                turned(0, 0)
                keys(0, 0)
                values(0, 0)
                queries(0, 0, 0)
                queries(0, 0, 4)
                maxima_out(0, 0)
                pipeline(act, step)
                gates(NG - 1, 1)

            @block.tensor
            def _(pe):
                pe.wait_ge(S["w"], 160)
                for k in range(NH * NE):
                    m = pe.matmul(ps[0][0:D, k * D:(k + 1) * D], wq_o[:, k, :], wk_o[:, k // NE, :], start=True, stop=True)
                m.then_inc(S["ps_w1"], 1)
                pe.wait_ge(S["qk_d"], 1)
                for n in range(NH):
                    pe.matmul(ps[2][0:H + 1, n * D:(n + 1) * D], hl_d[:, n, :], wv_d[:, n, :], start=True, stop=True)
                    m = pe.matmul(ps[1][0:H + 1, n * 64:(n + 1) * 64], hl_d[:, n, :], qk_d[:, n, :], start=True, stop=True)
                m.then_inc(S["ps_w2"], 1)
                pe.wait_ge(S["built"], 10 + 2 + 12 + 1 + 12)

                def turn(g, u):
                    pe.wait_ge(S["xn"], g + 1)
                    release(pe, 0, g)
                    for b in range(GB):
                        m = pe.transpose(PJ[0][0:H + 1, b * T:(b + 1) * T], xn[:, u, b, :], ident)
                    m.then_inc(S["ps_xt"], 1)

                def keys(g, u):
                    pe.wait_ge(S["xt"], g + 1)
                    for n in range(NH):
                        release(pe, 1 + n, g)
                        pe.matmul(PJ[(1 + n) % 2][0:Q_ROWS, :], w_k[:, n].rearrange("h r k d -> h (r k d)"), xt[:, u, :],
                                  start=True, stop=True).then_inc(S["ps_k"], 1)
                    release(pe, 5, g)
                    pe.matmul(PJ[5 % 2][:, :], w_np[:].rearrange("h n c -> h (n c)"), xt[:, u, :], start=True, stop=True)\
                        .then_inc(S["ps_np"], 1)
                    release(pe, 6, g)
                    for b in range(GB):
                        m = pe.matmul(PJ[6 % 2][:, b * 128:(b + 1) * 128], xt[:, u, b * T:(b + 1) * T], w_v[:], start=True, stop=True)
                    m.then_inc(S["ps_v"], 1)

                def queries(g, u, k0):
                    for k in range(k0, k0 + 4):
                        release(pe, 7 + k, g)
                        pe.matmul(PJ[(7 + k) % 2][0:Q_ROWS, :], w_q[:, k // NE, k % NE].rearrange("h r k d -> h (r k d)"),
                                  xt[:, u, :], start=True, stop=True).then_inc(S["ps_q"], 1)

                def maxima(g, u, b):
                    if b == 0:
                        pe.wait_ge(S["ql"], 8 * (g + 1))
                        pe.wait_ge(S["kl"], NH * (g + 1))
                    for j, blocks in enumerate(((3,), (2, 0), (1,))):
                        bank, at = MXB[(3 * b + j) % 2], 0
                        at_least(pe, S["mx"], 3 * (GB * g + b) + j - 1)
                        for a in blocks:
                            w = BLK * (a + 1)
                            o = bank[:, at:at + NH * w].rearrange("p (n w) -> p n w", n=NH)
                            pe.matmul(o[:, :, a * BLK:w], onehot[:], tri[:], start=(at == 0), stop=False, skip_group_check=True)
                            for n in range(NH):
                                q = Q[0:Q_ROWS, u, b, n // 2, a * 128:(a + 1) * 128].bitcast(BF16)
                                k = K[0:Q_ROWS, u, n, b, 0:w].bitcast(BF16)
                                m = pe.matmul(o[:, n, :], q[:, 1::2], k[:, 1::2], start=False, stop=True, skip_group_check=True)
                            at += NH * w
                        m.then_inc(S["ps_mx"], 1)

                def turn_maxima(g, u):
                    pe.wait_ge(S["nmax2"], g + 1)
                    release(pe, 15, g)
                    pe.transpose(PJ[15 % 2][:, 0:128], nmax2[:, u].rearrange("p b k r c -> p (b k r c)").bitcast(F32), ident)\
                        .then_inc(S["ps_ct"], 1)

                def scores(g, u, b):
                    if b == 0:
                        if isinstance(g, int):
                            pe.wait_ge(S[f"cmax{u}"], 64 * (g // 2 + 1))
                        else:
                            pe.wait_ge(S[f"cmax{u}"], 64 * ((g - u) // 2 + 1))
                    for n in range(NH):
                        at_least(pe, S["ex"], NH * (GB * g + b) + n - 1)
                        pe.matmul(SB_[n % 2][:, :], K[:, u, n, b, :], Q[:, u, b, n // 2, :], start=True, stop=True).then_inc(S["ps_s"], 1)

                def outputs(g, u, b):
                    pe.wait_ge(S["sel"], 2 * (GB * g + b) + 2)
                    pe.wait_ge(S["v"], g + 1)
                    at_least(pe, S["om"], GB * g + b)
                    for n in range(NH):
                        m = pe.matmul(OB[32 * n:32 * n + 32, :], V[:, u, b, n, :], P[:, b % 2, n, :], start=True, stop=True)
                    m.then_inc(S["ps_o"], 1)

                def natural(g, u, b):
                    pe.wait_ge(S["om"], GB * g + b + 1)
                    at_least(pe, S["oz"], GB * g + b)
                    for e in range(NE):
                        m = pe.matmul(ZB[:, e * 128:(e + 1) * 128], om[:, b % 2, e, :], sel[:, e, :], start=True, stop=True)
                    m.then_inc(S["ps_z"], 1)

                def step(g, u, front):
                    f, v = g + 1, 1 - u
                    if front:
                        turn(f, v)
                    scores(g, u, 0)
                    if front:
                        keys(f, v)
                    scores(g, u, 1)
                    outputs(g, u, 0)
                    if front:
                        queries(f, v, 0)
                    scores(g, u, 2)
                    outputs(g, u, 1)
                    natural(g, u, 0)
                    if front:
                        queries(f, v, 4)
                    scores(g, u, 3)
                    outputs(g, u, 2)
                    natural(g, u, 1)
                    if front:
                        maxima(f, v, 0)
                    outputs(g, u, 3)
                    if front:
                        maxima(f, v, 1)
                    natural(g, u, 2)
                    if front:
                        maxima(f, v, 2)
                    natural(g, u, 3)
                    if front:
                        maxima(f, v, 3)
                        turn_maxima(f, v)
                turn(0, 0)
                keys(0, 0)
                queries(0, 0, 0)
                queries(0, 0, 4)
                for b in range(GB):
                    maxima(0, 0, b)
                turn_maxima(0, 0)
                pipeline(pe, step)


def feed_forward(nc, ins, M, ps, out):
    H_all, cst, mix, res = M["H"], M["cst"], M["mix"], M["res"]
    DB = 8
    DG = B // DB
    NP = DB // 2
    ctx = ExitStack()
    with ctx:
        def sb(name, shape, dt=F32):
            return ctx.enter_context(nc.sbuf_tensor(name, shape, dt))
        fc = sb("d_fc", [128, 2, 128])
        fin = sb("d_fin", [128, 128 + 8])
        vec = sb("d_vec", [128, 6])
        z = sb("d_z", [T, 2, DB, H])
        zc = sb("d_zc", [T, 2, DB, H])
        sq = sb("d_sq", [T, 2, DB, H])
        y = sb("d_y", [T, 2, DB, H])
        sm = sb("d_sm", [T, 2, 4, DB * NH])
        fx = sb("d_fx", [128, 2, NP * T])
        live = sb("d_live", [128, 2, NP * T])
        r1 = sb("d_r1", [128, 2, NP * T])
        r2 = sb("d_r2", [128, 2, NP * T])
        hx = sb("d_hx", [128, 2, NP * T])
        fo = sb("d_fo", [128, 2, NP * T])
        lg = sb("d_lg", [T, 2, DB * NH])
        lw = sb("d_lw", [T, 2, DB * NH])
        lm = sb("d_lm", [T, 2, 3, DB])
        o = sb("d_o", [T, 2, DB, H])
        S = signals(nc, ctx, "d", "w zeroed z s1 m1 c1 q1 v1 w1 i1 y1 ps1 fx live ps2 r1 r2 ps3 h1 hx ps4 s2 m2 c2 q2 v2 w2 i2 y2 ps5 fo "
                    "ps6 lm lg e ls li lw o1 o2 out0 out1")
        ident = cst[:, C_ID:C_ID + 128]

        def heads(t):
            return t.rearrange("p b (n d) -> p (b n) d", n=NH)

        def each(t):
            return t.rearrange("p (c o) -> p c o", o=1).to_broadcast([T, DB * NH, D])

        def stages(eng, fs):
            def step(it):
                for f in fs:
                    for u in range(2):
                        f(2 * it + u, u)
            step(0)
            with eng.Fori(1, DG // 2) as it:
                step(it)

        with nc.Block() as block:
            @block.sync
            def _(sp):
                sp.wait_ge(S["zeroed"], 2)
                for k in range(128 // D):
                    r = slice(k * D, (k + 1) * D)
                    sp.dma_start(fc[r, 0, r], ins["fc1_t"]).then_inc(S["w"], 16)
                    sp.dma_start(fc[r, 1, r], ins["fc2_t"]).then_inc(S["w"], 16)
                    sp.dma_start(vec[r, :], ins["vectors"]).then_inc(S["w"], 16)
                for k in range(2):
                    sp.dma_start(fin[k * H:(k + 1) * H, 128 + 4 * k:132 + 4 * k], ins["fgate_t"]).then_inc(S["w"], 16)

                def store(g, u):
                    sp.wait_ge(S["o2"], g + 1)
                    sp.dma_start(out[bass.ds(g * DB, DB), :, :].rearrange("b s h -> s b h"), o[:, u]).then_inc(S[f"out{u}"], 16)
                stages(sp, [store])
                for u in range(2):
                    sp.wait_ge(S[f"out{u}"], 16 * (DG // 2))

            @block.gpsimd
            def _(pool):
                pool.memset(fc[:], 0.0).then_inc(S["zeroed"], 1)
                pool.memset(fin[:, 128:136], 0.0).then_inc(S["zeroed"], 1)

                def center(g, u):
                    pool.wait_ge(S["m1"], g + 1)
                    at_least(pool, S["y1"], g - 1)
                    pool.tensor_tensor(heads(zc[:, u]), heads(z[:, u]), each(sm[:, u, 1]), ALU.subtract).then_inc(S["c1"], 1)

                def root(g, u, k):
                    pool.wait_ge(S[f"w{k}"], g + 1)
                    pool.tensor_tensor(sm[:, u, 3], sm[:, u, 2], cst[:, C_NHALF:C_NHALF + 1].to_broadcast([T, DB * NH]), ALU.pow)\
                        .then_inc(S[f"i{k}"], 1)
                    pool.wait_ge(S[f"i{k}"], g + 1)
                    if k == 1:
                        at_least(pool, S["ps5"], g - 1)
                    pool.tensor_tensor(heads(y[:, u]), heads(zc[:, u]), each(sm[:, u, 3]), ALU.mult).then_inc(S[f"y{k}"], 1)

                def total(g, u):
                    pool.wait_ge(S["h1"], g + 1)
                    pool.tensor_tensor(hx[:, u], hx[:, u], fx[:, u], ALU.add).then_inc(S["hx"], 1)

                stages(pool, [center, lambda g, u: root(g, u, 1), total, lambda g, u: root(g, u, 2)])

            @block.vector
            def _(dve):
                dve.wait_ge(S["w"], 16 * 26)
                dve.tensor_copy(fin[:, 0:128], ident).then_inc(S["z"], 1)

                def inputs(g, u):
                    at_least(dve, S["c1"], g - 1)
                    dve.tensor_tensor(z[:, u], mix[:, bass.ds(g * DB, DB), :],
                                      res[:].rearrange("p (o c) -> p o c", o=1).to_broadcast([T, DB, H]), ALU.add).then_inc(S["z"], 1)
                    dve.wait_ge(S["z"], g + 2)
                    dve.tensor_reduce(sm[:, u, 0], heads(z[:, u]), X, ALU.add).then_inc(S["s1"], 1)
                    dve.wait_ge(S["s1"], g + 1)
                    dve.tensor_scalar(sm[:, u, 1], sm[:, u, 0], 1.0 / D, None, ALU.mult).then_inc(S["m1"], 1)

                def variance(g, u, k):
                    dve.wait_ge(S[f"q{k}"], g + 1)
                    dve.tensor_reduce(sm[:, u, 0], heads(sq[:, u]), X, ALU.add).then_inc(S[f"v{k}"], 1)
                    dve.wait_ge(S[f"v{k}"], g + 1)
                    dve.tensor_scalar(sm[:, u, 2], sm[:, u, 0], 1.0 / D, 1e-8, ALU.mult, ALU.add).then_inc(S[f"w{k}"], 1)

                def alive(g, u):
                    dve.wait_ge(S["fx"], g + 1)
                    dve.tensor_scalar(live[:, u], fx[:, u], 0.0, None, ALU.not_equal).then_inc(S["live"], 1)

                def hidden(g, u):
                    dve.wait_ge(S["r1"], g + 1)
                    dve.wait_ge(S["live"], g + 1)
                    dve.tensor_tensor(r2[:, u], r1[:, u], live[:, u], ALU.mult).then_inc(S["r2"], 1)

                def second(g, u):
                    dve.wait_ge(S["ps3"], g + 1)
                    dve.scalar_tensor_tensor(hx[:, u], ps[4 * u][:, :], vec[:, 3:4], live[:, u], ALU.add, ALU.mult).then_inc(S["h1"], 1)

                def center(g, u):
                    v = ps[4 * u + 1][:, :].rearrange("p (c d) -> p c d", d=D)
                    dve.wait_ge(S["ps4"], g + 1)
                    dve.tensor_reduce(sm[:, u, 0], v, X, ALU.add).then_inc(S["s2"], 1)
                    dve.wait_ge(S["s2"], g + 1)
                    dve.tensor_scalar(sm[:, u, 1], sm[:, u, 0], 1.0 / D, None, ALU.mult).then_inc(S["m2"], 1)
                    dve.wait_ge(S["m2"], g + 1)
                    dve.tensor_tensor(heads(zc[:, u]), v, each(sm[:, u, 1]), ALU.subtract).then_inc(S["c2"], 1)

                def logits(g, u):
                    dve.wait_ge(S["ps6"], g + 1)
                    for k in range(2):
                        v = ps[4 * u + 2 + k][:, 0:272].rearrange("p (q c) -> p q c", q=2)[:, :, 128:136].rearrange("p q (b n) -> p q b n", b=2)
                        dve.tensor_reduce(lm[:, u, 0, 4 * k:4 * k + 4].rearrange("p (q b) -> p q b", q=2), v, X, ALU.max).then_inc(S["lm"], 1)
                    dve.wait_ge(S["lm"], 2 * g + 2)
                    for k in range(2):
                        v = ps[4 * u + 2 + k][:, 0:272].rearrange("p (q c) -> p q c", q=2)[:, :, 128:136].rearrange("p q (b n) -> p q b n", b=2)
                        m = lm[:, u, 0, 4 * k:4 * k + 4].rearrange("p (q b o) -> p q b o", q=2, o=1)
                        dve.tensor_tensor(lg[:, u, 16 * k:16 * k + 16].rearrange("p (q b n) -> p q b n", q=2, b=2), v,
                                          m.to_broadcast([T, 2, 2, NH]), ALU.subtract).then_inc(S["lg"], 1)

                def gates(g, u):
                    dve.wait_ge(S["e"], g + 1)
                    v = lg[:, u].rearrange("p (b n) -> p b n", b=DB)
                    dve.tensor_reduce(lm[:, u, 1], v, X, ALU.add).then_inc(S["ls"], 1)
                    dve.wait_ge(S["ls"], g + 1)
                    dve.reciprocal(lm[:, u, 2], lm[:, u, 1]).then_inc(S["li"], 1)
                    dve.wait_ge(S["li"], g + 1)
                    dve.tensor_tensor(lw[:, u].rearrange("p (b n) -> p b n", b=DB), v,
                                      lm[:, u, 2].rearrange("p (b o) -> p b o", o=1).to_broadcast([T, DB, NH]), ALU.mult).then_inc(S["lw"], 1)
                    dve.wait_ge(S["lw"], g + 1)
                    if isinstance(g, int):
                        if g >= 2:
                            dve.wait_ge(S[f"out{u}"], 16 * (g // 2))
                    else:
                        dve.wait_ge(S[f"out{u}"], 16 * ((g - u) // 2))
                    for k in range(2):
                        v = ps[4 * u + 2 + k][:, 0:272].rearrange("p (q c) -> p q c", q=2)[:, :, 0:128].rearrange("p q (c d) -> p q c d", d=D)
                        w = lw[:, u, 16 * k:16 * k + 16].rearrange("p (q c o) -> p q c o", q=2, o=1)
                        dve.tensor_tensor(o[:, u, 4 * k:4 * k + 4, :].rearrange("p (q b) (n d) -> p q (b n) d", q=2, n=NH), v,
                                          w.to_broadcast([T, 2, 8, D]), ALU.mult).then_inc(S["o1"], 1)
                    dve.wait_ge(S["o1"], 2 * g + 2)
                    dve.tensor_tensor(o[:, u], o[:, u], H_all[:, bass.ds(g * DB, DB), :], ALU.add).then_inc(S["o2"], 1)

                stages(dve, [inputs, lambda g, u: variance(g, u, 1), alive, hidden, second, center,
                             lambda g, u: variance(g, u, 2), logits, gates])

            @block.scalar
            def _(act):
                act.wait_ge(S["w"], 16 * 26)

                def square(g, u, k):
                    act.wait_ge(S[f"c{k}"], g + 1)
                    act.activation(sq[:, u], zc[:, u], ACT.Square).then_inc(S[f"q{k}"], 1)

                def first(g, u):
                    act.wait_ge(S["ps1"], g + 1)
                    act.activation(fx[:, u], ps[4 * u][:, :], ACT.Identity, bias=vec[:, 1:2], scale=vec[:, 0:1]).then_inc(S["fx"], 1)

                def hidden(g, u):
                    act.wait_ge(S["ps2"], g + 1)
                    act.activation(r1[:, u], ps[4 * u + 1][:, :], ACT.Relu, bias=vec[:, 2:3]).then_inc(S["r1"], 1)

                def last(g, u):
                    act.wait_ge(S["ps5"], g + 1)
                    act.activation(fo[:, u], ps[4 * u][:, :], ACT.Identity, bias=vec[:, 5:6], scale=vec[:, 4:5]).then_inc(S["fo"], 1)

                def gates(g, u):
                    act.wait_ge(S["lg"], 2 * g + 2)
                    act.activation(lg[:, u], lg[:, u], ACT.Exp).then_inc(S["e"], 1)

                stages(act, [lambda g, u: square(g, u, 1), first, hidden, lambda g, u: square(g, u, 2), last, gates])

            @block.tensor
            def _(pe):
                pe.wait_ge(S["z"], 1)
                pe.wait_ge(S["w"], 16 * 26)

                def turn(g, u, k):
                    pe.wait_ge(S[f"y{k}"], g + 1)
                    for p in range(NP):
                        m = pe.transpose(ps[4 * u][:, p * T:(p + 1) * T], y[:, u, 2 * p:2 * p + 2, :].rearrange("p b c -> p (b c)"), ident)
                    m.then_inc(S["ps1" if k == 1 else "ps5"], 1)

                def first(g, u):
                    pe.wait_ge(S["fx"], g + 1)
                    pe.matmul(ps[4 * u + 1][:, :], fc[:, 0, :], fx[:, u], start=True, stop=True).then_inc(S["ps2"], 1)

                def second(g, u):
                    pe.wait_ge(S["r2"], g + 1)
                    pe.matmul(ps[4 * u][:, :], fc[:, 1, :], r2[:, u], start=True, stop=True).then_inc(S["ps3"], 1)

                def back(g, u):
                    pe.wait_ge(S["hx"], g + 1)
                    for p in range(NP):
                        m = pe.transpose(ps[4 * u + 1][:, p * 128:(p + 1) * 128], hx[:, u, p * T:(p + 1) * T], ident)
                    m.then_inc(S["ps4"], 1)

                def final(g, u):
                    pe.wait_ge(S["fo"], g + 1)
                    at_least(pe, S["o1"], 2 * (g - 1))
                    for p in range(NP):
                        m = pe.matmul(ps[4 * u + 2 + p // 2][:, (p % 2) * 136:(p % 2) * 136 + 136], fo[:, u, p * T:(p + 1) * T], fin[:],
                                      start=True, stop=True)
                    m.then_inc(S["ps6"], 1)

                stages(pe, [lambda g, u: turn(g, u, 1), first, second, back, lambda g, u: turn(g, u, 2), final])


INPUTS = ("x consts table b_oah W_in_t Wq Wk Wv Wo_t hl_d hl_t wq_o wk_o wv_d gate_b gate_w fc1_t fc2_t vectors fgate_t").split()


def build_program(nc, ins, out):
    ctx = ExitStack()
    with ctx:
        def sb(name, shape):
            return ctx.enter_context(nc.sbuf_tensor(name, shape, F32))
        M = {"H": sb("h_all", [T, B, H]),
             "mix": sb("mix", [T, B, H]),
             "res": sb("res", [T, H]),
             "cst": sb("cst", [128, N_CONST])}
        ps = [ctx.enter_context(nc.psum_tensor(f"bank{i}", [128, 512], F32)) for i in range(8)]
        token_graph(nc, ins, M, ps)
        relu_attention(nc, ins, M, ps)
        head_attention(nc, ins, M, ps)
        feed_forward(nc, ins, M, ps, out)


def kernel(**inputs):
    import concourse.bacc as _bacc
    from concourse.bass_utils import run_bass_kernel_spmd as _run

    a = {k.replace("L0_tok_", "").replace("L0_attn_", "").replace("L0_ffn_", "ffn_"): np.asarray(v) for k, v in inputs.items()}
    backwards = a["emb_table"][::-1]
    hl = np.concatenate([a["ffn_hl_w"], a["ffn_hl_b"][:, :, None]], 2)
    arrays = {
        "x": a["x"],
        "consts": shape_constants(),
        "table": np.concatenate([backwards, backwards])[:2 * T],
        "b_oah": a["b_oah"].reshape(1, H),
        "W_in_t": a["W_in"].T,
        "Wq": a["Wq"], "Wk": a["Wk"], "Wv": a["Wv"], "Wo_t": a["Wo"].T,
        "hl_d": hl.transpose(1, 0, 2),
        "hl_t": hl.transpose(2, 0, 1).reshape(H + 1, H),
        "wq_o": a["ffn_wq"].transpose(2, 0, 1, 3).reshape(D, NH * NE, D),
        "wk_o": a["ffn_wk"].transpose(1, 0, 2),
        "wv_d": a["ffn_wv"].transpose(2, 0, 1),
        "gate_b": a["ffn_gate_b"].reshape(1, NH * NE),
        "gate_w": a["ffn_gate_w"].reshape(NH, NE, NE, D).transpose(0, 3, 2, 1),
        "fc1_t": a["ffn_fc1_w"].T, "fc2_t": a["ffn_fc2_w"].T,
        "vectors": np.stack([a["ffn_" + n] for n in ("ln_g", "ln_b", "fc1_b", "fc2_b", "fnorm_g", "fnorm_b")], 1),
        "fgate_t": a["ffn_fgate_w"].T,
    }
    nc = _bacc.Bacc("TRN2", target_bir_lowering=False, num_devices=1)
    ins, data = {}, {}
    for name in INPUTS:
        v = np.ascontiguousarray(arrays[name])
        data["in_" + name] = v
        ins[name] = nc.dram_tensor("in_" + name, v.shape, mybir.dt.from_np(v.dtype), kind="ExternalInput").ap()
    out = nc.dram_tensor("out_h", (B, T, H), F32, kind="ExternalOutput").ap()
    build_program(nc, ins, out)
    return _run(nc, [data], core_ids=[0]).results[0]["out_h"]
```

```python
import numpy as np
import concourse.bass as bass
from concourse import mybir
from contextlib import ExitStack

F32 = mybir.dt.float32
F32R = mybir.dt.float32r
BF16 = mybir.dt.bfloat16
I32 = mybir.dt.int32
ALU = mybir.AluOpType
ACT = mybir.ActivationFunctionType
X = mybir.AxisListType.X

B, T, H = 128, 128, 64
NH, NE, D = 4, 4, 16
GB = 4
NG = B // GB
BLK = 32
NBLK = T // BLK

C_ID, C_KEEP_JI, C_KEEP_ML, C_ONE, C_RC = 0, 128, 256, 384, 385
C_NHALF = 386
C_ONEHOT, C_TRI, C_SEL, C_OWN = 388, 516, 644, 1156
N_CONST = 1156 + 512
NEVER = -1.0e30
Q_ROWS = 96
C_ROWS = 100


def shape_constants():
    c = np.zeros((128, N_CONST), np.float32)
    r = np.arange(128)
    c[:, C_ID:C_ID + 128] = np.eye(128)
    c[:, C_KEEP_JI:C_KEEP_JI + 128] = r[:, None] >= r[None, :]
    c[:, C_KEEP_ML:C_KEEP_ML + 128] = r[:, None] <= r[None, :]
    c[:, C_ONE] = 1.0
    c[:, C_RC] = 1.0 / np.maximum(r, 1)
    c[:, C_NHALF] = -0.5
    for e in range(NE):
        c[0:BLK, C_ONEHOT + e * BLK:C_ONEHOT + (e + 1) * BLK] = np.eye(BLK)
    for n in range(NH):
        c[0:BLK, C_TRI + n * BLK:C_TRI + (n + 1) * BLK] = np.where(r[None, :BLK] > r[:BLK, None], NEVER, 0)
    sel = c[:, C_SEL:C_SEL + 512].reshape(128, NE, 128)
    for n in range(NH):
        for d in range(D):
            sel[32 * n + d, :, 16 * n + d] = 1
        sel[32 * n + D, :, 64 + n] = 1
    own = c[:, C_OWN:C_OWN + 512].reshape(128, NH, 128)
    for n in range(NH):
        own[96 + 2 * (n % 2):98 + 2 * (n % 2), n, :] = 1
    return c


def at_least(eng, semaphore, value):
    if isinstance(value, int) and value <= 0:
        return
    eng.wait_ge(semaphore, value)


def pipeline(eng, step):
    step(0, 0, 2)
    step(1, 1, 2)
    with eng.Fori(1, NG // 2 - 1) as it:
        step(2 * it, 0, 2)
        step(2 * it + 1, 1, 2)
    step(NG - 2, 0, 1)
    step(NG - 1, 1, 0)


def signals(nc, ctx, prefix, names):
    return {n: ctx.enter_context(nc.semaphore(f"{prefix}_{n}")) for n in names.split()}


def load_inputs(nc, ctx, ins, S):
    pass


def token_graph(nc, ins, M, ps):
    H_all = M["H"]
    cst = M["cst"]
    ctx = ExitStack()
    with ctx:
        def sb(name, shape, dt=F32):
            return ctx.enter_context(nc.sbuf_tensor(name, shape, dt))
        ids = sb("a_ids", [B, T], I32)
        idf = sb("a_idf", [B, T])
        seen = sb("a_seen", [B, T])
        cnt = sb("a_cnt", [B, 4])
        row = sb("a_row", [1, B])
        row_i = sb("a_row_i", [1, B], I32)
        id_t = sb("a_id_t", [T, B])
        off_t = sb("a_off_t", [T, B])
        key_t = sb("a_key_t", [T, B])
        seen_t = sb("a_seen_t", [T, B])
        emb0 = sb("a_emb0", [1, H])
        sq0 = sb("a_sq0", [1, 2 * H])
        base = sb("a_base", [128, B // 2])
        w_in = sb("a_w_in", [128, 128])
        b_oah = sb("a_b_oah", [128, H])
        pe_rows = sb("a_pe_rows", [T, 2, GB, H + 1])
        id_rows = sb("a_id_rows", [128, 2, GB, T], I32)
        rel = sb("a_rel", [T, 2, GB, T])
        sq = sb("a_sq", [T, 2, GB, H])
        rn = sb("a_rn", [T, 2, GB, 2])
        agg = sb("a_agg", [T, 2, GB, H])
        inv = sb("a_inv", [128, 2, 4])
        xt = sb("a_xt", [128, 2, 2, T])
        S = signals(nc, ctx, "a", "ids consts weights zeroed ones idf seen count row row_i id_t off_t key_t seen_t "
                    "sq0 base ps_count ps_id ps_base pe_in0 pe_in1 row_in0 row_in1 rel sq ps_agg ps_nrm rn rn1 agg inv0 inv1 inv "
                    "ps_xt xt ps_h h")
        table = ins["table"]

        with nc.Block() as block:
            @block.sync
            def _(sp):
                sp.dma_start(ids[:], ins["x"]).then_inc(S["ids"], 16)
                sp.dma_start(cst[:], ins["consts"]).then_inc(S["consts"], 16)
                sp.dma_start(emb0[:], ins["table"][128:129, :]).then_inc(S["weights"], 16)
                sp.dma_start(b_oah[:], ins["b_oah"].to_broadcast([128, H])).then_inc(S["weights"], 16)
                sp.wait_ge(S["zeroed"], 1)
                sp.dma_start(w_in[0:H, 0:H], ins["W_in_t"]).then_inc(S["weights"], 16)
                sp.dma_start(w_in[H:128, H:128], ins["W_in_t"]).then_inc(S["weights"], 16)
                sp.wait_ge(S["row_i"], 1)
                sp.wait_ge(S["ones"], 2)

                def fetch(it):
                    for u in range(2):
                        g = 2 * it + u
                        at_least(sp, S["ps_agg"], g - 1)
                        at_least(sp, S["sq"], g - 1)
                        sp.dma_start(id_rows[:, u, :, :], ins["x"][bass.ds(g * GB, GB), :].rearrange("(o b) t -> o b t", o=1)
                                     .to_broadcast([128, GB, T])).then_inc(S[f"row_in{u}"], 16)
                        for q in range(GB):
                            first = sp.value_load(row_i[0:1, bass.ds(g * GB + q, 1)], min_val=0, max_val=T)
                            sp.dma_start(pe_rows[:, u, q, 0:H], table[bass.ds(first, T), :]).then_inc(S[f"pe_in{u}"], 16)

                fetch(0)
                with sp.Fori(1, NG // 2) as it:
                    fetch(it)

            @block.gpsimd
            def _(pool):
                pool.memset(w_in[:], 0.0).then_inc(S["zeroed"], 1)
                pool.wait_ge(S["consts"], 16)
                for u in range(2):
                    pool.memset(pe_rows[:, u, :, H:H + 1], 1.0).then_inc(S["ones"], 1)

                def step(it):
                    for u in range(2):
                        g = 2 * it + u
                        pool.wait_ge(S["inv0"], g + 1)
                        pool.tensor_tensor(inv[:, u, 2:4], inv[:, u, 0:2], cst[:, C_NHALF:C_NHALF + 1].to_broadcast([128, 2]), ALU.pow).then_inc(S["inv"], 1)
                step(0)
                with pool.Fori(1, NG // 2) as it:
                    step(it)

            @block.vector
            def _(dve):
                dve.wait_ge(S["ids"], 16)
                dve.tensor_copy(idf[:], ids[:]).then_inc(S["idf"], 1)
                dve.wait_ge(S["idf"], 1)
                dve.tensor_scalar(seen[:], idf[:], 0.0, None, ALU.not_equal).then_inc(S["seen"], 1)
                dve.wait_ge(S["seen"], 1)
                dve.tensor_reduce(cnt[:, 0:1], seen[:], X, ALU.add).then_inc(S["count"], 1)
                dve.wait_ge(S["count"], 1)
                dve.tensor_scalar(cnt[:, 1:2], cnt[:, 0:1], -1.0, float(T), ALU.mult, ALU.add).then_inc(S["count"], 1)
                dve.wait_ge(S["ps_count"], 1)
                dve.tensor_copy(row[:], ps[0][0:1, 0:B]).then_inc(S["row"], 1)
                dve.tensor_copy(row_i[:], ps[0][0:1, 0:B]).then_inc(S["row_i"], 1)
                dve.wait_ge(S["ps_id"], 1)
                dve.tensor_copy(id_t[:], ps[1][:, 0:B]).then_inc(S["id_t"], 1)
                dve.wait_ge(S["id_t"], 1)
                dve.tensor_scalar(off_t[:], id_t[:], 0.0, -0.5, ALU.is_equal, ALU.mult).then_inc(S["off_t"], 1)
                dve.tensor_scalar(seen_t[:], id_t[:], 0.0, None, ALU.not_equal).then_inc(S["seen_t"], 1)
                dve.wait_ge(S["off_t"], 1)
                dve.tensor_tensor(key_t[:], id_t[:], off_t[:], ALU.add).then_inc(S["key_t"], 1)
                dve.wait_ge(S["weights"], 64)
                for k in range(2):
                    dve.tensor_tensor(sq0[0:1, k * H:(k + 1) * H], emb0[:], emb0[:], ALU.mult).then_inc(S["sq0"], 1)
                dve.wait_ge(S["ps_base"], 1)
                dve.tensor_copy(base[:], ps[2][:, 0:B // 2]).then_inc(S["base"], 1)
                dve.wait_ge(S["base"], 1)
                dve.wait_ge(S["key_t"], 1)
                dve.wait_ge(S["seen_t"], 1)
                dve.wait_ge(S["consts"], 16)

                def graph(it, g, u):
                    dve.wait_ge(S[f"row_in{u}"], 16 * (it + 1))
                    at_least(dve, S["ps_agg"], g - 1)
                    for q in range(GB):
                        ins_ = dve.scalar_tensor_tensor(
                            rel[:, u, q, :], id_rows[:, u, q, :], key_t[:, bass.ds(g * GB + q, 1)],
                            cst[:, C_KEEP_JI:C_KEEP_JI + T], ALU.is_equal, ALU.mult)
                    ins_.then_inc(S["rel"], 1)
                    dve.wait_ge(S[f"pe_in{u}"], 16 * GB * (it + 1))
                    at_least(dve, S["ps_nrm"], g - 1)
                    for q in range(GB):
                        ins_ = dve.scalar_tensor_tensor(
                            sq[:, u, q, :], pe_rows[:, u, q, 0:H], seen_t[:, bass.ds(g * GB + q, 1)],
                            pe_rows[:, u, q, 0:H], ALU.mult, ALU.mult)
                    ins_.then_inc(S["sq"], 1)

                def mean(it, g, u):
                    a = ps[u][:, 0:GB * 66].rearrange("p (b c) -> p b c", b=GB)
                    dve.wait_ge(S["ps_agg"], g + 1)
                    dve.tensor_scalar(rn[:, u, :, 0:1], a[:, :, H:H + 1], 1.0, None, ALU.max).then_inc(S["rn"], 1)
                    dve.wait_ge(S["rn"], g + 1)
                    dve.reciprocal(rn[:, u, :, 1:2], rn[:, u, :, 0:1]).then_inc(S["rn1"], 1)
                    dve.wait_ge(S["rn1"], g + 1)
                    at_least(dve, S["ps_xt"], g - 1)
                    dve.tensor_tensor(agg[:, u, :, :], a[:, :, 0:H],
                                      rn[:, u, :, 1:2].to_broadcast([T, GB, H]), ALU.mult).then_inc(S["agg"], 1)
                    dve.wait_ge(S["ps_nrm"], g + 1)
                    at_least(dve, S["xt"], g - 1)
                    for p in range(2):
                        ins_ = dve.tensor_scalar(inv[:, u, p:p + 1], ps[2 + u][:, p:p + 1], base[:, bass.ds(2 * g + p, 1)], 1e-24,
                                                 ALU.add, ALU.max)
                    ins_.then_inc(S["inv0"], 1)

                def store(it, g, u):
                    dve.wait_ge(S["ps_h"], g + 1)
                    dve.tensor_tensor(H_all[:, bass.ds(g * GB, GB), :],
                                      ps[6 + u][:, 0:GB * H].rearrange("p (b c) -> p b c", b=GB),
                                      b_oah[:].rearrange("p (o c) -> p o c", o=1).to_broadcast([128, GB, H]), ALU.add).then_inc(S["h"], 1)

                def step(it):
                    for f in (graph, mean, store):
                        for u in range(2):
                            f(it, 2 * it + u, u)
                step(0)
                with dve.Fori(1, NG // 2) as it:
                    step(it)

            @block.scalar
            def _(act):
                def step(it):
                    for u in range(2):
                        g = 2 * it + u
                        act.wait_ge(S["ps_xt"], g + 1)
                        act.wait_ge(S["inv"], g + 1)
                        at_least(act, S["ps_h"], g - 1)
                        for p in range(2):
                            ins_ = act.activation(xt[:, u, p, :], ps[4 + u][:, p * T:(p + 1) * T], ACT.Copy,
                                                  scale=inv[:, u, 2 + p:3 + p])
                        ins_.then_inc(S["xt"], 1)
                step(0)
                with act.Fori(1, NG // 2) as it:
                    step(it)

            @block.tensor
            def _(pe):
                ident = cst[:, C_ID:C_ID + 128]
                pe.wait_ge(S["consts"], 16)
                pe.wait_ge(S["count"], 2)
                pe.transpose(ps[0][0:1, 0:B], cnt[:, 1:2], ident).then_inc(S["ps_count"], 1)
                pe.wait_ge(S["idf"], 1)
                pe.transpose(ps[1][:, 0:B], idf[:], ident).then_inc(S["ps_id"], 1)
                pe.wait_ge(S["sq0"], 2)
                pe.wait_ge(S["row"], 1)
                pairs = row[0:1, :].rearrange("o (p k) -> o k p", k=2)
                for k in range(2):
                    m = pe.matmul(ps[2][k * H:(k + 1) * H, 0:B // 2], sq0[0:1, k * H:(k + 1) * H], pairs[:, k, :],
                                  start=True, stop=True)
                m.then_inc(S["ps_base"], 1)
                pe.wait_ge(S["weights"], 64)
                pe.wait_ge(S["base"], 1)
                pe.wait_ge(S["id_t"], 1)
                pe.wait_ge(S["row_i"], 1)

                def gather(it, g, u):
                    pe.wait_ge(S["rel"], g + 1)
                    pe.wait_ge(S[f"pe_in{u}"], 16 * GB * (it + 1))
                    at_least(pe, S["agg"], g - 1)
                    for q in range(GB):
                        m = pe.matmul(ps[u][:, q * 66:q * 66 + H + 1], rel[:, u, q, :], pe_rows[:, u, q, :],
                                      start=True, stop=True)
                    m.then_inc(S["ps_agg"], 1)
                    pe.wait_ge(S["sq"], g + 1)
                    at_least(pe, S["inv0"], g - 1)
                    for p in range(2):
                        m = pe.matmul(ps[2 + u][:, p:p + 1], sq[:, u, 2 * p:2 * p + 2, :].rearrange("p b c -> p (b c)"),
                                      cst[:, C_ONE:C_ONE + 1], start=True, stop=True)
                    m.then_inc(S["ps_nrm"], 1)

                def turn(it, g, u):
                    pe.wait_ge(S["agg"], g + 1)
                    at_least(pe, S["xt"], g - 1)
                    for p in range(2):
                        m = pe.transpose(ps[4 + u][:, p * T:(p + 1) * T],
                                         agg[:, u, 2 * p:2 * p + 2, :].rearrange("p b c -> p (b c)"), ident)
                    m.then_inc(S["ps_xt"], 1)

                def project(it, g, u):
                    pe.wait_ge(S["xt"], g + 1)
                    at_least(pe, S["h"], g - 1)
                    for p in range(2):
                        m = pe.matmul(ps[6 + u][:, p * 128:(p + 1) * 128], xt[:, u, p, :], w_in[:], start=True, stop=True)
                    m.then_inc(S["ps_h"], 1)

                def step(it):
                    for f in (gather, turn, project):
                        for u in range(2):
                            f(it, 2 * it + u, u)
                step(0)
                with pe.Fori(1, NG // 2) as it:
                    step(it)


def norm_stats(dve, x, stats, tmp, mean, var, xc, S, g):
    for q in range(GB):
        i = dve.bn_stats(stats[:, q, :], x[:, q, :])
    i.then_inc(S["stats"], 1)
    dve.wait_ge(S["stats"], g + 1)
    dve.tensor_tensor(tmp[:, 0], stats[:, :, 1:2], stats[:, :, 4:5], ALU.add)
    dve.tensor_tensor(tmp[:, 1], stats[:, :, 1:2], stats[:, :, 4:5], ALU.subtract)
    dve.tensor_tensor(tmp[:, 2], stats[:, :, 2:3], stats[:, :, 5:6], ALU.add).then_inc(S["sums"], 1)
    dve.wait_ge(S["sums"], g + 1)
    dve.tensor_tensor(tmp[:, 3], tmp[:, 1], tmp[:, 1], ALU.mult)
    dve.tensor_scalar(mean[:], tmp[:, 0], 0.5, None, ALU.mult).then_inc(S["mean"], 1)
    dve.wait_ge(S["mean"], g + 1)
    dve.scalar_tensor_tensor(tmp[:, 4], tmp[:, 3], float(H // 4), tmp[:, 2], ALU.mult, ALU.add)
    dve.tensor_tensor(xc, x, mean[:].to_broadcast([T, GB, H]), ALU.subtract).then_inc(S["xc"], 1)
    dve.wait_ge(S["xc"], g + 1)
    dve.tensor_scalar(var, tmp[:, 4], 1.0 / H, 1e-5, ALU.mult, ALU.add).then_inc(S["var"], 1)


def relu_attention(nc, ins, M, ps):
    H_all, cst = M["H"], M["cst"]
    ctx = ExitStack()
    with ctx:
        def sb(name, shape, dt=F32):
            return ctx.enter_context(nc.sbuf_tensor(name, shape, dt))
        w4 = sb("b_w4", [H, 4, H])
        w_qk = sb("b_w_qk", [128, 128])
        w_vo = sb("b_w_vo", [128, 128])
        stats = sb("b_stats", [T, 2, GB, 6])
        tmp = sb("b_tmp", [T, 2, 5, GB, 1])
        mean = sb("b_mean", [T, 2, GB, 1])
        xc = sb("b_xc", [T, 2, GB, H])
        var = sb("b_var", [T, 2, GB, 1])
        rstd = sb("b_rstd", [T, 2, GB, 1])
        xn = sb("b_xn", [T, 2, GB, H])
        xt = sb("b_xt", [128, 2, 2, T])
        ubd = sb("b_ubd", [128, 2, 2, 2 * T])
        val = sb("b_val", [T, 2, 2, 2 * H])
        att = sb("b_att", [T, 2, GB, T])
        S = signals(nc, ctx, "b", "w4 zeroed ps_w w stats sums mean xc var rstd xn ps_xt xt u ps_v v ps_l att ps_c h")
        ident = cst[:, C_ID:C_ID + 128]
        with nc.Block() as block:
            @block.sync
            def _(sp):
                for k, n in enumerate(("Wq", "Wk", "Wv", "Wo_t")):
                    sp.dma_start(w4[:, k, :], ins[n]).then_inc(S["w4"], 16)

            @block.gpsimd
            def _(pool):
                for t in (w_qk, w_vo, ubd):
                    i = pool.memset(t[:], 0.0).then_inc(S["zeroed"], 1)

                def step(it):
                    for u in range(2):
                        g = 2 * it + u
                        pool.wait_ge(S["var"], g + 1)
                        pool.tensor_tensor(rstd[:, u, :, :], var[:, u, :, :], cst[:, C_NHALF:C_NHALF + 1].rearrange("p (o c) -> p o c", o=1).to_broadcast([T, GB, 1]),
                                           ALU.pow).then_inc(S["rstd"], 1)
                        pool.wait_ge(S["rstd"], g + 1)
                        at_least(pool, S["ps_xt"], g - 1)
                        pool.tensor_tensor(xn[:, u], xc[:, u], rstd[:, u].to_broadcast([T, GB, H]), ALU.mult).then_inc(S["xn"], 1)
                step(0)
                with pool.Fori(1, NG // 2) as it:
                    step(it)

            @block.vector
            def _(dve):
                dve.wait_ge(S["ps_w"], 1)
                dve.wait_ge(S["zeroed"], 3)
                for k in range(2):
                    r = slice(k * H, (k + 1) * H)
                    dve.tensor_copy(w_qk[r, r], ps[0][r, 0:H]).then_inc(S["w"], 1)
                    dve.tensor_copy(w_vo[r, r], ps[0][r, H:2 * H]).then_inc(S["w"], 1)

                def norm(it, g, u):
                    at_least(dve, S["xn"], g - 1)
                    norm_stats(dve, H_all[:, bass.ds(g * GB, GB), :], stats[:, u], tmp[:, u], mean[:, u], var[:, u], xc[:, u], S, g)

                def attend(it, g, u):
                    dve.wait_ge(S["ps_l"], g + 1)
                    at_least(dve, S["ps_c"], g - 1)
                    dve.scalar_tensor_tensor(att[:, u, :, :], ps[4 + u][:, :].rearrange("p (b l) -> p b l", b=GB), 0.0,
                                             cst[:, C_KEEP_ML:C_KEEP_ML + T].rearrange("p (o l) -> p o l", o=1)
                                             .to_broadcast([T, GB, T]), ALU.max, ALU.mult).then_inc(S["att"], 1)

                def store(it, g, u):
                    dve.wait_ge(S["ps_c"], g + 1)
                    c = ps[6 + u][:, :].rearrange("p (b c) -> p b c", b=GB)
                    for q in range(GB):
                        o = (q % 2) * H
                        i = dve.scalar_tensor_tensor(H_all[:, bass.ds(g * GB + q, 1), :], c[:, q:q + 1, o:o + H],
                                                     cst[:, C_RC:C_RC + 1], H_all[:, bass.ds(g * GB + q, 1), :],
                                                     ALU.mult, ALU.add)
                    i.then_inc(S["h"], 1)

                def step(it):
                    for f in (norm, attend, store):
                        for u in range(2):
                            f(it, 2 * it + u, u)
                step(0)
                with dve.Fori(1, NG // 2) as it:
                    step(it)

            @block.scalar
            def _(act):
                act.wait_ge(S["zeroed"], 3)

                def turned(it, g, u):
                    act.wait_ge(S["ps_xt"], g + 1)
                    at_least(act, S["ps_l"], g - 1)
                    act.activation(xt[:, u, :, :].rearrange("p a b -> p (a b)"), ps[u][:, 0:2 * T], ACT.Copy).then_inc(S["xt"], 1)

                def queries(it, g, u):
                    act.wait_ge(S["ps_v"], g + 1)
                    at_least(act, S["ps_l"], g - 1)
                    for k in range(2):
                        r = slice(k * H, (k + 1) * H)
                        i = act.activation(ubd[r, u, :, k * T:(k + 1) * T],
                                           ps[2 + u][r, 0:2 * T].rearrange("p (a b) -> p a b", a=2), ACT.Copy)
                    i.then_inc(S["u"], 1)

                def values(it, g, u):
                    act.wait_ge(S["ps_v"], g + 1)
                    at_least(act, S["ps_c"], g - 1)
                    act.activation(val[:, u, :, :].rearrange("p a b -> p (a b)"), ps[2 + u][:, 256:512], ACT.Copy).then_inc(S["v"], 1)

                def step(it):
                    for f in (turned, queries, values):
                        for u in range(2):
                            f(it, 2 * it + u, u)
                step(0)
                with act.Fori(1, NG // 2) as it:
                    step(it)

            @block.tensor
            def _(pe):
                pe.wait_ge(S["w4"], 64)
                for k in range(2):
                    r = slice(k * H, (k + 1) * H)
                    pe.matmul(ps[0][r, 0:H], w4[:, 0, :], w4[:, 1, :], start=True, stop=True)
                    m = pe.matmul(ps[0][r, H:2 * H], w4[:, 2, :], w4[:, 3, :], start=True, stop=True)
                m.then_inc(S["ps_w"], 1)
                pe.wait_ge(S["w"], 4)

                def turn(it, g, u):
                    pe.wait_ge(S["xn"], g + 1)
                    at_least(pe, S["xt"], g - 1)
                    for p in range(2):
                        m = pe.transpose(ps[u][:, p * T:(p + 1) * T], xn[:, u, 2 * p:2 * p + 2, :].rearrange("p b c -> p (b c)"), ident)
                    m.then_inc(S["ps_xt"], 1)

                def project(it, g, u):
                    pe.wait_ge(S["xt"], g + 1)
                    at_least(pe, S["v"], g - 1)
                    pe.matmul(ps[2 + u][:, 0:2 * T], w_qk[:], xt[:, u, :, :].rearrange("p a b -> p (a b)"), start=True, stop=True)
                    for p in range(2):
                        m = pe.matmul(ps[2 + u][:, 256 + p * 128:256 + (p + 1) * 128], xt[:, u, p, :], w_vo[:], start=True, stop=True)
                    m.then_inc(S["ps_v"], 1)

                def logits(it, g, u):
                    pe.wait_ge(S["u"], g + 1)
                    at_least(pe, S["att"], g - 1)
                    for p in range(2):
                        m = pe.matmul(ps[4 + u][:, p * 2 * T:(p + 1) * 2 * T], xt[:, u, p, :], ubd[:, u, p, :], start=True, stop=True)
                    m.then_inc(S["ps_l"], 1)

                def context(it, g, u):
                    pe.wait_ge(S["att"], g + 1)
                    pe.wait_ge(S["v"], g + 1)
                    at_least(pe, S["h"], g - 1)
                    for q in range(GB):
                        m = pe.matmul(ps[6 + u][:, q * 128:(q + 1) * 128], att[:, u, q, :], val[:, u, q // 2, :], start=True, stop=True)
                    m.then_inc(S["ps_c"], 1)

                def step(it):
                    for f in (turn, project, logits, context):
                        for u in range(2):
                            f(it, 2 * it + u, u)
                step(0)
                with pe.Fori(1, NG // 2) as it:
                    step(it)


def head_attention(nc, ins, M, ps):
    H_all, cst, mix, res = M["H"], M["cst"], M["mix"], M["res"]
    ctx = ExitStack()
    with ctx:
        def sb(name, shape, dt=F32):
            return ctx.enter_context(nc.sbuf_tensor(name, shape, dt))
        hl_d = sb("c_hl_d", [D, NH, H + 1])
        hl_t = sb("c_hl_t", [H + 1, H])
        wq_o = sb("c_wq_o", [D, NH * NE, D])
        wk_o = sb("c_wk_o", [D, NH, D])
        wv_d = sb("c_wv_d", [D, NH, D])
        qk_d = sb("c_qk_d", [D, NH, NE * D])
        w_q = sb("c_w_q", [128, 2, NE, 3, 2, D])
        w_k = sb("c_w_k", [128, NH, 3, 2, D])
        w_np = sb("c_w_np", [128, NH, 32])
        w_v = sb("c_w_v", [128, 128])
        gate_b = sb("c_gate_b", [128, NH * NE])
        onehot = sb("c_onehot", [128, 128], BF16)
        tri = sb("c_tri", [128, NH, BLK], BF16)
        sel = cst[:, C_SEL:C_SEL + 512].rearrange("p (e c) -> p e c", e=NE)

        stats = sb("c_stats", [T, 2, GB, 6])
        tmp = sb("c_tmp", [T, 2, 5, GB, 1])
        mean = sb("c_mean", [T, 2, GB, 1])
        xc = sb("c_xc", [T, 2, GB, H])
        var = sb("c_var", [T, 2, GB, 1])
        rstd = sb("c_rstd", [T, 2, GB, 1])
        xn = sb("c_xn", [T, 2, GB, H + 1])
        xt = sb("c_xt", [128, 2, GB * T])
        Q = sb("c_q", [C_ROWS, 2, GB, 2, NE * T], F32R)
        K = sb("c_k", [C_ROWS, 2, NH, GB, T], F32R)
        V = sb("c_v", [T, 2, GB, NH, 32])
        live = sb("c_live", [128, 2, GB, T])
        nmax = sb("c_nmax", [128, 2, GB, 16])
        nmax2 = sb("c_nmax2", [128, 2, GB, 2, 2, 8], F32R)
        nmax_t = sb("c_nmax_t", [128, 2, 128])
        P = sb("c_p", [T, 2, NH, NE * T])
        om = sb("c_om", [128, 2, NE, T])
        rs = sb("c_rs", [T, 2, GB, NE, NH])
        oz = sb("c_oz", [T, 2, GB, NE, NH, D])
        ty = sb("c_ty", [T, 2, GB, NE, NH * NE])
        lg = sb("c_lg", [T, 2, GB, NH * NE])
        lm = sb("c_lm", [T, 2, GB, NH])
        ls = sb("c_ls", [T, 2, GB, NH])
        li = sb("c_li", [T, 2, GB, NH])
        eg = sb("c_eg", [T, 2, GB, NH * NE])
        gs = sb("c_gs", [T, 2, GB, NH * NE])

        S = signals(nc, ctx, "c", "w zeroed ps_w1 ps_w2 qk_d built stats sums mean xc var rstd xn ps_xt xt ps_k kr kl ps_np live ps_v v "
                    "ps_q qr ql ps_mx mx nmax2r nmax2 ps_ct ct cmax0 cmax1 ps_s ex sel ps_o om ps_z rs oz "
                    "lg0 lg1 lm lg2 eg ls li gs prod mix res")
        ident = cst[:, C_ID:C_ID + 128]
        MXB, SB_, OB, ZB = ps[2:4], ps[4:6], ps[6], ps[7]

        TASKS = ["xt", "k0", "k1", "ct", "k2", "k3", "np", "v"] + [f"q{k}" for k in range(8)]

        def bank(task):
            return ps[TASKS.index(task) % 4]

        def release(pe, task, g):
            t = TASKS.index(task) - 4
            if t in (-2, -1):
                at_least(pe, S["mx"], 3 * GB * g)
            elif t in (-4, -3):
                at_least(pe, S["ql"], 8 * (g - 1) + 5 + t + 4 if not (isinstance(g, int) and g == 0) else 0)
            elif TASKS[t] == "ct":
                at_least(pe, S["ct"], g)
            elif TASKS[t][0] == "k":
                pe.wait_ge(S["kl"], NH * g + int(TASKS[t][1]) + 1)
            elif TASKS[t][0] == "q":
                pe.wait_ge(S["ql"], 8 * g + int(TASKS[t][1]) + 1)
            else:
                pe.wait_ge(S["live" if TASKS[t] == "np" else TASKS[t]], g + 1)

        with nc.Block() as block:
            @block.sync
            def _(sp):
                sp.dma_start(hl_d[:], ins["hl_d"]).then_inc(S["w"], 16)
                sp.dma_start(hl_t[:], ins["hl_t"]).then_inc(S["w"], 16)
                sp.dma_start(wq_o[:], ins["wq_o"]).then_inc(S["w"], 16)
                sp.dma_start(wk_o[:], ins["wk_o"]).then_inc(S["w"], 16)
                sp.dma_start(wv_d[:], ins["wv_d"]).then_inc(S["w"], 16)
                sp.dma_start(gate_b[:], ins["gate_b"].to_broadcast([128, NH * NE])).then_inc(S["w"], 16)
                for n in range(NH):
                    sp.dma_start(sel[32 * n:32 * n + D, :, 80 + 4 * n:84 + 4 * n], ins["gate_w"][n]).then_inc(S["w"], 16)

                def maxima(g, u):
                    sp.wait_ge(S["ct"], g + 1)
                    for b in range(GB):
                        sp.dma_start(Q[Q_ROWS:C_ROWS, u, b, :, :].bitcast(F32), nmax_t[32 * b:32 * b + 32, u, :]).then_inc(S[f"cmax{u}"], 16)
                maxima(0, 0)
                maxima(1, 1)
                with sp.Fori(1, NG // 2) as it:
                    maxima(2 * it, 0)
                    maxima(2 * it + 1, 1)

            @block.gpsimd
            def _(pool):
                for t in (w_q, w_k, w_np, V, w_v, xt):
                    i = pool.memset(t[:], 0.0).then_inc(S["zeroed"], 1)
                pool.wait_ge(S["zeroed"], 6)
                pool.memset(w_np[H:H + 1, :, D:32], 1.0).then_inc(S["zeroed"], 1)
                pool.wait_ge(S["zeroed"], 7)
                pool.memset(V[:, :, :, :, D:D + 1].rearrange("p u b n o -> p (u b n) o"), 1.0).then_inc(S["zeroed"], 1)
                pool.memset(xn[:, :, :, H:H + 1].rearrange("p u b o -> p (u b) o"), 1.0).then_inc(S["zeroed"], 1)

                def norm(g, u):
                    pool.wait_ge(S["var"], g + 1)
                    pool.tensor_tensor(rstd[:, u, :, :], var[:, u, :, :],
                                       cst[:, C_NHALF:C_NHALF + 1].rearrange("p (o c) -> p o c", o=1).to_broadcast([T, GB, 1]),
                                       ALU.pow).then_inc(S["rstd"], 1)
                    pool.wait_ge(S["rstd"], g + 1)
                    at_least(pool, S["ps_xt"], g - 1)
                    pool.tensor_tensor(xn[:, u, :, 0:H], xc[:, u], rstd[:, u].to_broadcast([T, GB, H]), ALU.mult).then_inc(S["xn"], 1)

                def select(g, b):
                    for m in range(2):
                        pool.wait_ge(S["ex"], 4 * (GB * g + b) + 2 * m + 2)
                        for h in range(2):
                            v = P[:, b % 2, 2 * m + h, :].rearrange("p (a e s) -> p a e s", a=NBLK, e=NE)
                            if h == 0:
                                pool.tensor_tensor(v[:, 0], v[:, 0], cst[:, C_KEEP_ML:C_KEEP_ML + BLK].rearrange("p (o s) -> p o s", o=1)
                                                   .to_broadcast([T, NE, BLK]), ALU.mult)
                            a = 1 - h
                            i = pool.affine_select(out=v[:, a:], in_=v[:, a:], compare_op=ALU.is_ge, fill=0.0, base=a * BLK,
                                                   pattern=[[BLK, NBLK - a], [0, NE], [1, BLK]], channel_multiplier=-1)
                        i.then_inc(S["sel"], 1)

                def mixing(g, u):
                    pool.wait_ge(S["gs"], g + 1)
                    for b in range(GB):
                        w = gs[:, u, b, :].rearrange("p (n e o) -> p e n o", n=NH, o=1)
                        i = pool.tensor_tensor(oz[:, u, b], oz[:, u, b], w.to_broadcast([T, NE, NH, D]), ALU.mult)
                    i.then_inc(S["prod"], 1)

                def step(g, u, front):
                    select(g, 0)
                    if not (isinstance(g, int) and g == 0):
                        mixing(g - 1, 1 - u)
                    select(g, 1)
                    if front == 2:
                        norm(g + 2, u)
                    select(g, 2)
                    select(g, 3)
                norm(0, 0)
                norm(1, 1)
                pipeline(pool, step)
                mixing(NG - 1, 1)

            @block.vector
            def _(dve):
                dve.tensor_copy(onehot[:], cst[:, C_ONEHOT:C_ONEHOT + 128]).then_inc(S["built"], 1)
                dve.tensor_copy(tri[:].rearrange("p n s -> p (n s)"), cst[:, C_TRI:C_TRI + 128]).then_inc(S["built"], 1)
                for u in range(2):
                    for b in range(GB):
                        dve.tensor_copy(K[Q_ROWS:C_ROWS, u, :, b, :],
                                        cst[Q_ROWS:C_ROWS, C_OWN:C_OWN + 512].rearrange("p (n t) -> p n t", n=NH)).then_inc(S["built"], 1)
                dve.wait_ge(S["w"], 160)
                dve.wait_ge(S["zeroed"], 9)
                dve.tensor_copy(w_np[0:H + 1, :, 0:D], hl_t[:].rearrange("h (n d) -> h n d", n=NH)).then_inc(S["built"], 1)
                dve.tensor_copy(w_v[0:H + 1, H:2 * H], hl_t[:]).then_inc(S["built"], 1)
                for n in range(NH):
                    for r in range(3):
                        dve.tensor_copy(w_k[0:H + 1, n, r, n % 2, :], hl_t[:, n * D:(n + 1) * D]).then_inc(S["built"], 1)
                dve.wait_ge(S["ps_w1"], 1)
                dve.tensor_scalar(qk_d[:].rearrange("d n c -> d (n c)"), ps[0][0:D, 0:NH * NE * D], float(D) ** 0.5, None,
                                  ALU.mult).then_inc(S["qk_d"], 1)
                dve.wait_ge(S["ps_w2"], 1)
                dve.tensor_copy(w_v[0:H + 1, 0:H], ps[2][0:H + 1, 0:H]).then_inc(S["built"], 1)
                for n in range(NH):
                    for r in range(3):
                        dve.tensor_copy(w_q[0:H + 1, n // 2, :, r, n % 2, :],
                                        ps[1][0:H + 1, n * 64:(n + 1) * 64].rearrange("h (e d) -> h e d", e=NE)).then_inc(S["built"], 1)

                def stat(g, u):
                    at_least(dve, S["xn"], g - 1)
                    norm_stats(dve, H_all[:, bass.ds(g * GB, GB), :], stats[:, u], tmp[:, u], mean[:, u], var[:, u], xc[:, u], S, g)

                def k_rest(g, u, n0):
                    for n in range(n0, n0 + 2):
                        dve.wait_ge(S["kr"], NH * g + n + 1)
                        k = K[64:96, u, n, :, :].rearrange("p b t -> p (b t)")
                        dve.tensor_tensor(k, bank(f"k{n}")[64:96, :], k.bitcast(F32), ALU.subtract).then_inc(S["kl"], 1)

                def alive(g, u):
                    dve.wait_ge(S["ps_np"], g + 1)
                    at_least(dve, S["om"], GB * (g - 1))
                    dve.tensor_scalar(live[:, u, :, :].rearrange("p b s -> p (b s)"), bank("np")[:, :], 0.0, None,
                                      ALU.not_equal).then_inc(S["live"], 1)

                def q_rest(g, u, k0, k1):
                    for k in range(k0, k1):
                        dve.wait_ge(S["qr"], 8 * g + k + 1)
                        m, e = k // NE, k % NE
                        q = Q[32:64, u, :, m, :].rearrange("p b (a e s) -> p b a e s", a=NBLK, e=NE)[:, :, :, e, :]
                        dve.tensor_tensor(q, bank(f"q{k}")[32:64, :].rearrange("p (b a s) -> p b a s", b=GB, s=BLK), q.bitcast(F32),
                                          ALU.subtract).then_inc(S["ql"], 1)

                def maxima(g, u, b):
                    out = nmax[:, u, b, :].rearrange("p (k m a) -> p m k a", k=2, m=2)
                    for j, blocks in enumerate(((3,), (2, 0), (1,))):
                        at = 0
                        dve.wait_ge(S["ps_mx"], 3 * (GB * g + b) + j + 1)
                        if b == 0 and j == 0:
                            at_least(dve, S["nmax2"], g - 1)
                        for a in blocks:
                            w = BLK * (a + 1)
                            i = dve.tensor_reduce(out[:, :, :, a], MXB[(3 * b + j) % 2][:, at:at + NH * w]
                                                  .rearrange("p (m k w) -> p m k w", m=2, k=2), X, ALU.max, negate=True)
                            at += NH * w
                        i.then_inc(S["mx"], 1)

                def split_max(g, u):
                    dve.wait_ge(S["mx"], 3 * GB * (g + 1))
                    at_least(dve, S["ps_ct"], g - 1)
                    v = nmax[:, u, :, :].rearrange("p b (k c) -> p b k c", k=2)
                    dve.tensor_copy(nmax2[:, u, :, :, 0, :], v).then_inc(S["nmax2r"], 1)
                    dve.wait_ge(S["nmax2r"], g + 1)
                    dve.tensor_tensor(nmax2[:, u, :, :, 1, :], v, nmax2[:, u, :, :, 0, :].bitcast(F32), ALU.subtract).then_inc(S["nmax2"], 1)

                def outputs(g, u, b):
                    dve.wait_ge(S["ps_o"], GB * g + b + 1)
                    at_least(dve, S["ps_z"], GB * g + b - 1)
                    dve.tensor_tensor(om[:, b % 2].rearrange("p e (a s) -> p e a s", a=NBLK),
                                      OB[:, :].rearrange("p (a e s) -> p e a s", a=NBLK, e=NE),
                                      live[:, u, b, :].rearrange("p (o a s) -> p o a s", o=1, a=NBLK).to_broadcast([128, NE, NBLK, BLK]),
                                      ALU.mult).then_inc(S["om"], 1)

                def scale(g, u, b):
                    z = ZB[:, :].rearrange("p (e c) -> p e c", e=NE)
                    dve.wait_ge(S["ps_z"], GB * g + b + 1)
                    if b == 0:
                        at_least(dve, S["mix"], g - 1)
                    dve.reciprocal(rs[:, u, b], z[:, :, 64:68]).then_inc(S["rs"], 1)
                    dve.wait_ge(S["rs"], GB * g + b + 1)
                    r = rs[:, u, b].rearrange("p e (n o) -> p e n o", o=1)
                    dve.tensor_tensor(oz[:, u, b], z[:, :, 0:64].rearrange("p e (n d) -> p e n d", n=NH),
                                      r.to_broadcast([T, NE, NH, D]), ALU.mult)
                    dve.tensor_tensor(ty[:, u, b].rearrange("p e (n k) -> p e n k", n=NH),
                                      z[:, :, 80:96].rearrange("p e (n k) -> p e n k", n=NH),
                                      r.to_broadcast([T, NE, NH, NE]), ALU.mult).then_inc(S["oz"], 1)

                def gate_logits(g, u):
                    dve.wait_ge(S["oz"], GB * (g + 1))
                    dve.tensor_reduce(lg[:, u], ty[:, u].rearrange("p b e c -> p b c e"), X, ALU.add).then_inc(S["lg0"], 1)
                    dve.wait_ge(S["lg0"], g + 1)
                    dve.tensor_tensor(lg[:, u], lg[:, u], gate_b[:].rearrange("p (o c) -> p o c", o=1).to_broadcast([T, GB, NH * NE]),
                                      ALU.add).then_inc(S["lg1"], 1)
                    dve.wait_ge(S["lg1"], g + 1)
                    v = lg[:, u].rearrange("p b (n e) -> p (b n) e", n=NH)
                    m = lm[:, u].rearrange("p b (n o) -> p (b n) o", o=1)
                    dve.tensor_reduce(lm[:, u].rearrange("p b n -> p (b n)"), v, X, ALU.max).then_inc(S["lm"], 1)
                    dve.wait_ge(S["lm"], g + 1)
                    dve.tensor_tensor(v, v, m.to_broadcast([T, GB * NH, NE]), ALU.subtract).then_inc(S["lg2"], 1)

                def gate_weights(g, u):
                    dve.wait_ge(S["eg"], g + 1)
                    v = eg[:, u].rearrange("p b (n e) -> p (b n) e", n=NH)
                    dve.tensor_reduce(ls[:, u].rearrange("p b n -> p (b n)"), v, X, ALU.add).then_inc(S["ls"], 1)
                    dve.wait_ge(S["ls"], g + 1)
                    dve.reciprocal(li[:, u], ls[:, u]).then_inc(S["li"], 1)
                    dve.wait_ge(S["li"], g + 1)
                    dve.tensor_tensor(gs[:, u].rearrange("p b (n e) -> p (b n) e", n=NH), v,
                                      li[:, u].rearrange("p b (n o) -> p (b n) o", o=1).to_broadcast([T, GB * NH, NE]),
                                      ALU.mult).then_inc(S["gs"], 1)

                def mixed(g, u):
                    dve.wait_ge(S["prod"], g + 1)
                    dve.tensor_reduce(mix[:, bass.ds(GB * g, GB), :], oz[:, u].rearrange("p b e n d -> p b (n d) e"),
                                      X, ALU.add).then_inc(S["mix"], 1)

                def step(g, u, front):
                    f, v = g + 1, 1 - u
                    if front == 2:
                        stat(g + 2, u)
                    if not (isinstance(g, int) and g == 0):
                        gate_weights(g - 1, v)
                    if front:
                        q_rest(f, v, 0, 7)
                    outputs(g, u, 0)
                    if front:
                        q_rest(f, v, 7, 8)
                    if not (isinstance(g, int) and g == 0):
                        mixed(g - 1, v)
                    if front:
                        maxima(f, v, 0)
                    outputs(g, u, 1)
                    scale(g, u, 0)
                    if front:
                        maxima(f, v, 1)
                    outputs(g, u, 2)
                    scale(g, u, 1)
                    if front:
                        maxima(f, v, 2)
                    outputs(g, u, 3)
                    scale(g, u, 2)
                    if front:
                        maxima(f, v, 3)
                        split_max(f, v)
                    if front == 2:
                        k_rest(g + 2, u, 0)
                    scale(g, u, 3)
                    if front == 2:
                        k_rest(g + 2, u, 2)
                        alive(g + 2, u)
                    gate_logits(g, u)

                stat(0, 0)
                stat(1, 1)
                k_rest(0, 0, 0)
                k_rest(0, 0, 2)
                alive(0, 0)
                q_rest(0, 0, 0, 8)
                for b in range(GB):
                    maxima(0, 0, b)
                split_max(0, 0)
                k_rest(1, 1, 0)
                k_rest(1, 1, 2)
                alive(1, 1)
                pipeline(dve, step)
                gate_weights(NG - 1, 1)
                mixed(NG - 1, 1)

            @block.scalar
            def _(act):
                def turned(g, u):
                    act.wait_ge(S["ps_xt"], g + 1)
                    if isinstance(g, int) and g == 0:
                        act.wait_ge(S["zeroed"], 9)
                    at_least(act, S["ps_q"], 8 * (g - 1))
                    act.activation(xt[0:H + 1, u, :], bank("xt")[0:H + 1, :], ACT.Copy).then_inc(S["xt"], 1)

                def keys(g, u, n0):
                    for n in range(n0, n0 + 2):
                        act.wait_ge(S["ps_k"], NH * g + n + 1)
                        at_least(act, S["ps_s"], NH * GB * (g - 1))
                        act.activation(K[0:Q_ROWS, u, n, :, :].rearrange("p b t -> p (b t)"), bank(f"k{n}")[0:Q_ROWS, :],
                                       ACT.Copy).then_inc(S["kr"], 1)

                def values(g, u):
                    act.wait_ge(S["ps_v"], g + 1)
                    at_least(act, S["ps_o"], GB * (g - 1))
                    v = bank("v")[:, :].rearrange("p (b c) -> p b c", b=GB)
                    i = act.activation(V[:, u, :, :, 0:D], v[:, :, 0:H].rearrange("p b (n d) -> p b n d", n=NH), ACT.Copy)
                    if isinstance(g, int) and g == 0:
                        for n in range(NH):
                            i = act.activation(res[:, n * D:(n + 1) * D], v[:, n, H + n * D:H + (n + 1) * D], ACT.Copy)
                    i.then_inc(S["v"], 1)

                def query(g, u, k):
                    act.wait_ge(S["ps_q"], 8 * g + k + 1)
                    m, e = k // NE, k % NE
                    act.activation(Q[0:Q_ROWS, u, :, m, :].rearrange("p b (a e s) -> p b a e s", a=NBLK, e=NE)[:, :, :, e, :],
                                       bank(f"q{k}")[0:Q_ROWS, :].rearrange("p (b a s) -> p b a s", b=GB, s=BLK), ACT.Copy).then_inc(S["qr"], 1)

                def maxima_out(g, u):
                    act.wait_ge(S["ps_ct"], g + 1)
                    if isinstance(g, int):
                        if g >= 2:
                            act.wait_ge(S[f"cmax{u}"], 64 * (g // 2))
                    else:
                        act.wait_ge(S[f"cmax{u}"], 64 * ((g - u) // 2))
                    act.activation(nmax_t[:, u, :], bank("ct")[:, 0:128], ACT.Copy).then_inc(S["ct"], 1)

                def weights(g, b, n):
                    act.wait_ge(S["ps_s"], NH * (GB * g + b) + n + 1)
                    at_least(act, S["ps_o"], GB * g + b - 1)
                    act.activation(P[:, b % 2, n, :], SB_[n % 2][:, :], ACT.Exp).then_inc(S["ex"], 1)

                def gates(g, u):
                    act.wait_ge(S["lg2"], g + 1)
                    act.activation(eg[:, u], lg[:, u], ACT.Exp).then_inc(S["eg"], 1)

                def step(g, u, front):
                    f, v = g + 1, 1 - u
                    if not (isinstance(g, int) and g == 0):
                        gates(g - 1, v)
                    for b in range(GB):
                        for n in range(NH):
                            weights(g, b, n)
                            if front and b < 2 and n > 0:
                                query(f, v, 4 * b + n - 1)
                        if front and b < 2:
                            query(f, v, 4 * b + 3)
                    if front == 2:
                        turned(g + 2, u)
                        keys(g + 2, u, 0)
                    if front:
                        maxima_out(f, v)
                    if front == 2:
                        keys(g + 2, u, 2)
                        values(g + 2, u)
                turned(0, 0)
                keys(0, 0, 0)
                keys(0, 0, 2)
                values(0, 0)
                for k in range(8):
                    query(0, 0, k)
                turned(1, 1)
                keys(1, 1, 0)
                maxima_out(0, 0)
                keys(1, 1, 2)
                values(1, 1)
                pipeline(act, step)
                gates(NG - 1, 1)

            @block.tensor
            def _(pe):
                pe.wait_ge(S["w"], 160)
                for k in range(NH * NE):
                    m = pe.matmul(ps[0][0:D, k * D:(k + 1) * D], wq_o[:, k, :], wk_o[:, k // NE, :], start=True, stop=True)
                m.then_inc(S["ps_w1"], 1)
                pe.wait_ge(S["qk_d"], 1)
                for n in range(NH):
                    pe.matmul(ps[2][0:H + 1, n * D:(n + 1) * D], hl_d[:, n, :], wv_d[:, n, :], start=True, stop=True)
                    m = pe.matmul(ps[1][0:H + 1, n * 64:(n + 1) * 64], hl_d[:, n, :], qk_d[:, n, :], start=True, stop=True)
                m.then_inc(S["ps_w2"], 1)
                pe.wait_ge(S["built"], 10 + 2 + 12 + 1 + 12)

                def turn(g, u):
                    pe.wait_ge(S["xn"], g + 1)
                    release(pe, "xt", g)
                    for b in range(GB):
                        m = pe.transpose(bank("xt")[0:H + 1, b * T:(b + 1) * T], xn[:, u, b, :], ident)
                    m.then_inc(S["ps_xt"], 1)

                def keys(g, u, n0):
                    pe.wait_ge(S["xt"], g + 1)
                    for n in range(n0, n0 + 2):
                        release(pe, f"k{n}", g)
                        pe.matmul(bank(f"k{n}")[0:Q_ROWS, :], w_k[:, n].rearrange("h r k d -> h (r k d)"), xt[:, u, :],
                                  start=True, stop=True).then_inc(S["ps_k"], 1)

                def values(g, u):
                    release(pe, "np", g)
                    pe.matmul(bank("np")[:, :], w_np[:].rearrange("h n c -> h (n c)"), xt[:, u, :], start=True, stop=True)\
                        .then_inc(S["ps_np"], 1)
                    release(pe, "v", g)
                    for b in range(GB):
                        m = pe.matmul(bank("v")[:, b * 128:(b + 1) * 128], xt[:, u, b * T:(b + 1) * T], w_v[:], start=True, stop=True)
                    m.then_inc(S["ps_v"], 1)

                def query(g, u, k):
                    release(pe, f"q{k}", g)
                    pe.matmul(bank(f"q{k}")[0:Q_ROWS, :], w_q[:, k // NE, k % NE].rearrange("h r k d -> h (r k d)"),
                              xt[:, u, :], start=True, stop=True).then_inc(S["ps_q"], 1)

                def maxima(g, u, b, j):
                    if b == 0 and j == 0:
                        pe.wait_ge(S["ql"], 8 * (g + 1))
                        pe.wait_ge(S["kl"], NH * (g + 1))
                    blocks = ((3,), (2, 0), (1,))[j]
                    held, at = MXB[(3 * b + j) % 2], 0
                    at_least(pe, S["mx"], 3 * (GB * g + b) + j - 1)
                    for a in blocks:
                        w = BLK * (a + 1)
                        o = held[:, at:at + NH * w].rearrange("p (n w) -> p n w", n=NH)
                        pe.matmul(o[:, :, a * BLK:w], onehot[:], tri[:], start=(at == 0), stop=False, skip_group_check=True)
                        for n in range(NH):
                            q = Q[0:Q_ROWS, u, b, n // 2, a * 128:(a + 1) * 128].bitcast(BF16)
                            k = K[0:Q_ROWS, u, n, b, 0:w].bitcast(BF16)
                            m = pe.matmul(o[:, n, :], q[:, 1::2], k[:, 1::2], start=False, stop=True, skip_group_check=True)
                        at += NH * w
                    m.then_inc(S["ps_mx"], 1)

                def turn_maxima(g, u):
                    pe.wait_ge(S["nmax2"], g + 1)
                    release(pe, "ct", g + 1)
                    pe.transpose(bank("ct")[:, 0:128], nmax2[:, u].rearrange("p b k r c -> p (b k r c)").bitcast(F32), ident)\
                        .then_inc(S["ps_ct"], 1)

                def scores(g, u, b, n):
                    if b == 0 and n == 0:
                        if isinstance(g, int):
                            pe.wait_ge(S[f"cmax{u}"], 64 * (g // 2 + 1))
                        else:
                            pe.wait_ge(S[f"cmax{u}"], 64 * ((g - u) // 2 + 1))
                    at_least(pe, S["ex"], NH * (GB * g + b) + n - 1)
                    pe.matmul(SB_[n % 2][:, :], K[:, u, n, b, :], Q[:, u, b, n // 2, :], start=True, stop=True).then_inc(S["ps_s"], 1)

                def outputs(g, u, b):
                    pe.wait_ge(S["sel"], 2 * (GB * g + b) + 2)
                    pe.wait_ge(S["v"], g + 1)
                    at_least(pe, S["om"], GB * g + b)
                    for n in range(NH):
                        m = pe.matmul(OB[32 * n:32 * n + 32, :], V[:, u, b, n, :], P[:, b % 2, n, :], start=True, stop=True)
                    m.then_inc(S["ps_o"], 1)

                def natural(g, u, b):
                    pe.wait_ge(S["om"], GB * g + b + 1)
                    at_least(pe, S["oz"], GB * g + b)
                    for e in range(NE):
                        m = pe.matmul(ZB[:, e * 128:(e + 1) * 128], om[:, b % 2, e, :], sel[:, e, :], start=True, stop=True)
                    m.then_inc(S["ps_z"], 1)

                def step(g, u, front):
                    f, v = g + 1, 1 - u
                    for b in range(2):
                        for n in range(NH):
                            scores(g, u, b, n)
                            if front and n > 0:
                                query(f, v, 4 * b + n - 1)
                        if b == 1:
                            outputs(g, u, 0)
                        if front:
                            query(f, v, 4 * b + 3)
                    for b in range(2):
                        for n in range(NH):
                            scores(g, u, 2 + b, n)
                            if front and n in (1, 2):
                                maxima(f, v, b, n - 1)
                        outputs(g, u, 1 + b)
                        if front:
                            maxima(f, v, b, 2)
                        natural(g, u, b)
                    if front:
                        maxima(f, v, 2, 0)
                        maxima(f, v, 2, 1)
                    outputs(g, u, 3)
                    if front:
                        maxima(f, v, 2, 2)
                    natural(g, u, 2)
                    if front:
                        maxima(f, v, 3, 0)
                        maxima(f, v, 3, 1)
                    if front == 2:
                        turn(g + 2, u)
                    if front:
                        maxima(f, v, 3, 2)
                    if front == 2:
                        keys(g + 2, u, 0)
                    natural(g, u, 3)
                    if front:
                        turn_maxima(f, v)
                    if front == 2:
                        keys(g + 2, u, 2)
                        values(g + 2, u)
                turn(0, 0)
                keys(0, 0, 0)
                keys(0, 0, 2)
                values(0, 0)
                for k in range(8):
                    query(0, 0, k)
                for b in range(GB):
                    for j in range(3):
                        maxima(0, 0, b, j)
                turn(1, 1)
                keys(1, 1, 0)
                turn_maxima(0, 0)
                keys(1, 1, 2)
                values(1, 1)
                pipeline(pe, step)


def feed_forward(nc, ins, M, ps, out):
    H_all, cst, mix, res = M["H"], M["cst"], M["mix"], M["res"]
    DB = 8
    DG = B // DB
    NP = DB // 2
    ctx = ExitStack()
    with ctx:
        def sb(name, shape, dt=F32):
            return ctx.enter_context(nc.sbuf_tensor(name, shape, dt))
        fc = sb("d_fc", [128, 2, 128])
        fin = sb("d_fin", [128, 128 + 8])
        vec = sb("d_vec", [128, 6])
        z = sb("d_z", [T, 2, DB, H])
        zc = sb("d_zc", [T, 2, DB, H])
        sq = sb("d_sq", [T, 2, DB, H])
        y = sb("d_y", [T, 2, DB, H])
        sm = sb("d_sm", [T, 2, 4, DB * NH])
        fx = sb("d_fx", [128, 2, NP * T])
        live = sb("d_live", [128, 2, NP * T])
        r1 = sb("d_r1", [128, 2, NP * T])
        r2 = sb("d_r2", [128, 2, NP * T])
        hx = sb("d_hx", [128, 2, NP * T])
        fo = sb("d_fo", [128, 2, NP * T])
        lg = sb("d_lg", [T, 2, DB * NH])
        lw = sb("d_lw", [T, 2, DB * NH])
        lm = sb("d_lm", [T, 2, 3, DB])
        o = sb("d_o", [T, 2, DB, H])
        S = signals(nc, ctx, "d", "w zeroed z s1 m1 c1 q1 v1 w1 i1 y1 ps1 fx live ps2 r1 r2 ps3 h1 hx ps4 s2 m2 c2 q2 v2 w2 i2 y2 ps5 fo "
                    "ps6 lm lg e ls li lw o1 o2 out0 out1")
        ident = cst[:, C_ID:C_ID + 128]

        def heads(t):
            return t.rearrange("p b (n d) -> p (b n) d", n=NH)

        def each(t):
            return t.rearrange("p (c o) -> p c o", o=1).to_broadcast([T, DB * NH, D])

        def stages(eng, fs):
            def step(it):
                for f in fs:
                    for u in range(2):
                        f(2 * it + u, u)
            step(0)
            with eng.Fori(1, DG // 2) as it:
                step(it)

        with nc.Block() as block:
            @block.sync
            def _(sp):
                sp.wait_ge(S["zeroed"], 2)
                for k in range(128 // D):
                    r = slice(k * D, (k + 1) * D)
                    sp.dma_start(fc[r, 0, r], ins["fc1_t"]).then_inc(S["w"], 16)
                    sp.dma_start(fc[r, 1, r], ins["fc2_t"]).then_inc(S["w"], 16)
                    sp.dma_start(vec[r, :], ins["vectors"]).then_inc(S["w"], 16)
                for k in range(2):
                    sp.dma_start(fin[k * H:(k + 1) * H, 128 + 4 * k:132 + 4 * k], ins["fgate_t"]).then_inc(S["w"], 16)

                def store(g, u):
                    sp.wait_ge(S["o2"], g + 1)
                    sp.dma_start(out[bass.ds(g * DB, DB), :, :].rearrange("b s h -> s b h"), o[:, u]).then_inc(S[f"out{u}"], 16)
                stages(sp, [store])
                for u in range(2):
                    sp.wait_ge(S[f"out{u}"], 16 * (DG // 2))

            @block.gpsimd
            def _(pool):
                pool.memset(fc[:], 0.0).then_inc(S["zeroed"], 1)
                pool.memset(fin[:, 128:136], 0.0).then_inc(S["zeroed"], 1)

                def center(g, u):
                    pool.wait_ge(S["m1"], g + 1)
                    at_least(pool, S["y1"], g - 1)
                    pool.tensor_tensor(heads(zc[:, u]), heads(z[:, u]), each(sm[:, u, 1]), ALU.subtract).then_inc(S["c1"], 1)

                def root(g, u, k):
                    pool.wait_ge(S[f"w{k}"], g + 1)
                    pool.tensor_tensor(sm[:, u, 3], sm[:, u, 2], cst[:, C_NHALF:C_NHALF + 1].to_broadcast([T, DB * NH]), ALU.pow)\
                        .then_inc(S[f"i{k}"], 1)
                    pool.wait_ge(S[f"i{k}"], g + 1)
                    if k == 1:
                        at_least(pool, S["ps5"], g - 1)
                    pool.tensor_tensor(heads(y[:, u]), heads(zc[:, u]), each(sm[:, u, 3]), ALU.mult).then_inc(S[f"y{k}"], 1)

                def total(g, u):
                    pool.wait_ge(S["h1"], g + 1)
                    pool.tensor_tensor(hx[:, u], hx[:, u], fx[:, u], ALU.add).then_inc(S["hx"], 1)

                stages(pool, [center, lambda g, u: root(g, u, 1), total, lambda g, u: root(g, u, 2)])

            @block.vector
            def _(dve):
                dve.wait_ge(S["w"], 16 * 26)
                dve.tensor_copy(fin[:, 0:128], ident).then_inc(S["z"], 1)

                def inputs(g, u):
                    at_least(dve, S["c1"], g - 1)
                    dve.tensor_tensor(z[:, u], mix[:, bass.ds(g * DB, DB), :],
                                      res[:].rearrange("p (o c) -> p o c", o=1).to_broadcast([T, DB, H]), ALU.add).then_inc(S["z"], 1)
                    dve.wait_ge(S["z"], g + 2)
                    dve.tensor_reduce(sm[:, u, 0], heads(z[:, u]), X, ALU.add).then_inc(S["s1"], 1)
                    dve.wait_ge(S["s1"], g + 1)
                    dve.tensor_scalar(sm[:, u, 1], sm[:, u, 0], 1.0 / D, None, ALU.mult).then_inc(S["m1"], 1)

                def variance(g, u, k):
                    dve.wait_ge(S[f"q{k}"], g + 1)
                    dve.tensor_reduce(sm[:, u, 0], heads(sq[:, u]), X, ALU.add).then_inc(S[f"v{k}"], 1)
                    dve.wait_ge(S[f"v{k}"], g + 1)
                    dve.tensor_scalar(sm[:, u, 2], sm[:, u, 0], 1.0 / D, 1e-8, ALU.mult, ALU.add).then_inc(S[f"w{k}"], 1)

                def alive(g, u):
                    dve.wait_ge(S["fx"], g + 1)
                    dve.tensor_scalar(live[:, u], fx[:, u], 0.0, None, ALU.not_equal).then_inc(S["live"], 1)

                def hidden(g, u):
                    dve.wait_ge(S["r1"], g + 1)
                    dve.wait_ge(S["live"], g + 1)
                    dve.tensor_tensor(r2[:, u], r1[:, u], live[:, u], ALU.mult).then_inc(S["r2"], 1)

                def second(g, u):
                    dve.wait_ge(S["ps3"], g + 1)
                    dve.scalar_tensor_tensor(hx[:, u], ps[4 * u][:, :], vec[:, 3:4], live[:, u], ALU.add, ALU.mult).then_inc(S["h1"], 1)

                def center(g, u):
                    v = ps[4 * u + 1][:, :].rearrange("p (c d) -> p c d", d=D)
                    dve.wait_ge(S["ps4"], g + 1)
                    dve.tensor_reduce(sm[:, u, 0], v, X, ALU.add).then_inc(S["s2"], 1)
                    dve.wait_ge(S["s2"], g + 1)
                    dve.tensor_scalar(sm[:, u, 1], sm[:, u, 0], 1.0 / D, None, ALU.mult).then_inc(S["m2"], 1)
                    dve.wait_ge(S["m2"], g + 1)
                    dve.tensor_tensor(heads(zc[:, u]), v, each(sm[:, u, 1]), ALU.subtract).then_inc(S["c2"], 1)

                def logits(g, u):
                    dve.wait_ge(S["ps6"], g + 1)
                    for k in range(2):
                        v = ps[4 * u + 2 + k][:, 0:272].rearrange("p (q c) -> p q c", q=2)[:, :, 128:136].rearrange("p q (b n) -> p q b n", b=2)
                        dve.tensor_reduce(lm[:, u, 0, 4 * k:4 * k + 4].rearrange("p (q b) -> p q b", q=2), v, X, ALU.max).then_inc(S["lm"], 1)
                    dve.wait_ge(S["lm"], 2 * g + 2)
                    for k in range(2):
                        v = ps[4 * u + 2 + k][:, 0:272].rearrange("p (q c) -> p q c", q=2)[:, :, 128:136].rearrange("p q (b n) -> p q b n", b=2)
                        m = lm[:, u, 0, 4 * k:4 * k + 4].rearrange("p (q b o) -> p q b o", q=2, o=1)
                        dve.tensor_tensor(lg[:, u, 16 * k:16 * k + 16].rearrange("p (q b n) -> p q b n", q=2, b=2), v,
                                          m.to_broadcast([T, 2, 2, NH]), ALU.subtract).then_inc(S["lg"], 1)

                def gates(g, u):
                    dve.wait_ge(S["e"], g + 1)
                    v = lg[:, u].rearrange("p (b n) -> p b n", b=DB)
                    dve.tensor_reduce(lm[:, u, 1], v, X, ALU.add).then_inc(S["ls"], 1)
                    dve.wait_ge(S["ls"], g + 1)
                    dve.reciprocal(lm[:, u, 2], lm[:, u, 1]).then_inc(S["li"], 1)
                    dve.wait_ge(S["li"], g + 1)
                    dve.tensor_tensor(lw[:, u].rearrange("p (b n) -> p b n", b=DB), v,
                                      lm[:, u, 2].rearrange("p (b o) -> p b o", o=1).to_broadcast([T, DB, NH]), ALU.mult).then_inc(S["lw"], 1)
                    dve.wait_ge(S["lw"], g + 1)
                    if isinstance(g, int):
                        if g >= 2:
                            dve.wait_ge(S[f"out{u}"], 16 * (g // 2))
                    else:
                        dve.wait_ge(S[f"out{u}"], 16 * ((g - u) // 2))
                    for k in range(2):
                        v = ps[4 * u + 2 + k][:, 0:272].rearrange("p (q c) -> p q c", q=2)[:, :, 0:128].rearrange("p q (c d) -> p q c d", d=D)
                        w = lw[:, u, 16 * k:16 * k + 16].rearrange("p (q c o) -> p q c o", q=2, o=1)
                        dve.tensor_tensor(o[:, u, 4 * k:4 * k + 4, :].rearrange("p (q b) (n d) -> p q (b n) d", q=2, n=NH), v,
                                          w.to_broadcast([T, 2, 8, D]), ALU.mult).then_inc(S["o1"], 1)
                    dve.wait_ge(S["o1"], 2 * g + 2)
                    dve.tensor_tensor(o[:, u], o[:, u], H_all[:, bass.ds(g * DB, DB), :], ALU.add).then_inc(S["o2"], 1)

                stages(dve, [inputs, lambda g, u: variance(g, u, 1), alive, hidden, second, center,
                             lambda g, u: variance(g, u, 2), logits, gates])

            @block.scalar
            def _(act):
                act.wait_ge(S["w"], 16 * 26)

                def square(g, u, k):
                    act.wait_ge(S[f"c{k}"], g + 1)
                    act.activation(sq[:, u], zc[:, u], ACT.Square).then_inc(S[f"q{k}"], 1)

                def first(g, u):
                    act.wait_ge(S["ps1"], g + 1)
                    act.activation(fx[:, u], ps[4 * u][:, :], ACT.Identity, bias=vec[:, 1:2], scale=vec[:, 0:1]).then_inc(S["fx"], 1)

                def hidden(g, u):
                    act.wait_ge(S["ps2"], g + 1)
                    act.activation(r1[:, u], ps[4 * u + 1][:, :], ACT.Relu, bias=vec[:, 2:3]).then_inc(S["r1"], 1)

                def last(g, u):
                    act.wait_ge(S["ps5"], g + 1)
                    act.activation(fo[:, u], ps[4 * u][:, :], ACT.Identity, bias=vec[:, 5:6], scale=vec[:, 4:5]).then_inc(S["fo"], 1)

                def gates(g, u):
                    act.wait_ge(S["lg"], 2 * g + 2)
                    act.activation(lg[:, u], lg[:, u], ACT.Exp).then_inc(S["e"], 1)

                stages(act, [lambda g, u: square(g, u, 1), first, hidden, lambda g, u: square(g, u, 2), last, gates])

            @block.tensor
            def _(pe):
                pe.wait_ge(S["z"], 1)
                pe.wait_ge(S["w"], 16 * 26)

                def turn(g, u, k):
                    pe.wait_ge(S[f"y{k}"], g + 1)
                    for p in range(NP):
                        m = pe.transpose(ps[4 * u][:, p * T:(p + 1) * T], y[:, u, 2 * p:2 * p + 2, :].rearrange("p b c -> p (b c)"), ident)
                    m.then_inc(S["ps1" if k == 1 else "ps5"], 1)

                def first(g, u):
                    pe.wait_ge(S["fx"], g + 1)
                    pe.matmul(ps[4 * u + 1][:, :], fc[:, 0, :], fx[:, u], start=True, stop=True).then_inc(S["ps2"], 1)

                def second(g, u):
                    pe.wait_ge(S["r2"], g + 1)
                    pe.matmul(ps[4 * u][:, :], fc[:, 1, :], r2[:, u], start=True, stop=True).then_inc(S["ps3"], 1)

                def back(g, u):
                    pe.wait_ge(S["hx"], g + 1)
                    for p in range(NP):
                        m = pe.transpose(ps[4 * u + 1][:, p * 128:(p + 1) * 128], hx[:, u, p * T:(p + 1) * T], ident)
                    m.then_inc(S["ps4"], 1)

                def final(g, u):
                    pe.wait_ge(S["fo"], g + 1)
                    at_least(pe, S["o1"], 2 * (g - 1))
                    for p in range(NP):
                        m = pe.matmul(ps[4 * u + 2 + p // 2][:, (p % 2) * 136:(p % 2) * 136 + 136], fo[:, u, p * T:(p + 1) * T], fin[:],
                                      start=True, stop=True)
                    m.then_inc(S["ps6"], 1)

                stages(pe, [lambda g, u: turn(g, u, 1), first, second, back, lambda g, u: turn(g, u, 2), final])


INPUTS = ("x consts table b_oah W_in_t Wq Wk Wv Wo_t hl_d hl_t wq_o wk_o wv_d gate_b gate_w fc1_t fc2_t vectors fgate_t").split()


def build_program(nc, ins, out):
    ctx = ExitStack()
    with ctx:
        def sb(name, shape):
            return ctx.enter_context(nc.sbuf_tensor(name, shape, F32))
        M = {"H": sb("h_all", [T, B, H]),
             "mix": sb("mix", [T, B, H]),
             "res": sb("res", [T, H]),
             "cst": sb("cst", [128, N_CONST])}
        ps = [ctx.enter_context(nc.psum_tensor(f"bank{i}", [128, 512], F32)) for i in range(8)]
        token_graph(nc, ins, M, ps)
        relu_attention(nc, ins, M, ps)
        head_attention(nc, ins, M, ps)
        feed_forward(nc, ins, M, ps, out)


def kernel(**inputs):
    import concourse.bacc as _bacc
    from concourse.bass_utils import run_bass_kernel_spmd as _run

    a = {k.replace("L0_tok_", "").replace("L0_attn_", "").replace("L0_ffn_", "ffn_"): np.asarray(v) for k, v in inputs.items()}
    backwards = a["emb_table"][::-1]
    hl = np.concatenate([a["ffn_hl_w"], a["ffn_hl_b"][:, :, None]], 2)
    arrays = {
        "x": a["x"],
        "consts": shape_constants(),
        "table": np.concatenate([backwards, backwards])[:2 * T],
        "b_oah": a["b_oah"].reshape(1, H),
        "W_in_t": a["W_in"].T,
        "Wq": a["Wq"], "Wk": a["Wk"], "Wv": a["Wv"], "Wo_t": a["Wo"].T,
        "hl_d": hl.transpose(1, 0, 2),
        "hl_t": hl.transpose(2, 0, 1).reshape(H + 1, H),
        "wq_o": a["ffn_wq"].transpose(2, 0, 1, 3).reshape(D, NH * NE, D),
        "wk_o": a["ffn_wk"].transpose(1, 0, 2),
        "wv_d": a["ffn_wv"].transpose(2, 0, 1),
        "gate_b": a["ffn_gate_b"].reshape(1, NH * NE),
        "gate_w": a["ffn_gate_w"].reshape(NH, NE, NE, D).transpose(0, 3, 2, 1),
        "fc1_t": a["ffn_fc1_w"].T, "fc2_t": a["ffn_fc2_w"].T,
        "vectors": np.stack([a["ffn_" + n] for n in ("ln_g", "ln_b", "fc1_b", "fc2_b", "fnorm_g", "fnorm_b")], 1),
        "fgate_t": a["ffn_fgate_w"].T,
    }
    nc = _bacc.Bacc("TRN2", target_bir_lowering=False, num_devices=1)
    ins, data = {}, {}
    for name in INPUTS:
        v = np.ascontiguousarray(arrays[name])
        data["in_" + name] = v
        ins[name] = nc.dram_tensor("in_" + name, v.shape, mybir.dt.from_np(v.dtype), kind="ExternalInput").ap()
    out = nc.dram_tensor("out_h", (B, T, H), F32, kind="ExternalOutput").ap()
    build_program(nc, ins, out)
    return _run(nc, [data], core_ids=[0]).results[0]["out_h"]
```

```python
import numpy as np
import concourse.bass as bass
from concourse import mybir
from contextlib import ExitStack

F32 = mybir.dt.float32
F32R = mybir.dt.float32r
BF16 = mybir.dt.bfloat16
I32 = mybir.dt.int32
ALU = mybir.AluOpType
ACT = mybir.ActivationFunctionType
X = mybir.AxisListType.X

B, T, H = 128, 128, 64
NH, NE, D = 4, 4, 16
GB = 4
NG = B // GB
BLK = 32
NBLK = T // BLK

C_ID, C_KEEP_JI, C_KEEP_ML, C_ONE, C_RC = 0, 128, 256, 384, 385
C_NHALF = 386
C_ONEHOT, C_TRI, C_SEL, C_OWN = 388, 516, 644, 1156
C_BLOCK = 1156 + 512
N_CONST = C_BLOCK + 512
NEVER = -1.0e30
Q_ROWS = 96
M_ROWS = 100
C_ROWS = 103


def shape_constants():
    c = np.zeros((128, N_CONST), np.float32)
    r = np.arange(128)
    c[:, C_ID:C_ID + 128] = np.eye(128)
    c[:, C_KEEP_JI:C_KEEP_JI + 128] = r[:, None] >= r[None, :]
    c[:, C_KEEP_ML:C_KEEP_ML + 128] = r[:, None] <= r[None, :]
    c[:, C_ONE] = 1.0
    c[:, C_RC] = 1.0 / np.maximum(r, 1)
    c[:, C_NHALF] = -0.5
    for a in range(NBLK):
        rows = slice(a * BLK, (a + 1) * BLK)
        for e in range(NE):
            c[rows, C_ONEHOT + e * BLK:C_ONEHOT + (e + 1) * BLK] = np.eye(BLK)
        for n in range(NH):
            c[rows, C_TRI + n * BLK:C_TRI + (n + 1) * BLK] = np.where(r[None, :BLK] > r[:BLK, None], NEVER, 0)
    sel = c[:, C_SEL:C_SEL + 512].reshape(128, NE, 128)
    for n in range(NH):
        for d in range(D):
            sel[32 * n + d, :, 16 * n + d] = 1
        sel[32 * n + D, :, 64 + n] = 1
    own = c[:, C_OWN:C_OWN + 512].reshape(128, NH, 128)
    for n in range(NH):
        own[96 + 2 * (n % 2):98 + 2 * (n % 2), n, :] = 1
    for k in range(NBLK - 1):
        own[M_ROWS + k, :, (k + 1) * BLK:] = 1
        c[M_ROWS + k, C_BLOCK + k * 128:C_BLOCK + (k + 1) * 128] = NEVER
    return c


def at_least(eng, semaphore, value):
    if isinstance(value, int) and value <= 0:
        return
    eng.wait_ge(semaphore, value)


def pipeline(eng, step):
    step(0, 0, 2)
    step(1, 1, 2)
    with eng.Fori(1, NG // 2 - 1) as it:
        step(2 * it, 0, 2)
        step(2 * it + 1, 1, 2)
    step(NG - 2, 0, 1)
    step(NG - 1, 1, 0)


def rounds(eng, pairs, stages):
    last = max(late for late, _ in stages)

    def step(it, odd):
        for late, f in stages:
            pair = it - late
            if isinstance(pair, int) and not 0 <= pair < pairs:
                continue
            for u in range(2):
                f(pair, 2 * pair + u, u, 2 * ((odd - late) % 2) + u)

    first = last + 1 + (last + 1) % 2
    for it in range(first):
        step(it, it % 2)
    with eng.Fori(first // 2, pairs // 2) as k:
        step(2 * k, 0)
        step(2 * k + 1, 1)
    for it in range(pairs, pairs + last):
        step(it, it % 2)


def signals(nc, ctx, prefix, names):
    return {n: ctx.enter_context(nc.semaphore(f"{prefix}_{n}")) for n in names.split()}


def token_graph(nc, ins, M, ps):
    H_all = M["H"]
    cst = M["cst"]
    ctx = ExitStack()
    with ctx:
        def sb(name, shape, dt=F32):
            return ctx.enter_context(nc.sbuf_tensor(name, shape, dt))
        ids = sb("a_ids", [B, T], I32)
        idf = sb("a_idf", [B, T])
        seen = sb("a_seen", [B, T])
        cnt = sb("a_cnt", [B, 4])
        row = sb("a_row", [1, B])
        row_i = sb("a_row_i", [1, B], I32)
        id_t = sb("a_id_t", [T, B])
        off_t = sb("a_off_t", [T, B])
        key_t = sb("a_key_t", [T, B])
        seen_t = sb("a_seen_t", [T, B])
        emb0 = sb("a_emb0", [1, H])
        sq0 = sb("a_sq0", [1, 2 * H])
        base = sb("a_base", [128, B // 2])
        w_in = sb("a_w_in", [128, 128])
        b_oah = sb("a_b_oah", [128, H])
        pe_rows = sb("a_pe_rows", [T, 4, GB, H + 1])
        id_rows = sb("a_id_rows", [128, 4, GB, T], I32)
        rel = sb("a_rel", [T, 4, GB, T])
        sq = sb("a_sq", [T, 4, GB, H])
        rn = sb("a_rn", [T, 2, GB, 2])
        agg = sb("a_agg", [T, 2, GB, H])
        inv = sb("a_inv", [128, 4, 4])
        xt = sb("a_xt", [128, 2, 2, T])
        S = signals(nc, ctx, "a", "ids consts weights zeroed ones idf seen count row row_i id_t off_t key_t seen_t "
                    "sq0 base ps_count ps_id ps_base pe_in0 pe_in1 pe_in2 pe_in3 row_in0 row_in1 row_in2 row_in3 rel sq ps_agg ps_nrm rn rn1 agg inv0 inv1 inv "
                    "ps_xt xt ps_h h stats")
        table = ins["table"]

        def nth(pair, s):
            return (pair - s // 2) // 2 + 1

        def fetch(eng, it, g, u, s, mine):
            if u != mine:
                return
            at_least(eng, S["ps_agg"], g - 3)
            at_least(eng, S["sq"], g - 3)
            eng.dma_start(id_rows[:, s, :, :], ins["x"][bass.ds(g * GB, GB), :].rearrange("(o b) t -> o b t", o=1)
                          .to_broadcast([128, GB, T])).then_inc(S[f"row_in{s}"], 16)
            for q in range(GB):
                first = eng.value_load(row_i[0:1, bass.ds(g * GB + q, 1)], min_val=0, max_val=T)
                eng.dma_start(pe_rows[:, s, q, 0:H], table[bass.ds(first, T), :]).then_inc(S[f"pe_in{s}"], 16)

        with nc.Block() as block:
            @block.sync
            def _(sp):
                sp.dma_start(ids[:], ins["x"]).then_inc(S["ids"], 16)
                sp.dma_start(cst[:], ins["consts"]).then_inc(S["consts"], 16)
                sp.dma_start(emb0[:], ins["table"][128:129, :]).then_inc(S["weights"], 16)
                sp.dma_start(b_oah[:], ins["b_oah"].to_broadcast([128, H])).then_inc(S["weights"], 16)
                sp.wait_ge(S["zeroed"], 1)
                sp.dma_start(w_in[0:H, 0:H], ins["W_in_t"]).then_inc(S["weights"], 16)
                sp.dma_start(w_in[H:128, H:128], ins["W_in_t"]).then_inc(S["weights"], 16)
                sp.wait_ge(S["row_i"], 1)
                sp.wait_ge(S["ones"], 4)

                rounds(sp, NG // 2, [(0, lambda it, g, u, s: fetch(sp, it, g, u, s, 0))])

            @block.gpsimd
            def _(pool):
                pool.memset(w_in[:], 0.0).then_inc(S["zeroed"], 1)
                pool.wait_ge(S["consts"], 16)
                for u in range(4):
                    pool.memset(pe_rows[:, u, :, H:H + 1], 1.0).then_inc(S["ones"], 1)

                def roots(it, g, u, s):
                    pool.wait_ge(S["inv0"], g + 1)
                    pool.tensor_tensor(inv[:, s, 2:4], inv[:, s, 0:2], cst[:, C_NHALF:C_NHALF + 1].to_broadcast([128, 2]), ALU.pow).then_inc(S["inv"], 1)

                rounds(pool, NG // 2, [(1, roots)])

            @block.vector
            def _(dve):
                dve.wait_ge(S["ids"], 16)
                dve.tensor_copy(idf[:], ids[:]).then_inc(S["idf"], 1)
                dve.wait_ge(S["idf"], 1)
                dve.tensor_scalar(seen[:], idf[:], 0.0, None, ALU.not_equal).then_inc(S["seen"], 1)
                dve.wait_ge(S["seen"], 1)
                dve.tensor_reduce(cnt[:, 0:1], seen[:], X, ALU.add).then_inc(S["count"], 1)
                dve.wait_ge(S["count"], 1)
                dve.tensor_scalar(cnt[:, 1:2], cnt[:, 0:1], -1.0, float(T), ALU.mult, ALU.add).then_inc(S["count"], 1)
                dve.wait_ge(S["ps_count"], 1)
                dve.tensor_copy(row[:], ps[0][0:1, 0:B]).then_inc(S["row"], 1)
                dve.tensor_copy(row_i[:], ps[0][0:1, 0:B]).then_inc(S["row_i"], 1)
                dve.wait_ge(S["ps_id"], 1)
                dve.tensor_copy(id_t[:], ps[1][:, 0:B]).then_inc(S["id_t"], 1)
                dve.wait_ge(S["id_t"], 1)
                dve.tensor_scalar(off_t[:], id_t[:], 0.0, -0.5, ALU.is_equal, ALU.mult).then_inc(S["off_t"], 1)
                dve.tensor_scalar(seen_t[:], id_t[:], 0.0, None, ALU.not_equal).then_inc(S["seen_t"], 1)
                dve.wait_ge(S["off_t"], 1)
                dve.tensor_tensor(key_t[:], id_t[:], off_t[:], ALU.add).then_inc(S["key_t"], 1)
                dve.wait_ge(S["weights"], 64)
                for k in range(2):
                    dve.tensor_tensor(sq0[0:1, k * H:(k + 1) * H], emb0[:], emb0[:], ALU.mult).then_inc(S["sq0"], 1)
                dve.wait_ge(S["ps_base"], 1)
                dve.tensor_copy(base[:], ps[2][:, 0:B // 2]).then_inc(S["base"], 1)
                dve.wait_ge(S["base"], 1)
                dve.wait_ge(S["key_t"], 1)
                dve.wait_ge(S["seen_t"], 1)
                dve.wait_ge(S["consts"], 16)

                def graph(it, g, u, s):
                    dve.wait_ge(S[f"row_in{s}"], 16 * nth(it, s))
                    at_least(dve, S["ps_agg"], g - 3)
                    for q in range(GB):
                        ins_ = dve.scalar_tensor_tensor(
                            rel[:, s, q, :], id_rows[:, s, q, :], key_t[:, bass.ds(g * GB + q, 1)],
                            cst[:, C_KEEP_JI:C_KEEP_JI + T], ALU.is_equal, ALU.mult)
                    ins_.then_inc(S["rel"], 1)
                    dve.wait_ge(S[f"pe_in{s}"], 16 * GB * nth(it, s))
                    at_least(dve, S["ps_nrm"], g - 3)
                    for q in range(GB):
                        ins_ = dve.scalar_tensor_tensor(
                            sq[:, s, q, :], pe_rows[:, s, q, 0:H], seen_t[:, bass.ds(g * GB + q, 1)],
                            pe_rows[:, s, q, 0:H], ALU.mult, ALU.mult)
                    ins_.then_inc(S["sq"], 1)

                def mean(it, g, u, s):
                    a = ps[u][:, 0:GB * 66].rearrange("p (b c) -> p b c", b=GB)
                    dve.wait_ge(S["ps_agg"], g + 1)
                    dve.tensor_scalar(rn[:, u, :, 0:1], a[:, :, H:H + 1], 1.0, None, ALU.max).then_inc(S["rn"], 1)
                    dve.wait_ge(S["rn"], g + 1)
                    dve.reciprocal(rn[:, u, :, 1:2], rn[:, u, :, 0:1]).then_inc(S["rn1"], 1)
                    dve.wait_ge(S["rn1"], g + 1)
                    at_least(dve, S["ps_xt"], g - 1)
                    dve.tensor_tensor(agg[:, u, :, :], a[:, :, 0:H],
                                      rn[:, u, :, 1:2].to_broadcast([T, GB, H]), ALU.mult).then_inc(S["agg"], 1)
                    dve.wait_ge(S["ps_nrm"], g + 1)
                    at_least(dve, S["xt"], g - 3)
                    for p in range(2):
                        ins_ = dve.tensor_scalar(inv[:, s, p:p + 1], ps[2 + u][:, p:p + 1], base[:, bass.ds(2 * g + p, 1)], 1e-24,
                                                 ALU.add, ALU.max)
                    ins_.then_inc(S["inv0"], 1)

                def store(it, g, u, s):
                    dve.wait_ge(S["ps_h"], g + 1)
                    dve.tensor_tensor(H_all[:, bass.ds(g * GB, GB), :],
                                      ps[6 + u][:, 0:GB * H].rearrange("p (b c) -> p b c", b=GB),
                                      b_oah[:].rearrange("p (o c) -> p o c", o=1).to_broadcast([128, GB, H]), ALU.add).then_inc(S["h"], 1)

                def statistics(it, g, u, s):
                    dve.wait_ge(S["h"], g + 1)
                    gather_stats(dve, M["stats"], H_all, g).then_inc(S["stats"], 1)

                rounds(dve, NG // 2, [(0, graph), (1, mean), (2, store), (3, statistics)])
                dve.wait_ge(S["stats"], NG)

            @block.scalar
            def _(act):
                act.wait_ge(S["row_i"], 1)
                act.wait_ge(S["ones"], 4)

                def turned(it, g, u, s):
                    act.wait_ge(S["ps_xt"], g + 1)
                    act.wait_ge(S["inv"], g + 1)
                    at_least(act, S["ps_h"], g - 1)
                    for p in range(2):
                        ins_ = act.activation(xt[:, u, p, :], ps[4 + u][:, p * T:(p + 1) * T], ACT.Copy,
                                              scale=inv[:, s, 2 + p:3 + p])
                    ins_.then_inc(S["xt"], 1)

                rounds(act, NG // 2, [(0, lambda it, g, u, s: fetch(act, it, g, u, s, 1)), (2, turned)])

            @block.tensor
            def _(pe):
                ident = cst[:, C_ID:C_ID + 128]
                pe.wait_ge(S["consts"], 16)
                pe.wait_ge(S["count"], 2)
                pe.transpose(ps[0][0:1, 0:B], cnt[:, 1:2], ident).then_inc(S["ps_count"], 1)
                pe.wait_ge(S["idf"], 1)
                pe.transpose(ps[1][:, 0:B], idf[:], ident).then_inc(S["ps_id"], 1)
                pe.wait_ge(S["sq0"], 2)
                pe.wait_ge(S["row"], 1)
                pairs = row[0:1, :].rearrange("o (p k) -> o k p", k=2)
                for k in range(2):
                    m = pe.matmul(ps[2][k * H:(k + 1) * H, 0:B // 2], sq0[0:1, k * H:(k + 1) * H], pairs[:, k, :],
                                  start=True, stop=True)
                m.then_inc(S["ps_base"], 1)
                pe.wait_ge(S["weights"], 64)
                pe.wait_ge(S["base"], 1)
                pe.wait_ge(S["id_t"], 1)
                pe.wait_ge(S["row_i"], 1)

                def gather(it, g, u, s):
                    pe.wait_ge(S["rel"], g + 1)
                    pe.wait_ge(S[f"pe_in{s}"], 16 * GB * nth(it, s))
                    at_least(pe, S["agg"], g - 1)
                    for q in range(GB):
                        m = pe.matmul(ps[u][:, q * 66:q * 66 + H + 1], rel[:, s, q, :], pe_rows[:, s, q, :],
                                      start=True, stop=True)
                    m.then_inc(S["ps_agg"], 1)
                    pe.wait_ge(S["sq"], g + 1)
                    at_least(pe, S["inv0"], g - 1)
                    for p in range(2):
                        m = pe.matmul(ps[2 + u][:, p:p + 1], sq[:, s, 2 * p:2 * p + 2, :].rearrange("p b c -> p (b c)"),
                                      cst[:, C_ONE:C_ONE + 1], start=True, stop=True)
                    m.then_inc(S["ps_nrm"], 1)

                def turn(it, g, u, s):
                    pe.wait_ge(S["agg"], g + 1)
                    at_least(pe, S["xt"], g - 1)
                    for p in range(2):
                        m = pe.transpose(ps[4 + u][:, p * T:(p + 1) * T],
                                         agg[:, u, 2 * p:2 * p + 2, :].rearrange("p b c -> p (b c)"), ident)
                    m.then_inc(S["ps_xt"], 1)

                def project(it, g, u, s):
                    pe.wait_ge(S["xt"], g + 1)
                    at_least(pe, S["h"], g - 1)
                    for p in range(2):
                        m = pe.matmul(ps[6 + u][:, p * 128:(p + 1) * 128], xt[:, u, p, :], w_in[:], start=True, stop=True)
                    m.then_inc(S["ps_h"], 1)

                rounds(pe, NG // 2, [(2, turn), (1, gather), (2, project)])


class LayerNorm:

    def __init__(self, nc, ctx, prefix, stats):
        def sb(name, n=B):
            return ctx.enter_context(nc.sbuf_tensor(f"{prefix}_ln_{name}", [T, n], F32))
        self.stats = stats
        self.mean, self.var, self.root, self.rstd = sb("mean"), sb("var"), sb("root"), sb("rstd")
        self.tmp = [sb(f"tmp{k}") for k in range(4)]
        self.S = signals(nc, ctx, f"{prefix}_ln", "step root")

    def on_vector(self, dve):
        def part(k):
            return self.stats[:, :, k:k + 1].rearrange("p b o -> p (b o)")

        def done(i, n):
            i.then_inc(self.S["step"], 1)
            dve.wait_ge(self.S["step"], n)
        total, apart, squares, apart2 = self.tmp
        dve.tensor_tensor(total[:], part(1), part(4), ALU.add)
        dve.tensor_tensor(apart[:], part(1), part(4), ALU.subtract)
        done(dve.tensor_tensor(squares[:], part(2), part(5), ALU.add), 1)
        dve.tensor_tensor(apart2[:], apart[:], apart[:], ALU.mult)
        done(dve.tensor_scalar(self.mean[:], total[:], 0.5, None, ALU.mult), 2)
        done(dve.scalar_tensor_tensor(squares[:], apart2[:], float(H // 4), squares[:], ALU.mult, ALU.add), 3)
        dve.tensor_scalar(self.var[:], squares[:], 1.0 / H, 1e-5, ALU.mult, ALU.add).then_inc(self.S["step"], 1)
        dve.wait_ge(self.S["root"], 1)
        done(dve.reciprocal(total[:], self.root[:]), 5)
        done(dve.tensor_tensor(apart[:], total[:], total[:], ALU.mult), 6)
        done(dve.scalar_tensor_tensor(apart2[:], self.var[:], -0.5, apart[:], ALU.mult, ALU.mult), 7)
        done(dve.scalar_tensor_tensor(self.rstd[:], apart2[:], 1.5, total[:], ALU.add, ALU.mult), 8)

    def on_scalar(self, act):
        act.wait_ge(self.S["step"], 4)
        act.activation(self.root[:], self.var[:], ACT.Sqrt).then_inc(self.S["root"], 1)

    def apply(self, dve, out, x, g):
        for q in range(GB):
            b = bass.ds(g * GB + q, 1)
            i = dve.tensor_scalar(out[:, q, :], x[:, b, :], self.mean[:, b], self.rstd[:, b], ALU.subtract, ALU.mult)
        return i


def gather_stats(dve, stats, x, g):
    for q in range(GB):
        b = bass.ds(g * GB + q, 1)
        i = dve.bn_stats(stats[:, b, :], x[:, b, :])
    return i


def relu_attention(nc, ins, M, ps):
    H_all, cst = M["H"], M["cst"]
    ctx = ExitStack()
    with ctx:
        def sb(name, shape, dt=F32):
            return ctx.enter_context(nc.sbuf_tensor(name, shape, dt))
        w4 = sb("b_w4", [H, 4, H])
        w_qk = sb("b_w_qk", [128, 128])
        w_vo = sb("b_w_vo", [128, 128])
        ln = LayerNorm(nc, ctx, "b", M["stats"])
        xn = sb("b_xn", [T, 2, GB, H])
        xt = sb("b_xt", [128, 4, 2, T])
        ubd = sb("b_ubd", [128, 4, 2, 2 * T])
        val = sb("b_val", [T, 4, 2, 2 * H])
        att = sb("b_att", [T, 2, GB, T])
        S = signals(nc, ctx, "b", "w4 zeroed ps_w w xn stats ps_xt xt u ps_v v ps_l att ps_c h")
        ident = cst[:, C_ID:C_ID + 128]
        with nc.Block() as block:
            @block.sync
            def _(sp):
                for k, n in enumerate(("Wq", "Wk", "Wv", "Wo_t")):
                    sp.dma_start(w4[:, k, :], ins[n]).then_inc(S["w4"], 16)

            @block.gpsimd
            def _(pool):
                for t in (w_qk, w_vo, ubd):
                    i = pool.memset(t[:], 0.0).then_inc(S["zeroed"], 1)

            @block.vector
            def _(dve):
                dve.wait_ge(S["ps_w"], 1)
                dve.wait_ge(S["zeroed"], 3)
                for k in range(2):
                    r = slice(k * H, (k + 1) * H)
                    dve.tensor_copy(w_qk[r, r], ps[0][r, 0:H]).then_inc(S["w"], 1)
                    dve.tensor_copy(w_vo[r, r], ps[0][r, H:2 * H]).then_inc(S["w"], 1)

                ln.on_vector(dve)

                def norm(it, g, u, s):
                    at_least(dve, S["ps_xt"], g - 1)
                    ln.apply(dve, xn[:, u], H_all, g).then_inc(S["xn"], 1)

                def attend(it, g, u, s):
                    dve.wait_ge(S["ps_l"], g + 1)
                    at_least(dve, S["ps_c"], g - 1)
                    dve.scalar_tensor_tensor(att[:, u, :, :], ps[4 + u][:, :].rearrange("p (b l) -> p b l", b=GB), 0.0,
                                             cst[:, C_KEEP_ML:C_KEEP_ML + T].rearrange("p (o l) -> p o l", o=1)
                                             .to_broadcast([T, GB, T]), ALU.max, ALU.mult).then_inc(S["att"], 1)

                def store(it, g, u, s):
                    dve.wait_ge(S["ps_c"], g + 1)
                    c = ps[6 + u][:, :].rearrange("p (b c) -> p b c", b=GB)
                    for q in range(GB):
                        o = (q % 2) * H
                        i = dve.scalar_tensor_tensor(H_all[:, bass.ds(g * GB + q, 1), :], c[:, q:q + 1, o:o + H],
                                                     cst[:, C_RC:C_RC + 1], H_all[:, bass.ds(g * GB + q, 1), :],
                                                     ALU.mult, ALU.add)
                    i.then_inc(S["h"], 1)

                def statistics(it, g, u, s):
                    dve.wait_ge(S["h"], g + 1)
                    gather_stats(dve, M["stats"], H_all, g).then_inc(S["stats"], 1)

                rounds(dve, NG // 2, [(3, attend), (0, norm), (4, statistics), (3, store)])
                dve.wait_ge(S["stats"], NG)

            @block.scalar
            def _(act):
                ln.on_scalar(act)
                act.wait_ge(S["zeroed"], 3)

                def turned(it, g, u, s):
                    act.wait_ge(S["ps_xt"], g + 1)
                    at_least(act, S["ps_l"], g - 3)
                    act.activation(xt[:, s, :, :].rearrange("p a b -> p (a b)"), ps[u][:, 0:2 * T], ACT.Copy).then_inc(S["xt"], 1)

                def queries(it, g, u, s):
                    act.wait_ge(S["ps_v"], g + 1)
                    at_least(act, S["ps_l"], g - 3)
                    for k in range(2):
                        r = slice(k * H, (k + 1) * H)
                        i = act.activation(ubd[r, s, :, k * T:(k + 1) * T],
                                           ps[2 + u][r, 0:2 * T].rearrange("p (a b) -> p a b", a=2), ACT.Copy)
                    i.then_inc(S["u"], 1)

                def values(it, g, u, s):
                    act.wait_ge(S["ps_v"], g + 1)
                    at_least(act, S["ps_c"], g - 3)
                    act.activation(val[:, s, :, :].rearrange("p a b -> p (a b)"), ps[2 + u][:, 256:512], ACT.Copy).then_inc(S["v"], 1)

                rounds(act, NG // 2, [(2, turned), (2, queries), (2, values)])

            @block.tensor
            def _(pe):
                pe.wait_ge(S["w4"], 64)
                for k in range(2):
                    r = slice(k * H, (k + 1) * H)
                    pe.matmul(ps[0][r, 0:H], w4[:, 0, :], w4[:, 1, :], start=True, stop=True)
                    m = pe.matmul(ps[0][r, H:2 * H], w4[:, 2, :], w4[:, 3, :], start=True, stop=True)
                m.then_inc(S["ps_w"], 1)
                pe.wait_ge(S["w"], 4)

                def turn(it, g, u, s):
                    pe.wait_ge(S["xn"], g + 1)
                    at_least(pe, S["xt"], g - 1)
                    for p in range(2):
                        m = pe.transpose(ps[u][:, p * T:(p + 1) * T], xn[:, u, 2 * p:2 * p + 2, :].rearrange("p b c -> p (b c)"), ident)
                    m.then_inc(S["ps_xt"], 1)

                def project(it, g, u, s):
                    pe.wait_ge(S["xt"], g + 1)
                    at_least(pe, S["v"], g - 1)
                    pe.matmul(ps[2 + u][:, 0:2 * T], w_qk[:], xt[:, s, :, :].rearrange("p a b -> p (a b)"), start=True, stop=True)
                    for p in range(2):
                        m = pe.matmul(ps[2 + u][:, 256 + p * 128:256 + (p + 1) * 128], xt[:, s, p, :], w_vo[:], start=True, stop=True)
                    m.then_inc(S["ps_v"], 1)

                def logits(it, g, u, s):
                    pe.wait_ge(S["u"], g + 1)
                    at_least(pe, S["att"], g - 1)
                    for p in range(2):
                        m = pe.matmul(ps[4 + u][:, p * 2 * T:(p + 1) * 2 * T], xt[:, s, p, :], ubd[:, s, p, :], start=True, stop=True)
                    m.then_inc(S["ps_l"], 1)

                def context(it, g, u, s):
                    pe.wait_ge(S["att"], g + 1)
                    pe.wait_ge(S["v"], g + 1)
                    at_least(pe, S["h"], g - 1)
                    for q in range(GB):
                        m = pe.matmul(ps[6 + u][:, q * 128:(q + 1) * 128], att[:, u, q, :], val[:, s, q // 2, :], start=True, stop=True)
                    m.then_inc(S["ps_c"], 1)

                rounds(pe, NG // 2, [(3, logits), (1, turn), (2, project), (3, context)])


def head_attention(nc, ins, M, ps):
    H_all, cst, mix, res = M["H"], M["cst"], M["mix"], M["res"]
    ctx = ExitStack()
    with ctx:
        def sb(name, shape, dt=F32):
            return ctx.enter_context(nc.sbuf_tensor(name, shape, dt))
        hl_d = sb("c_hl_d", [D, NH, H + 1])
        hl_t = sb("c_hl_t", [H + 1, H])
        wq_o = sb("c_wq_o", [D, NH * NE, D])
        wk_o = sb("c_wk_o", [D, NH, D])
        wv_d = sb("c_wv_d", [D, NH, D])
        qk_d = sb("c_qk_d", [D, NH, NE * D])
        w = sb("c_w", [128, 10, 128])
        wr = sb("c_wr", [128, 10, 128], F32R)
        wl = sb("c_wl", [128, 10, 128], F32R)
        w_v = sb("c_w_v", [128, 128])
        bias = sb("c_bias", [128, 13])
        one_v = sb("c_one_v", [128, 128], F32R)
        bias_v = sb("c_bias_v", [128, 2, 128], F32R)

        def query_weights(t, m, e):
            return t[:].rearrange("h a c -> h (a c)")[:, (m * NE + e) * 96:(m * NE + e + 1) * 96]

        def key_weights(t, n):
            return t[:].rearrange("h a c -> h (a c)")[:, (8 + n) * 96:(9 + n) * 96]

        def live_weights(t):
            return t[:].rearrange("h a c -> h (a c)")[:, 12 * 96:12 * 96 + 128]
        gate_b = sb("c_gate_b", [128, NH * NE])
        onehot = sb("c_onehot", [128, 128], BF16)
        tri = sb("c_tri", [128, NH, BLK], BF16)
        sel = cst[:, C_SEL:C_SEL + 512].rearrange("p (e c) -> p e c", e=NE)

        ln = LayerNorm(nc, ctx, "c", M["stats"])
        xn = sb("c_xn", [T, 2, GB, H])
        xt = sb("c_xt", [128, 2, GB * T], F32R)
        Q = sb("c_q", [C_ROWS, 2, 2, GB, NE * T], F32R)
        K = sb("c_k", [C_ROWS, 2, NH, GB, T], F32R)
        V = sb("c_v", [T, 2, GB, NH, 32])
        live = sb("c_live", [128, 2, GB, T])
        nmax = sb("c_nmax", [128, 2, 2, 2, GB, NBLK])
        nmax2 = sb("c_nmax2", [128, 2, 2, 2, 2 * GB * NBLK], F32R)
        nmax_t = sb("c_nmax_t", [128, 2, 128])
        P = sb("c_p", [T, 2, NH, NE * T])
        om = sb("c_om", [128, 2, NE, T])
        rs = sb("c_rs", [T, 2, GB, NE, NH])
        oz = sb("c_oz", [T, 2, GB, NE, NH, D])
        ty = sb("c_ty", [T, 2, GB, NE, NH * NE])
        lg = sb("c_lg", [T, 2, GB, NH * NE])
        lm = sb("c_lm", [T, 2, GB, NH])
        ls = sb("c_ls", [T, 2, GB, NH])
        li = sb("c_li", [T, 2, GB, NH])
        eg = sb("c_eg", [T, 2, GB, NH * NE])
        gs = sb("c_gs", [T, 2, GB, NH * NE])

        S = signals(nc, ctx, "c", "w zeroed ps_w1 ps_w2 qk_d built ps_bias bias twice halves xn ps_xt xt xl ps_k kr kl ps_np live ps_v v "
                    "ps_q qr ql ps_mx mx nmax2r nmax2 ps_ct ct cmax0 cmax1 ps_s ex ps_o om ps_z rs oz "
                    "lg0 lg1 lm lg2 eg ls li gs prod half mix res")
        ident = cst[:, C_ID:C_ID + 128]
        MXB, SB_, OB, ZB = ps[2:4], ps[4:6], ps[6], ps[7]

        TASKS = ["xt", "ct", "k0", "k1", "k2", "k3", "np", "v"] + [f"q{k}" for k in range(8)]

        def bank(task):
            return ps[TASKS.index(task) % 4]

        def release(pe, task, g):
            t = TASKS.index(task) - 4
            if t in (-2, -1):
                at_least(pe, S["mx"], 3 * GB * g)
            elif t in (-4, -3):
                at_least(pe, S["ql"], 8 * (g - 1) + 5 + t + 4 if not (isinstance(g, int) and g == 0) else 0)
            elif TASKS[t] == "ct":
                at_least(pe, S["ct"], g)
            elif TASKS[t][0] == "k":
                pe.wait_ge(S["kl"], NH * g + int(TASKS[t][1]) + 1)
            elif TASKS[t][0] == "q":
                pe.wait_ge(S["ql"], 8 * g + int(TASKS[t][1]) + 1)
            else:
                pe.wait_ge(S[{"xt": "xl", "np": "live", "v": "v"}[TASKS[t]]], g + 1)

        with nc.Block() as block:
            @block.sync
            def _(sp):
                sp.dma_start(hl_d[:], ins["hl_d"]).then_inc(S["w"], 16)
                sp.dma_start(hl_t[:], ins["hl_t"]).then_inc(S["w"], 16)
                sp.dma_start(wq_o[:], ins["wq_o"]).then_inc(S["w"], 16)
                sp.dma_start(wk_o[:], ins["wk_o"]).then_inc(S["w"], 16)
                sp.dma_start(wv_d[:], ins["wv_d"]).then_inc(S["w"], 16)
                sp.dma_start(gate_b[:], ins["gate_b"].to_broadcast([128, NH * NE])).then_inc(S["w"], 16)
                for n in range(NH):
                    sp.dma_start(sel[32 * n:32 * n + D, :, 80 + 4 * n:84 + 4 * n], ins["gate_w"][n]).then_inc(S["w"], 16)

                sp.wait_ge(S["bias"], 4)
                sp.dma_start(w[H:128, :, :], w[0:H, :, :]).then_inc(S["twice"], 16)
                sp.dma_start(w_v[H:128, :], w_v[0:H, :]).then_inc(S["twice"], 16)

                def maxima(g, u):
                    sp.wait_ge(S["ct"], g + 1)
                    sp.dma_start(Q[Q_ROWS:M_ROWS, u].rearrange("p m b c -> p (m b c)").bitcast(F32), nmax_t[:, u, :]).then_inc(S[f"cmax{u}"], 16)
                maxima(0, 0)
                maxima(1, 1)
                with sp.Fori(1, NG // 2) as it:
                    maxima(2 * it, 0)
                    maxima(2 * it + 1, 1)

            @block.gpsimd
            def _(pool):
                for t in (w, V, w_v):
                    pool.memset(t[:], 0.0).then_inc(S["zeroed"], 1)
                pool.memset(one_v[:].bitcast(F32), 1.0).then_inc(S["zeroed"], 1)
                pool.wait_ge(S["zeroed"], 4)
                pool.memset(live_weights(w)[H:H + 1].rearrange("h (n c) -> h n c", n=NH)[:, :, D:32], 1.0).then_inc(S["zeroed"], 1)
                pool.wait_ge(S["zeroed"], 5)
                pool.memset(V[:, :, :, :, D:D + 1].rearrange("p u b n o -> p (u b n) o"), 1.0).then_inc(S["zeroed"], 1)

                def mixing(g, u):
                    pool.wait_ge(S["gs"], g + 1)
                    for b in range(GB):
                        w = gs[:, u, b, :].rearrange("p (n e o) -> p e n o", n=NH, o=1)
                        i = pool.tensor_tensor(oz[:, u, b], oz[:, u, b], w.to_broadcast([T, NE, NH, D]), ALU.mult)
                    i.then_inc(S["prod"], 1)
                    pool.wait_ge(S["prod"], g + 1)
                    pool.tensor_tensor(oz[:, u, :, 0:2], oz[:, u, :, 0:2], oz[:, u, :, 2:4], ALU.add).then_inc(S["half"], 1)

                def step(g, u, front):
                    if not (isinstance(g, int) and g == 0):
                        mixing(g - 1, 1 - u)
                pipeline(pool, step)
                mixing(NG - 1, 1)

            @block.vector
            def _(dve):
                ln.on_vector(dve)
                dve.tensor_copy(onehot[:], cst[:, C_ONEHOT:C_ONEHOT + 128]).then_inc(S["built"], 1)
                dve.tensor_copy(tri[:].rearrange("p n s -> p (n s)"), cst[:, C_TRI:C_TRI + 128]).then_inc(S["built"], 1)
                for u in range(2):
                    for m in range(2):
                        dve.tensor_copy(Q[Q_ROWS:C_ROWS, u, m], cst[Q_ROWS:C_ROWS, C_BLOCK:C_BLOCK + 512]
                                        .rearrange("p (o c) -> p o c", o=1).to_broadcast([C_ROWS - Q_ROWS, GB, 512])).then_inc(S["built"], 1)
                for u in range(2):
                    for b in range(GB):
                        dve.tensor_copy(K[Q_ROWS:C_ROWS, u, :, b, :],
                                        cst[Q_ROWS:C_ROWS, C_OWN:C_OWN + 512].rearrange("p (n t) -> p n t", n=NH)).then_inc(S["built"], 1)
                dve.wait_ge(S["w"], 160)
                dve.wait_ge(S["zeroed"], 6)
                dve.tensor_copy(live_weights(w)[0:H + 1].rearrange("h (n c) -> h n c", n=NH)[:, :, 0:D], hl_t[:].rearrange("h (n d) -> h n d", n=NH)).then_inc(S["built"], 1)
                dve.tensor_copy(w_v[0:H + 1, H:2 * H], hl_t[:]).then_inc(S["built"], 1)
                for n in range(NH):
                    for r in range(3):
                        dve.tensor_copy(key_weights(w, n)[0:H + 1, (2 * r + n % 2) * D:(2 * r + n % 2 + 1) * D], hl_t[:, n * D:(n + 1) * D]).then_inc(S["built"], 1)
                dve.wait_ge(S["ps_w1"], 1)
                dve.tensor_scalar(qk_d[:].rearrange("d n c -> d (n c)"), ps[0][0:D, 0:NH * NE * D], float(D) ** 0.5, None,
                                  ALU.mult).then_inc(S["qk_d"], 1)
                dve.wait_ge(S["ps_w2"], 1)
                dve.tensor_copy(w_v[0:H + 1, 0:H], ps[2][0:H + 1, 0:H]).then_inc(S["built"], 1)
                for n in range(NH):
                    for r in range(3):
                        for e in range(NE):
                            dve.tensor_copy(query_weights(w, n // 2, e)[0:H + 1, (2 * r + n % 2) * D:(2 * r + n % 2 + 1) * D],
                                            ps[1][0:H + 1, n * 64 + e * D:n * 64 + (e + 1) * D]).then_inc(S["built"], 1)
                dve.wait_ge(S["ps_bias"], 1)
                dve.tensor_copy(bias[0:Q_ROWS, 0:12], ps[3][0:Q_ROWS, 0:12]).then_inc(S["bias"], 1)
                dve.tensor_copy(bias[:, 12:13], ps[3][:, 12:13]).then_inc(S["bias"], 1)
                dve.wait_ge(S["built"], 14 + 2 + 12 + 1 + 48)
                dve.tensor_copy(bias_v[H:H + 1, 0, :], w_v[H:H + 1, :]).then_inc(S["bias"], 1)
                dve.wait_ge(S["bias"], 3)
                dve.tensor_tensor(bias_v[H:H + 1, 1, :], w_v[H:H + 1, :], bias_v[H:H + 1, 0, :].bitcast(F32), ALU.subtract).then_inc(S["bias"], 1)
                dve.wait_ge(S["twice"], 32)
                dve.tensor_copy(wr[:], w[:]).then_inc(S["halves"], 1)
                dve.wait_ge(S["halves"], 1)
                dve.tensor_tensor(wl[:], w[:], wr[:].bitcast(F32), ALU.subtract).then_inc(S["halves"], 1)

                def norm(g, u):
                    at_least(dve, S["ps_xt"], g - 1)
                    ln.apply(dve, xn[:, u], H_all, g).then_inc(S["xn"], 1)

                def x_rest(g, u):
                    dve.wait_ge(S["xt"], g + 1)
                    x = xt[H:128, u, :]
                    dve.tensor_tensor(x, bank("xt")[H:128, :], x.bitcast(F32), ALU.subtract).then_inc(S["xl"], 1)

                def k_rest(g, u, n0):
                    for n in range(n0, n0 + 2):
                        dve.wait_ge(S["kr"], NH * g + n + 1)
                        k = K[64:96, u, n, :, :].rearrange("p b t -> p (b t)")
                        dve.scalar_tensor_tensor(k, bank(f"k{n}")[64:96, :], bias[64:96, 8 + n:9 + n], k.bitcast(F32),
                                                 ALU.add, ALU.subtract).then_inc(S["kl"], 1)

                def alive(g, u):
                    dve.wait_ge(S["ps_np"], g + 1)
                    at_least(dve, S["om"], GB * (g - 1))
                    dve.tensor_scalar(live[:, u, :, :].rearrange("p b s -> p (b s)"), bank("np")[:, :], bias[:, 12:13], 0.0,
                                      ALU.add, ALU.not_equal).then_inc(S["live"], 1)

                def q_rest(g, u, k0, k1):
                    for k in range(k0, k1):
                        dve.wait_ge(S["qr"], 8 * g + k + 1)
                        m, e = k // NE, k % NE
                        q = Q[32:64, u, m].rearrange("p b (a e s) -> p (b a) e s", a=NBLK, e=NE)[:, :, e, :]
                        dve.scalar_tensor_tensor(q, bank(f"q{k}")[32:64, :].rearrange("p (a s) -> p a s", s=BLK),
                                                 bias[32:64, k:k + 1], q.bitcast(F32), ALU.add, ALU.subtract).then_inc(S["ql"], 1)

                def maxima(g, u, b, j0, j1):
                    for j in range(j0, j1):
                        blocks = ((3,), (2, 0), (1,))[j]
                        at = 0
                        dve.wait_ge(S["ps_mx"], 3 * (GB * g + b) + j + 1)
                        if b == 0 and j == 0:
                            at_least(dve, S["nmax2"], g - 1)
                        for a in blocks:
                            w = BLK * (a + 1)
                            i = dve.tensor_reduce(nmax[:, u, :, :, b, a].rearrange("p k m -> p m k"), MXB[(3 * b + j) % 2][:, at:at + NH * w]
                                                  .rearrange("p (m k w) -> p m k w", m=2, k=2), X, ALU.max, negate=True)
                            at += NH * w
                        i.then_inc(S["mx"], 1)

                def split_max(g, u):
                    dve.wait_ge(S["mx"], 3 * GB * (g + 1))
                    at_least(dve, S["ps_ct"], g - 1)
                    v = nmax[:, u].rearrange("p k m b a -> p k (m b a)")
                    dve.tensor_copy(nmax2[:, u, :, 0, :], v).then_inc(S["nmax2r"], 1)
                    dve.wait_ge(S["nmax2r"], g + 1)
                    dve.tensor_tensor(nmax2[:, u, :, 1, :], v, nmax2[:, u, :, 0, :].bitcast(F32), ALU.subtract).then_inc(S["nmax2"], 1)

                def outputs(g, u, b):
                    dve.wait_ge(S["ps_o"], GB * g + b + 1)
                    at_least(dve, S["ps_z"], GB * g + b - 1)
                    dve.tensor_tensor(om[:, b % 2].rearrange("p e (a s) -> p e a s", a=NBLK),
                                      OB[:, :].rearrange("p (a e s) -> p e a s", a=NBLK, e=NE),
                                      live[:, u, b, :].rearrange("p (o a s) -> p o a s", o=1, a=NBLK).to_broadcast([128, NE, NBLK, BLK]),
                                      ALU.mult).then_inc(S["om"], 1)

                def scale(g, u, b):
                    z = ZB[:, :].rearrange("p (e c) -> p e c", e=NE)
                    dve.wait_ge(S["ps_z"], GB * g + b + 1)
                    if b == 0:
                        at_least(dve, S["mix"], g - 1)
                    dve.reciprocal(rs[:, u, b], z[:, :, 64:68]).then_inc(S["rs"], 1)
                    dve.wait_ge(S["rs"], GB * g + b + 1)
                    r = rs[:, u, b].rearrange("p e (n o) -> p e n o", o=1)
                    dve.tensor_tensor(oz[:, u, b], z[:, :, 0:64].rearrange("p e (n d) -> p e n d", n=NH),
                                      r.to_broadcast([T, NE, NH, D]), ALU.mult)
                    dve.tensor_tensor(ty[:, u, b].rearrange("p e (n k) -> p e n k", n=NH),
                                      z[:, :, 80:96].rearrange("p e (n k) -> p e n k", n=NH),
                                      r.to_broadcast([T, NE, NH, NE]), ALU.mult).then_inc(S["oz"], 1)

                def gate_logits(g, u):
                    dve.wait_ge(S["oz"], GB * (g + 1))
                    dve.tensor_reduce(lg[:, u], ty[:, u].rearrange("p b e c -> p b c e"), X, ALU.add).then_inc(S["lg0"], 1)
                    dve.wait_ge(S["lg0"], g + 1)
                    dve.tensor_tensor(lg[:, u], lg[:, u], gate_b[:].rearrange("p (o c) -> p o c", o=1).to_broadcast([T, GB, NH * NE]),
                                      ALU.add).then_inc(S["lg1"], 1)
                    dve.wait_ge(S["lg1"], g + 1)
                    v = lg[:, u].rearrange("p b (n e) -> p (b n) e", n=NH)
                    m = lm[:, u].rearrange("p b (n o) -> p (b n) o", o=1)
                    dve.tensor_reduce(lm[:, u].rearrange("p b n -> p (b n)"), v, X, ALU.max).then_inc(S["lm"], 1)
                    dve.wait_ge(S["lm"], g + 1)
                    dve.tensor_tensor(v, v, m.to_broadcast([T, GB * NH, NE]), ALU.subtract).then_inc(S["lg2"], 1)

                def gate_weights(g, u):
                    dve.wait_ge(S["eg"], g + 1)
                    v = eg[:, u].rearrange("p b (n e) -> p (b n) e", n=NH)
                    dve.tensor_reduce(ls[:, u].rearrange("p b n -> p (b n)"), v, X, ALU.add).then_inc(S["ls"], 1)
                    dve.wait_ge(S["ls"], g + 1)
                    dve.reciprocal(li[:, u], ls[:, u]).then_inc(S["li"], 1)
                    dve.wait_ge(S["li"], g + 1)
                    dve.tensor_tensor(gs[:, u].rearrange("p b (n e) -> p (b n) e", n=NH), v,
                                      li[:, u].rearrange("p b (n o) -> p (b n) o", o=1).to_broadcast([T, GB * NH, NE]),
                                      ALU.mult).then_inc(S["gs"], 1)

                def mixed(g, u):
                    dve.wait_ge(S["half"], g + 1)
                    m = mix[:, bass.ds(GB * g, GB), :].rearrange("p b (n d) -> p b n d", n=NH)
                    dve.tensor_tensor(m, oz[:, u, :, 0], oz[:, u, :, 1], ALU.add).then_inc(S["mix"], 1)

                def step(g, u, front):
                    f, v = g + 1, 1 - u
                    behind = not (isinstance(g, int) and g == 0)
                    if front == 2:
                        norm(g + 2, u)
                    if front:
                        q_rest(f, v, 2, 4)
                    if behind:
                        scale(g - 1, v, 3)
                    if front:
                        q_rest(f, v, 4, 8)
                    for b in range(3):
                        if front and b > 0:
                            maxima(f, v, b, 0, 2)
                        outputs(g, u, b)
                        if front:
                            maxima(f, v, b, 2 if b > 0 else 0, 3)
                        if b == 1:
                            scale(g, u, 0)
                        if behind and b == 0:
                            gate_logits(g - 1, v)
                        if behind and b == 2:
                            gate_weights(g - 1, v)
                    if front:
                        maxima(f, v, 3, 0, 3)
                        split_max(f, v)
                    if front == 2:
                        x_rest(g + 2, u)
                    scale(g, u, 1)
                    if behind:
                        mixed(g - 1, v)
                    if front == 2:
                        k_rest(g + 2, u, 0)
                    scale(g, u, 2)
                    if front == 2:
                        k_rest(g + 2, u, 2)
                    outputs(g, u, 3)
                    if front == 2:
                        alive(g + 2, u)
                        q_rest(g + 2, u, 0, 2)

                norm(0, 0)
                norm(1, 1)
                x_rest(0, 0)
                k_rest(0, 0, 0)
                k_rest(0, 0, 2)
                alive(0, 0)
                q_rest(0, 0, 0, 8)
                for b in range(GB):
                    maxima(0, 0, b, 0, 3)
                split_max(0, 0)
                x_rest(1, 1)
                k_rest(1, 1, 0)
                k_rest(1, 1, 2)
                alive(1, 1)
                q_rest(1, 1, 0, 2)
                pipeline(dve, step)
                scale(NG - 1, 1, 3)
                gate_logits(NG - 1, 1)
                gate_weights(NG - 1, 1)
                mixed(NG - 1, 1)

            @block.scalar
            def _(act):
                def turned(g, u):
                    act.wait_ge(S["ps_xt"], g + 1)
                    at_least(act, S["ps_q"], 8 * (g - 1))
                    act.activation(xt[:, u, :], bank("xt")[:, :], ACT.Copy).then_inc(S["xt"], 1)

                def keys(g, u, n0):
                    for n in range(n0, n0 + 2):
                        act.wait_ge(S["ps_k"], NH * g + n + 1)
                        at_least(act, S["ps_s"], NH * GB * (g - 1))
                        act.activation(K[0:Q_ROWS, u, n, :, :].rearrange("p b t -> p (b t)"), bank(f"k{n}")[0:Q_ROWS, :],
                                       ACT.Identity, bias=bias[0:Q_ROWS, 8 + n:9 + n]).then_inc(S["kr"], 1)

                def values(g, u):
                    act.wait_ge(S["ps_v"], g + 1)
                    at_least(act, S["ps_o"], GB * (g - 1))
                    v = bank("v")[:, :].rearrange("p (b c) -> p b c", b=GB)
                    i = act.activation(V[:, u, :, :, 0:D], v[:, :, 0:H].rearrange("p b (n d) -> p b n d", n=NH), ACT.Copy)
                    if isinstance(g, int) and g == 0:
                        for n in range(NH):
                            i = act.activation(res[:, n * D:(n + 1) * D], v[:, n, H + n * D:H + (n + 1) * D], ACT.Copy)
                    i.then_inc(S["v"], 1)

                def query(g, u, k):
                    act.wait_ge(S["ps_q"], 8 * g + k + 1)
                    m, e = k // NE, k % NE
                    act.activation(Q[0:Q_ROWS, u, m].rearrange("p b (a e s) -> p (b a) e s", a=NBLK, e=NE)[:, :, e, :],
                                       bank(f"q{k}")[0:Q_ROWS, :].rearrange("p (a s) -> p a s", s=BLK),
                                   ACT.Identity, bias=bias[0:Q_ROWS, k:k + 1]).then_inc(S["qr"], 1)

                def maxima_out(g, u):
                    act.wait_ge(S["ps_ct"], g + 1)
                    if isinstance(g, int):
                        if g >= 2:
                            act.wait_ge(S[f"cmax{u}"], 16 * (g // 2))
                    else:
                        act.wait_ge(S[f"cmax{u}"], 16 * ((g - u) // 2))
                    act.activation(nmax_t[:, u, :], bank("ct")[:, 0:128], ACT.Copy).then_inc(S["ct"], 1)

                def weights(g, b, n):
                    act.wait_ge(S["ps_s"], NH * (GB * g + b) + n + 1)
                    at_least(act, S["ps_o"], GB * g + b - 1)
                    act.activation(P[:, b % 2, n, :], SB_[n % 2][:, :], ACT.Exp).then_inc(S["ex"], 1)

                def gates(g, u):
                    act.wait_ge(S["lg2"], g + 1)
                    act.activation(eg[:, u], lg[:, u], ACT.Exp).then_inc(S["eg"], 1)

                def step(g, u, front):
                    f, v = g + 1, 1 - u
                    for b in range(GB):
                        for n in range(NH):
                            weights(g, b, n)
                            if front and b == 0 and n > 0:
                                query(f, v, 2 * n)
                                query(f, v, 2 * n + 1)
                        if b == 2 and not (isinstance(g, int) and g == 0):
                            gates(g - 1, v)
                    if front == 2:
                        turned(g + 2, u)
                    if front:
                        maxima_out(f, v)
                    if front == 2:
                        keys(g + 2, u, 0)
                        keys(g + 2, u, 2)
                        query(g + 2, u, 0)
                        query(g + 2, u, 1)
                        values(g + 2, u)
                ln.on_scalar(act)
                act.wait_ge(S["bias"], 4)
                turned(0, 0)
                keys(0, 0, 0)
                keys(0, 0, 2)
                values(0, 0)
                for k in range(8):
                    query(0, 0, k)
                turned(1, 1)
                maxima_out(0, 0)
                keys(1, 1, 0)
                keys(1, 1, 2)
                query(1, 1, 0)
                query(1, 1, 1)
                values(1, 1)
                pipeline(act, step)
                gates(NG - 1, 1)

            @block.tensor
            def _(pe):
                pe.wait_ge(S["w"], 160)
                for k in range(NH * NE):
                    m = pe.matmul(ps[0][0:D, k * D:(k + 1) * D], wq_o[:, k, :], wk_o[:, k // NE, :], start=True, stop=True)
                m.then_inc(S["ps_w1"], 1)
                pe.wait_ge(S["qk_d"], 1)
                for n in range(NH):
                    pe.matmul(ps[2][0:H + 1, n * D:(n + 1) * D], hl_d[:, n, :], wv_d[:, n, :], start=True, stop=True)
                    m = pe.matmul(ps[1][0:H + 1, n * 64:(n + 1) * 64], hl_d[:, n, :], qk_d[:, n, :], start=True, stop=True)
                m.then_inc(S["ps_w2"], 1)
                pe.wait_ge(S["built"], 14 + 2 + 12 + 1 + 48)
                last_row = ident[0:H + 1, H:H + 1]
                for k in range(8):
                    pe.matmul(ps[3][0:Q_ROWS, k:k + 1], query_weights(w, k // NE, k % NE)[0:H + 1], last_row, start=True, stop=True)
                for n in range(NH):
                    pe.matmul(ps[3][0:Q_ROWS, 8 + n:9 + n], key_weights(w, n)[0:H + 1], last_row, start=True, stop=True)
                pe.matmul(ps[3][:, 12:13], live_weights(w)[0:H + 1], last_row, start=True, stop=True).then_inc(S["ps_bias"], 1)
                pe.wait_ge(S["bias"], 4)
                pe.wait_ge(S["halves"], 2)

                def turn(g, u):
                    pe.wait_ge(S["xn"], g + 1)
                    release(pe, "xt", g)
                    for b in range(GB):
                        for k in range(2):
                            m = pe.matmul(bank("xt")[k * H:(k + 1) * H, b * T:(b + 1) * T], xn[:, u, b, :], ident, start=True, stop=True)
                    m.then_inc(S["ps_xt"], 1)

                def product(out, weights, u):
                    pe.matmul(out, weights(wr), xt[:, u, :], start=True, stop=False)
                    return pe.matmul(out, weights(wl), xt[:, u, :], start=False, stop=True)

                def keys(g, u, n0):
                    pe.wait_ge(S["xl"], g + 1)
                    for n in range(n0, n0 + 2):
                        release(pe, f"k{n}", g)
                        product(bank(f"k{n}")[0:Q_ROWS, :], lambda t: key_weights(t, n), u).then_inc(S["ps_k"], 1)

                def alive(g, u):
                    release(pe, "np", g)
                    product(bank("np")[:, :], live_weights, u).then_inc(S["ps_np"], 1)

                def values(g, u):
                    release(pe, "v", g)
                    for r in range(2):
                        pe.matmul(bank("v")[:, :].rearrange("p (b c) -> p b c", b=GB), one_v[H:H + 1, :],
                                  bias_v[H:H + 1, r:r + 1, :].to_broadcast([1, GB, 128]), start=(r == 0), stop=False, skip_group_check=True)
                    for b in range(GB):
                        m = pe.matmul(bank("v")[:, b * 128:(b + 1) * 128], xt[:, u, b * T:(b + 1) * T].bitcast(F32), w_v[:],
                                      start=False, stop=True, skip_group_check=True)
                    m.then_inc(S["ps_v"], 1)

                def query(g, u, k):
                    release(pe, f"q{k}", g)
                    product(bank(f"q{k}")[0:Q_ROWS, :], lambda t: query_weights(t, k // NE, k % NE), u).then_inc(S["ps_q"], 1)

                def maxima(g, u, b, j):
                    if b == 0 and j == 0:
                        pe.wait_ge(S["ql"], 8 * (g + 1))
                        pe.wait_ge(S["kl"], NH * (g + 1))
                    blocks = ((3,), (2, 0), (1,))[j]
                    held, at = MXB[(3 * b + j) % 2], 0
                    at_least(pe, S["mx"], 3 * (GB * g + b) + j - 1)
                    for a in blocks:
                        w = BLK * (a + 1)
                        o = held[:, at:at + NH * w].rearrange("p (n w) -> p n w", n=NH)
                        pe.matmul(o[:, :, a * BLK:w], onehot[:], tri[:], start=(at == 0), stop=False, skip_group_check=True)
                        for n in range(NH):
                            q = Q[0:Q_ROWS, u, n // 2, b, a * 128:(a + 1) * 128].bitcast(BF16)
                            k = K[0:Q_ROWS, u, n, b, 0:w].bitcast(BF16)
                            m = pe.matmul(o[:, n, :], q[:, 1::2], k[:, 1::2], start=False, stop=True, skip_group_check=True)
                        at += NH * w
                    m.then_inc(S["ps_mx"], 1)

                def turn_maxima(g, u):
                    pe.wait_ge(S["nmax2"], g + 1)
                    release(pe, "ct", g + 1)
                    pe.transpose(bank("ct")[:, 0:128], nmax2[:, u].rearrange("p k r c -> p (k r c)").bitcast(F32), ident)\
                        .then_inc(S["ps_ct"], 1)

                def scores(g, u, b, n):
                    if b == 0 and n == 0:
                        if isinstance(g, int):
                            pe.wait_ge(S[f"cmax{u}"], 16 * (g // 2 + 1))
                        else:
                            pe.wait_ge(S[f"cmax{u}"], 16 * ((g - u) // 2 + 1))
                    at_least(pe, S["ex"], NH * (GB * g + b) + n - 1)
                    pe.matmul(SB_[n % 2][:, :], K[:, u, n, b, :], Q[:, u, n // 2, b, :], start=True, stop=False, skip_group_check=True)
                    for a in range(NBLK):
                        r = slice(a * BLK, (a + 1) * BLK)
                        m = pe.matmul(SB_[n % 2][r, a * 128:(a + 1) * 128], tri[r, 0, :], onehot[r, :], start=False, stop=True,
                                      skip_group_check=True)
                    m.then_inc(S["ps_s"], 1)

                def outputs(g, u, b):
                    pe.wait_ge(S["ex"], NH * (GB * g + b) + NH)
                    pe.wait_ge(S["v"], g + 1)
                    at_least(pe, S["om"], GB * g + b)
                    for n in range(NH):
                        m = pe.matmul(OB[32 * n:32 * n + 32, :], V[:, u, b, n, :], P[:, b % 2, n, :], start=True, stop=True)
                    m.then_inc(S["ps_o"], 1)

                def natural(g, u, b):
                    pe.wait_ge(S["om"], GB * g + b + 1)
                    at_least(pe, S["oz"], GB * g + b)
                    for e in range(NE):
                        m = pe.matmul(ZB[:, e * 128:(e + 1) * 128], om[:, b % 2, e, :], sel[:, e, :], start=True, stop=True)
                    m.then_inc(S["ps_z"], 1)

                def step(g, u, front):
                    f, v = g + 1, 1 - u
                    for n in range(NH):
                        scores(g, u, 0, n)
                        if front and n > 0:
                            query(f, v, 2 * n)
                            query(f, v, 2 * n + 1)
                        if n == 1 and not (isinstance(g, int) and g == 0):
                            natural(g - 1, v, 3)
                    for b in range(3):
                        for n in range(NH):
                            scores(g, u, 1 + b, n)
                            if (b, n) == (0, 1):
                                outputs(g, u, 0)
                            if front and n in (1, 2):
                                maxima(f, v, b, n - 1)
                        if b > 0:
                            outputs(g, u, b)
                        if front:
                            maxima(f, v, b, 2)
                        if b == 1:
                            natural(g, u, 0)
                    if front:
                        maxima(f, v, 3, 0)
                        maxima(f, v, 3, 1)
                    if front == 2:
                        turn(g + 2, u)
                    if front:
                        maxima(f, v, 3, 2)
                    natural(g, u, 1)
                    if front:
                        turn_maxima(f, v)
                    if front == 2:
                        keys(g + 2, u, 0)
                    natural(g, u, 2)
                    if front == 2:
                        keys(g + 2, u, 2)
                    outputs(g, u, 3)
                    if front == 2:
                        alive(g + 2, u)
                        query(g + 2, u, 0)
                        query(g + 2, u, 1)
                        values(g + 2, u)
                turn(0, 0)
                keys(0, 0, 0)
                keys(0, 0, 2)
                alive(0, 0)
                values(0, 0)
                for k in range(8):
                    query(0, 0, k)
                for b in range(GB):
                    for j in range(3):
                        maxima(0, 0, b, j)
                turn(1, 1)
                turn_maxima(0, 0)
                keys(1, 1, 0)
                keys(1, 1, 2)
                alive(1, 1)
                query(1, 1, 0)
                query(1, 1, 1)
                values(1, 1)
                pipeline(pe, step)
                natural(NG - 1, 1, 3)


def feed_forward(nc, ins, M, ps, out):
    H_all, cst, mix, res = M["H"], M["cst"], M["mix"], M["res"]
    DB = 8
    DG = B // DB
    NP = DB // 2
    HB = DB * NH
    ctx = ExitStack()
    with ctx:
        def sb(name, shape):
            return ctx.enter_context(nc.sbuf_tensor(name, shape, F32))
        fc = sb("d_fc", [128, 2, 128])
        fin = sb("d_fin", [128, 128 + 8])
        vec = sb("d_vec", [128, 6])
        sq = sb("d_sq", [T, 2, DB * H])
        total = sb("d_total", [T, 2, HB])
        var = sb("d_var", [T, B * NH])
        rstd = sb("d_rstd", [T, B * NH])
        root = sb("d_root", [T, B * NH])
        y = sb("d_y", [T, 2, DB * H])
        fx = sb("d_fx", [128, 4, NP * T])
        live = sb("d_live", [128, 2, NP * T])
        r1 = sb("d_r1", [128, 2, NP * T])
        r2 = sb("d_r2", [128, 2, NP * T])
        hx = sb("d_hx", [128, 2, NP * T])
        fo = sb("d_fo", [128, 2, NP * T])
        lg = sb("d_lg", [T, 2, HB])
        lw = sb("d_lw", [T, 2, HB])
        lm = sb("d_lm", [T, 2, 3, DB])
        o = sb("d_o", [T, 2, DB, H])
        S = signals(nc, ctx, "d", "w zeroed fin z tot1 zc1 sq1 var1 v root newton rstd "
                    "y1 ps_t1 fx live ps_m1 r1 r2 ps_m2 hx ps_b tot2 zc2 sq2 var2 "
                    "y2 ps_t2 fo ps_f lm lg e ls li lw o1 o2 out0 out1")
        ident = cst[:, C_ID:C_ID + 128]

        def heads(t):
            return t.rearrange("p (c d) -> p c d", d=D)

        def flat(t, g):
            return t[:, bass.ds(g * DB, DB), :].rearrange("p b (n d) -> p (b n) d", n=NH)

        def each(t):
            return t.rearrange("p (c o) -> p c o", o=1).to_broadcast([T, HB, D])

        def stages(eng, fs):
            rounds(eng, DG // 2, [(late, lambda it, g, u, s, f=f: f(g, u, s)) for late, f in fs])

        with nc.Block() as block:
            @block.sync
            def _(sp):
                sp.wait_ge(S["zeroed"], 2)
                for k in range(128 // D):
                    r = slice(k * D, (k + 1) * D)
                    sp.dma_start(fc[r, 0, r], ins["fc1_t"]).then_inc(S["w"], 16)
                    sp.dma_start(fc[r, 1, r], ins["fc2_t"]).then_inc(S["w"], 16)
                    sp.dma_start(vec[r, :], ins["vectors"]).then_inc(S["w"], 16)
                for k in range(2):
                    sp.dma_start(fin[k * H:(k + 1) * H, 128 + 4 * k:132 + 4 * k], ins["fgate_t"]).then_inc(S["w"], 16)

                def store(g, u, s):
                    sp.wait_ge(S["o2"], g + 1)
                    sp.dma_start(out[bass.ds(g * DB, DB), :, :].rearrange("b s h -> s b h"), o[:, u]).then_inc(S[f"out{u}"], 16)
                stages(sp, [(0, store)])
                for u in range(2):
                    sp.wait_ge(S[f"out{u}"], 16 * (DG // 2))

            @block.gpsimd
            def _(pool):
                pool.memset(fc[:], 0.0).then_inc(S["zeroed"], 1)
                pool.memset(fin[:, 128:136], 0.0).then_inc(S["zeroed"], 1)
                with pool.Fori(0, DG) as g:
                    m = mix[:, bass.ds(g * DB, DB), :]
                    pool.tensor_tensor(m, m, res[:].rearrange("p (o c) -> p o c", o=1).to_broadcast([T, DB, H]), ALU.add).then_inc(S["z"], 1)

            @block.vector
            def _(dve):
                dve.tensor_copy(fin[:, 0:128], ident).then_inc(S["fin"], 1)

                def center(g, u, k, source):
                    at_least(dve, S[f"zc{k}"], g - 1)
                    dve.tensor_reduce(total[:, u], source, X, ALU.add).then_inc(S[f"tot{k}"], 1)
                    dve.wait_ge(S[f"tot{k}"], g + 1)
                    dve.scalar_tensor_tensor(flat(mix, g), each(total[:, u]), -1.0 / D, source, ALU.mult, ALU.add).then_inc(S[f"zc{k}"], 1)

                def variance(g, u, k):
                    dve.wait_ge(S[f"sq{k}"], g + 1)
                    dve.tensor_reduce(var[:, bass.ds(g * HB, HB)], heads(sq[:, u]), X, ALU.add).then_inc(S[f"var{k}"], 1)

                def roots(k):
                    dve.wait_ge(S[f"var{k}"], DG)
                    dve.tensor_scalar(var[:], var[:], 1.0 / D, 1e-8, ALU.mult, ALU.add).then_inc(S["v"], 1)
                    dve.wait_ge(S["root"], k)
                    if k == 2:
                        dve.wait_ge(S["y1"], DG)
                    dve.reciprocal(rstd[:], root[:]).then_inc(S["newton"], 1)
                    dve.wait_ge(S["newton"], 3 * k - 2)
                    dve.tensor_tensor(root[:], rstd[:], rstd[:], ALU.mult).then_inc(S["newton"], 1)
                    dve.wait_ge(S["newton"], 3 * k - 1)
                    dve.scalar_tensor_tensor(var[:], var[:], -0.5, root[:], ALU.mult, ALU.mult).then_inc(S["newton"], 1)
                    dve.wait_ge(S["newton"], 3 * k - 0)
                    dve.scalar_tensor_tensor(rstd[:], var[:], 1.5, rstd[:], ALU.add, ALU.mult).then_inc(S["rstd"], 1)
                    dve.wait_ge(S["rstd"], k)

                def statistics(g, u, s):
                    dve.wait_ge(S["z"], g + 1)
                    center(g, u, 1, flat(mix, g))

                stages(dve, [(0, statistics), (1, lambda g, u, s: variance(g, u, 1))])
                roots(1)
                dve.wait_ge(S["w"], 16 * 26)

                def scaled(g, u, k):
                    at_least(dve, S[f"ps_t{k}"], g - 1)
                    dve.tensor_tensor(heads(y[:, u]), flat(mix, g), rstd[:, bass.ds(g * HB, HB)].rearrange("p (c o) -> p c o", o=1)
                                      .to_broadcast([T, HB, D]), ALU.mult).then_inc(S[f"y{k}"], 1)

                def alive(g, u, s):
                    dve.wait_ge(S["fx"], g + 1)
                    dve.tensor_scalar(live[:, u], fx[:, s], 0.0, None, ALU.not_equal).then_inc(S["live"], 1)

                def hidden(g, u, s):
                    dve.wait_ge(S["r1"], g + 1)
                    dve.wait_ge(S["live"], g + 1)
                    dve.tensor_tensor(r2[:, u], r1[:, u], live[:, u], ALU.mult).then_inc(S["r2"], 1)

                def second(g, u, s):
                    dve.wait_ge(S["ps_m2"], g + 1)
                    dve.scalar_tensor_tensor(hx[:, u], ps[4 * u + 2][:, :], vec[:, 3:4], live[:, u], ALU.add, ALU.mult).then_inc(S["hx"], 1)

                def center_second(g, u, s):
                    dve.wait_ge(S["ps_b"], g + 1)
                    center(g, u, 2, heads(ps[4 * u + 3][:, :]))

                stages(dve, [(0, lambda g, u, s: scaled(g, u, 1)), (2, lambda g, u, s: variance(g, u, 2)), (1, alive), (1, hidden), (1, second),
                             (1, center_second)])
                roots(2)

                def logits(g, u, s):
                    dve.wait_ge(S["ps_f"], g + 1)
                    for k in range(2):
                        v = ps[4 * u + 1 + k][:, 0:272].rearrange("p (q c) -> p q c", q=2)[:, :, 128:136].rearrange("p q (b n) -> p q b n", b=2)
                        dve.tensor_reduce(lm[:, u, 0, 4 * k:4 * k + 4].rearrange("p (q b) -> p q b", q=2), v, X, ALU.max).then_inc(S["lm"], 1)
                    dve.wait_ge(S["lm"], 2 * g + 2)
                    for k in range(2):
                        v = ps[4 * u + 1 + k][:, 0:272].rearrange("p (q c) -> p q c", q=2)[:, :, 128:136].rearrange("p q (b n) -> p q b n", b=2)
                        m = lm[:, u, 0, 4 * k:4 * k + 4].rearrange("p (q b o) -> p q b o", q=2, o=1)
                        dve.tensor_tensor(lg[:, u, 16 * k:16 * k + 16].rearrange("p (q b n) -> p q b n", q=2, b=2), v,
                                          m.to_broadcast([T, 2, 2, NH]), ALU.subtract).then_inc(S["lg"], 1)

                def gates(g, u, s):
                    dve.wait_ge(S["e"], g + 1)
                    v = lg[:, u].rearrange("p (b n) -> p b n", b=DB)
                    dve.tensor_reduce(lm[:, u, 1], v, X, ALU.add).then_inc(S["ls"], 1)
                    dve.wait_ge(S["ls"], g + 1)
                    dve.reciprocal(lm[:, u, 2], lm[:, u, 1]).then_inc(S["li"], 1)
                    dve.wait_ge(S["li"], g + 1)
                    dve.tensor_tensor(lw[:, u].rearrange("p (b n) -> p b n", b=DB), v,
                                      lm[:, u, 2].rearrange("p (b o) -> p b o", o=1).to_broadcast([T, DB, NH]), ALU.mult).then_inc(S["lw"], 1)

                def result(g, u, s):
                    dve.wait_ge(S["lw"], g + 1)
                    if isinstance(g, int):
                        if g >= 2:
                            dve.wait_ge(S[f"out{u}"], 16 * (g // 2))
                    else:
                        dve.wait_ge(S[f"out{u}"], 16 * ((g - u) // 2))
                    for k in range(2):
                        v = ps[4 * u + 1 + k][:, 0:272].rearrange("p (q c) -> p q c", q=2)[:, :, 0:128].rearrange("p q (c d) -> p q c d", d=D)
                        w = lw[:, u, 16 * k:16 * k + 16].rearrange("p (q c o) -> p q c o", q=2, o=1)
                        dve.tensor_tensor(o[:, u, 4 * k:4 * k + 4, :].rearrange("p (q b) (n d) -> p q (b n) d", q=2, n=NH), v,
                                          w.to_broadcast([T, 2, 8, D]), ALU.mult).then_inc(S["o1"], 1)

                def add_stream(g, u, s):
                    dve.wait_ge(S["o1"], 2 * g + 2)
                    dve.tensor_tensor(o[:, u], o[:, u], H_all[:, bass.ds(g * DB, DB), :], ALU.add).then_inc(S["o2"], 1)

                stages(dve, [(0, lambda g, u, s: scaled(g, u, 2)), (1, logits), (1, gates), (1, result), (1, add_stream)])

            @block.scalar
            def _(act):
                act.wait_ge(S["w"], 16 * 26)

                def square(g, u, k):
                    act.wait_ge(S[f"zc{k}"], g + 1)
                    at_least(act, S[f"var{k}"], g - 1)
                    act.activation(sq[:, u], mix[:, bass.ds(g * DB, DB), :].rearrange("p b h -> p (b h)"), ACT.Square).then_inc(S[f"sq{k}"], 1)

                def roots(k):
                    act.wait_ge(S["v"], k)
                    act.activation(root[:], var[:], ACT.Sqrt).then_inc(S["root"], 1)

                def first(g, u, s):
                    act.wait_ge(S["ps_t1"], g + 1)
                    at_least(act, S["ps_b"], g - 3)
                    act.activation(fx[:, s], ps[4 * u][:, :], ACT.Identity, bias=vec[:, 1:2], scale=vec[:, 0:1]).then_inc(S["fx"], 1)

                def hidden(g, u, s):
                    act.wait_ge(S["ps_m1"], g + 1)
                    act.activation(r1[:, u], ps[4 * u + 1][:, :], ACT.Relu, bias=vec[:, 2:3]).then_inc(S["r1"], 1)

                def last(g, u, s):
                    act.wait_ge(S["ps_t2"], g + 1)
                    act.activation(fo[:, u], ps[4 * u][:, :], ACT.Identity, bias=vec[:, 5:6], scale=vec[:, 4:5]).then_inc(S["fo"], 1)

                def gates(g, u, s):
                    act.wait_ge(S["lg"], 2 * g + 2)
                    act.activation(lg[:, u], lg[:, u], ACT.Exp).then_inc(S["e"], 1)

                stages(act, [(0, lambda g, u, s: square(g, u, 1))])
                roots(1)
                stages(act, [(1, hidden), (0, first), (1, lambda g, u, s: square(g, u, 2))])
                roots(2)
                stages(act, [(0, last), (0, gates)])

            @block.tensor
            def _(pe):
                pe.wait_ge(S["fin"], 1)
                pe.wait_ge(S["w"], 16 * 26)

                def turn(g, u, k):
                    pe.wait_ge(S[f"y{k}"], g + 1)
                    if k == 1:
                        at_least(pe, S["fx"], g - 1)
                    for p in range(NP):
                        m = pe.transpose(ps[4 * u][:, p * T:(p + 1) * T], y[:, u, p * 2 * H:(p + 1) * 2 * H], ident)
                    m.then_inc(S[f"ps_t{k}"], 1)

                def first(g, u, s):
                    pe.wait_ge(S["fx"], g + 1)
                    pe.matmul(ps[4 * u + 1][:, :], fc[:, 0, :], fx[:, s], start=True, stop=True).then_inc(S["ps_m1"], 1)

                def second(g, u, s):
                    pe.wait_ge(S["r2"], g + 1)
                    pe.matmul(ps[4 * u + 2][:, :], fc[:, 1, :], r2[:, u], start=True, stop=True).then_inc(S["ps_m2"], 1)

                def back(g, u, s):
                    pe.wait_ge(S["hx"], g + 1)
                    at_least(pe, S["zc2"], g - 1)
                    for p in range(NP):
                        c = slice(p * T, (p + 1) * T)
                        pe.matmul(ps[4 * u + 3][:, c], hx[:, u, c], ident, start=True, stop=False)
                        m = pe.matmul(ps[4 * u + 3][:, c], fx[:, s, c], ident, start=False, stop=True)
                    m.then_inc(S["ps_b"], 1)

                def final(g, u, s):
                    pe.wait_ge(S["fo"], g + 1)
                    at_least(pe, S["o1"], 2 * (g - 1))
                    for p in range(NP):
                        m = pe.matmul(ps[4 * u + 1 + p // 2][:, (p % 2) * 136:(p % 2) * 136 + 136], fo[:, u, p * T:(p + 1) * T], fin[:],
                                      start=True, stop=True)
                    m.then_inc(S["ps_f"], 1)

                stages(pe, [(1, first), (0, lambda g, u, s: turn(g, u, 1)), (1, second), (1, back)])
                stages(pe, [(1, final), (0, lambda g, u, s: turn(g, u, 2))])


INPUTS = ("x consts table b_oah W_in_t Wq Wk Wv Wo_t hl_d hl_t wq_o wk_o wv_d gate_b gate_w fc1_t fc2_t vectors fgate_t").split()


def build_program(nc, ins, out):
    ctx = ExitStack()
    with ctx:
        def sb(name, shape):
            return ctx.enter_context(nc.sbuf_tensor(name, shape, F32))
        M = {"H": sb("h_all", [T, B, H]),
             "mix": sb("mix", [T, B, H]),
             "res": sb("res", [T, H]),
             "stats": sb("stats", [T, B, 6]),
             "cst": sb("cst", [128, N_CONST])}
        ps = [ctx.enter_context(nc.psum_tensor(f"bank{i}", [128, 512], F32)) for i in range(8)]
        token_graph(nc, ins, M, ps)
        relu_attention(nc, ins, M, ps)
        head_attention(nc, ins, M, ps)
        feed_forward(nc, ins, M, ps, out)


def kernel(**inputs):
    import concourse.bacc as _bacc
    from concourse.bass_utils import run_bass_kernel_spmd as _run

    a = {k.replace("L0_tok_", "").replace("L0_attn_", "").replace("L0_ffn_", "ffn_"): np.asarray(v) for k, v in inputs.items()}
    backwards = a["emb_table"][::-1]
    hl = np.concatenate([a["ffn_hl_w"], a["ffn_hl_b"][:, :, None]], 2)
    arrays = {
        "x": a["x"],
        "consts": shape_constants(),
        "table": np.concatenate([backwards, backwards])[:2 * T],
        "b_oah": a["b_oah"].reshape(1, H),
        "W_in_t": a["W_in"].T,
        "Wq": a["Wq"], "Wk": a["Wk"], "Wv": a["Wv"], "Wo_t": a["Wo"].T,
        "hl_d": hl.transpose(1, 0, 2),
        "hl_t": hl.transpose(2, 0, 1).reshape(H + 1, H),
        "wq_o": a["ffn_wq"].transpose(2, 0, 1, 3).reshape(D, NH * NE, D),
        "wk_o": a["ffn_wk"].transpose(1, 0, 2),
        "wv_d": a["ffn_wv"].transpose(2, 0, 1),
        "gate_b": a["ffn_gate_b"].reshape(1, NH * NE),
        "gate_w": a["ffn_gate_w"].reshape(NH, NE, NE, D).transpose(0, 3, 2, 1),
        "fc1_t": a["ffn_fc1_w"].T, "fc2_t": a["ffn_fc2_w"].T,
        "vectors": np.stack([a["ffn_" + n] for n in ("ln_g", "ln_b", "fc1_b", "fc2_b", "fnorm_g", "fnorm_b")], 1),
        "fgate_t": a["ffn_fgate_w"].T,
    }
    nc = _bacc.Bacc("TRN2", target_bir_lowering=False, num_devices=1)
    ins, data = {}, {}
    for name in INPUTS:
        v = np.ascontiguousarray(arrays[name])
        data["in_" + name] = v
        ins[name] = nc.dram_tensor("in_" + name, v.shape, mybir.dt.from_np(v.dtype), kind="ExternalInput").ap()
    out = nc.dram_tensor("out_h", (B, T, H), F32, kind="ExternalOutput").ap()
    build_program(nc, ins, out)
    return _run(nc, [data], core_ids=[0]).results[0]["out_h"]
```
